# Optimizing a Trainium2 kernel written in Bass

```python
import numpy as np
import jax
import jax.numpy as jnp

def _softmax(x, axis=-1):
    return jax.nn.softmax(x, axis=axis)

def _gelu(x):
    return jax.nn.gelu(x, approximate=True)

def _silu(x):
    return jax.nn.silu(x)

def _sigmoid(x):
    return jax.nn.sigmoid(x)

def _layernorm(x, axis=-1, eps=1e-05):
    m = jnp.mean(x, axis=axis, keepdims=True)
    v = jnp.var(x, axis=axis, keepdims=True)
    return (x - m) / jnp.sqrt(v + eps)

def _scatter_add(tgt, idx, src, axis=0):
    return tgt.at[idx].add(src)

def _segment_sum(src, seg, n):
    return jax.ops.segment_sum(src, seg, n)
kernel_name = 'mk_lm_tower_d2_tok_ids512_r4_41dcf4'

def setup_inputs(seed: int=0):
    np.random.seed(seed)
    _w = jnp.asarray

    def _rec_inputs():
        import jax
        import jax.numpy as jnp
        _rk = jax.random.key(seed)
        x = jax.random.randint(jax.random.fold_in(_rk, 1), (8, 512), 0, 12564, jnp.int32)
        return x
    x = _rec_inputs()

    def _L0_tok_setup():
        import jax, jax.numpy as jnp
        import numpy as np
        VOCAB = 50257
        UNITS = 128
        key = jax.random.key(seed)
        k_ids, k_w = jax.random.split(key)
        ids = jax.random.randint(k_ids, (8, 512), 0, VOCAB, dtype=jnp.int32)
        w = jax.random.normal(k_w, (VOCAB, UNITS), dtype=jnp.float32) * 0.05
        return {'input': ids, 'w': w}
    _L0_tok_all = _L0_tok_setup()
    _L0_tok_in = {k: v for k, v in _L0_tok_all.items() if k in ('w',)}
    del _L0_tok_all

    def _L0_attn_setup():
        import jax, jax.numpy as jnp
        import numpy as np
        B, T, D = (8, 1024, 128)
        EXPAND = 2
        DI = D * EXPAND
        K = 7
        LN_EPS = 1e-05

        def _seq_mixer(x, conv_w, conv_b, proj_w, proj_b):
            C = x.shape[-1]
            xp = jnp.pad(x, ((0, 0), (K - 1, 0), (0, 0)))
            y = jax.lax.conv_general_dilated(xp.transpose(0, 2, 1), conv_w, window_strides=(1,), padding='VALID', dimension_numbers=('NCH', 'OIH', 'NCH'), feature_group_count=C)
            y = y.transpose(0, 2, 1) + conv_b
            y = jnp.einsum('btc,oc->bto', y, proj_w) + proj_b
            return jax.nn.silu(y)

        def _shift_right(x):
            return jnp.pad(x, ((0, 0), (1, 0), (0, 0)))[:, :-1, :]
        key = jax.random.key(seed)
        ks = jax.random.split(key, 12)
        s = 0.02
        return {'x': jax.random.normal(ks[0], (B, T, D), dtype=jnp.float32), 'in_proj_w': jax.random.normal(ks[1], (2 * DI, D), dtype=jnp.float32) * s, 'conv_fwd_w': jax.random.normal(ks[2], (DI, 1, K), dtype=jnp.float32) * s, 'conv_fwd_b': jnp.zeros((DI,), dtype=jnp.float32), 'proj_fwd_w': jax.random.normal(ks[3], (DI, DI), dtype=jnp.float32) * s, 'proj_fwd_b': jnp.zeros((DI,), dtype=jnp.float32), 'conv_bwd_w': jax.random.normal(ks[4], (DI, 1, K), dtype=jnp.float32) * s, 'conv_bwd_b': jnp.zeros((DI,), dtype=jnp.float32), 'proj_bwd_w': jax.random.normal(ks[5], (DI, DI), dtype=jnp.float32) * s, 'proj_bwd_b': jnp.zeros((DI,), dtype=jnp.float32), 'diag_weight': jnp.full((DI,), 0.1, dtype=jnp.float32), 'gate_scale': jnp.full((1,), 0.5, dtype=jnp.float32), 'out_proj_w': jax.random.normal(ks[6], (D, DI), dtype=jnp.float32) * s, 'ln_g': jnp.ones((D,), dtype=jnp.float32), 'ln_b': jnp.zeros((D,), dtype=jnp.float32)}
    _L0_attn_all = _L0_attn_setup()
    _L0_attn_in = {k: v for k, v in _L0_attn_all.items() if k in ('in_proj_w', 'conv_fwd_w', 'conv_fwd_b', 'proj_fwd_w', 'proj_fwd_b', 'conv_bwd_w', 'conv_bwd_b', 'proj_bwd_w', 'proj_bwd_b', 'diag_weight', 'gate_scale', 'out_proj_w', 'ln_g', 'ln_b')}
    del _L0_attn_all

    def _L0_ffn_setup():
        import jax, jax.numpy as jnp
        import numpy as np
        B, S, D, F, E = (4, 512, 128, 512, 8)
        key = jax.random.key(seed)
        k = jax.random.split(key, 5)
        x = jax.random.normal(k[0], (B, S, D), dtype=jnp.float32)
        Ws = jax.random.normal(k[1], (D, E), dtype=jnp.float32) * 0.02
        bs = jnp.zeros((E,), dtype=jnp.float32)
        W1 = jax.random.normal(k[2], (E, D, F), dtype=jnp.float32) * 0.02
        b1 = jnp.zeros((E, F), dtype=jnp.float32)
        W2 = jax.random.normal(k[3], (E, F, D), dtype=jnp.float32) * 0.02
        b2 = jnp.zeros((E, D), dtype=jnp.float32)
        return {'x': x, 'Ws': Ws, 'bs': bs, 'W1': W1, 'b1': b1, 'W2': W2, 'b2': b2}
    _L0_ffn_all = _L0_ffn_setup()
    _L0_ffn_in = {k: v for k, v in _L0_ffn_all.items() if k in ('Ws', 'bs', 'W1', 'b1', 'W2', 'b2')}
    del _L0_ffn_all

    def _L1_attn_setup():
        import jax, jax.numpy as jnp
        import numpy as np
        D_MODEL = 128
        D_STATE = 128
        D_CONV = 4
        EXPAND = 2
        HEADDIM = 64
        CHUNK = 64
        D_INNER = EXPAND * D_MODEL
        NHEADS = D_INNER // HEADDIM
        CONV_DIM = D_INNER + 2 * D_STATE
        D_IN_PROJ = 2 * D_INNER + 2 * D_STATE + NHEADS
        BATCH, SEQLEN = (2, 2048)

        def segsum(a):
            T = a.shape[-1]
            a = jnp.broadcast_to(a[..., :, None], a.shape + (T,))
            a = jnp.where(jnp.tril(jnp.ones((T, T), bool), -1), a, 0.0)
            a = jnp.cumsum(a, axis=-2)
            return jnp.where(jnp.tril(jnp.ones((T, T), bool), 0), a, -jnp.inf)

        def ssd(x, A, B, C):
            b, l, h, p = x.shape
            c = l // CHUNK
            x = x.reshape(b, c, CHUNK, h, p)
            A = jnp.transpose(A.reshape(b, c, CHUNK, h), (0, 3, 1, 2))
            B = B.reshape(b, c, CHUNK, -1)
            C = C.reshape(b, c, CHUNK, -1)
            A_cumsum = jnp.cumsum(A, axis=-1)
            L = jnp.exp(segsum(A))
            Y_diag = jnp.einsum('bcln,bcsn,bhcls,bcshp->bclhp', C, B, L, x)
            decay_states = jnp.exp(A_cumsum[..., -1:] - A_cumsum)
            states = jnp.einsum('bcln,bhcl,bclhp->bchpn', B, decay_states, x)
            init = jnp.zeros_like(states[:, :1])
            A_pad = jnp.pad(A_cumsum[..., -1], ((0, 0), (0, 0), (1, 0)))
            decay_chunk = jnp.exp(segsum(A_pad))
            new_states = jnp.einsum('bhzc,bchpn->bzhpn', decay_chunk, jnp.concatenate([init, states], axis=1))
            states = new_states[:, :-1]
            state_decay_out = jnp.exp(A_cumsum)
            Y_off = jnp.einsum('bchpn,bcsn,bhcs->bcshp', states, C, state_decay_out)
            return (Y_diag + Y_off).reshape(b, l, h, p)

        def mamba2_block(u, in_proj_w, conv_w, conv_b, dt_bias, A_log, D_skip, norm_w, ssm_out_w):
            b, l, _ = u.shape
            zxbcdt = u @ in_proj_w.T
            z = zxbcdt[..., :D_INNER]
            xBC = zxbcdt[..., D_INNER:D_INNER + CONV_DIM]
            dt = jax.nn.softplus(zxbcdt[..., -NHEADS:] + dt_bias)
            conv = jax.lax.conv_general_dilated(jnp.transpose(xBC, (0, 2, 1)), conv_w, (1,), [(D_CONV - 1, 0)], dimension_numbers=('NCH', 'OIH', 'NCH'), feature_group_count=CONV_DIM)
            xBC = jax.nn.silu(jnp.transpose(conv + conv_b[None, :, None], (0, 2, 1)))
            xh = xBC[..., :D_INNER].reshape(b, l, NHEADS, HEADDIM)
            Bm = xBC[..., D_INNER:D_INNER + D_STATE]
            Cm = xBC[..., -D_STATE:]
            A = -jnp.exp(A_log)
            y = ssd(xh * dt[..., None], A * dt, Bm, Cm)
            y = y + xh * D_skip[None, None, :, None]
            y = y.reshape(b, l, D_INNER)
            y = y * jax.nn.silu(z)
            y = y * jax.lax.rsqrt(jnp.mean(y * y, axis=-1, keepdims=True) + 1e-05) * norm_w
            return y @ ssm_out_w.T
        key = jax.random.key(seed)
        ks = jax.random.split(key, 8)
        s = 0.02
        return {'x': jax.random.normal(ks[0], (BATCH, SEQLEN, D_MODEL), jnp.float32), 'in_proj_w': jax.random.normal(ks[1], (D_IN_PROJ, D_MODEL), jnp.float32) * s, 'conv_w': jax.random.normal(ks[2], (CONV_DIM, 1, D_CONV), jnp.float32) * s, 'conv_b': jnp.zeros((CONV_DIM,), jnp.float32), 'dt_bias': jax.random.normal(ks[3], (NHEADS,), jnp.float32) * s, 'A_log': jnp.log(jnp.arange(1, NHEADS + 1, dtype=jnp.float32)), 'D_skip': jnp.ones((NHEADS,), jnp.float32), 'norm_w': jnp.ones((D_INNER,), jnp.float32), 'ssm_out_w': jax.random.normal(ks[4], (D_MODEL, D_INNER), jnp.float32) * s, 'fuse_w': jax.random.normal(ks[5], (D_MODEL, 2 * D_MODEL), jnp.float32) * s, 'fuse_b': jnp.zeros((D_MODEL,), jnp.float32)}
    _L1_attn_all = _L1_attn_setup()
    _L1_attn_in = {k: v for k, v in _L1_attn_all.items() if k in ('in_proj_w', 'conv_w', 'conv_b', 'dt_bias', 'A_log', 'D_skip', 'norm_w', 'ssm_out_w', 'fuse_w', 'fuse_b')}
    del _L1_attn_all

    def _L1_ffn_setup():
        import jax, jax.numpy as jnp
        import numpy as np
        B, S, H, E, K = (8, 1024, 128, 8, 2)
        key = jax.random.key(seed)
        ks = jax.random.split(key, 7)
        s_h = 1.0 / np.sqrt(H)
        s_2h = 1.0 / np.sqrt(2 * H)
        return {'x': jax.random.normal(ks[0], (B, S, H), dtype=jnp.float32), 'gate_w': jax.random.uniform(ks[1], (H, E), minval=-s_h, maxval=s_h, dtype=jnp.float32), 'gate_b': jax.random.uniform(ks[2], (E,), minval=-s_h, maxval=s_h, dtype=jnp.float32), 'w1': jax.random.uniform(ks[3], (E, H, 2 * H), minval=-s_h, maxval=s_h, dtype=jnp.float32), 'b1': jax.random.uniform(ks[4], (E, 2 * H), minval=-s_h, maxval=s_h, dtype=jnp.float32), 'w2': jax.random.uniform(ks[5], (E, 2 * H, H), minval=-s_2h, maxval=s_2h, dtype=jnp.float32), 'b2': jax.random.uniform(ks[6], (E, H), minval=-s_2h, maxval=s_2h, dtype=jnp.float32)}
    _L1_ffn_all = _L1_ffn_setup()
    _L1_ffn_in = {k: v for k, v in _L1_ffn_all.items() if k in ('gate_w', 'gate_b', 'w1', 'b1', 'w2', 'b2')}
    del _L1_ffn_all
    return {'x': x, 'L0_tok_w': _L0_tok_in['w'], 'L0_attn_in_proj_w': _L0_attn_in['in_proj_w'], 'L0_attn_conv_fwd_w': _L0_attn_in['conv_fwd_w'], 'L0_attn_conv_fwd_b': _L0_attn_in['conv_fwd_b'], 'L0_attn_proj_fwd_w': _L0_attn_in['proj_fwd_w'], 'L0_attn_proj_fwd_b': _L0_attn_in['proj_fwd_b'], 'L0_attn_conv_bwd_w': _L0_attn_in['conv_bwd_w'], 'L0_attn_conv_bwd_b': _L0_attn_in['conv_bwd_b'], 'L0_attn_proj_bwd_w': _L0_attn_in['proj_bwd_w'], 'L0_attn_proj_bwd_b': _L0_attn_in['proj_bwd_b'], 'L0_attn_diag_weight': _L0_attn_in['diag_weight'], 'L0_attn_gate_scale': _L0_attn_in['gate_scale'], 'L0_attn_out_proj_w': _L0_attn_in['out_proj_w'], 'L0_attn_ln_g': _L0_attn_in['ln_g'], 'L0_attn_ln_b': _L0_attn_in['ln_b'], 'L0_ffn_Ws': _L0_ffn_in['Ws'], 'L0_ffn_bs': _L0_ffn_in['bs'], 'L0_ffn_W1': _L0_ffn_in['W1'], 'L0_ffn_b1': _L0_ffn_in['b1'], 'L0_ffn_W2': _L0_ffn_in['W2'], 'L0_ffn_b2': _L0_ffn_in['b2'], 'L1_attn_in_proj_w': _L1_attn_in['in_proj_w'], 'L1_attn_conv_w': _L1_attn_in['conv_w'], 'L1_attn_conv_b': _L1_attn_in['conv_b'], 'L1_attn_dt_bias': _L1_attn_in['dt_bias'], 'L1_attn_A_log': _L1_attn_in['A_log'], 'L1_attn_D_skip': _L1_attn_in['D_skip'], 'L1_attn_norm_w': _L1_attn_in['norm_w'], 'L1_attn_ssm_out_w': _L1_attn_in['ssm_out_w'], 'L1_attn_fuse_w': _L1_attn_in['fuse_w'], 'L1_attn_fuse_b': _L1_attn_in['fuse_b'], 'L1_ffn_gate_w': _L1_ffn_in['gate_w'], 'L1_ffn_gate_b': _L1_ffn_in['gate_b'], 'L1_ffn_w1': _L1_ffn_in['w1'], 'L1_ffn_b1': _L1_ffn_in['b1'], 'L1_ffn_w2': _L1_ffn_in['w2'], 'L1_ffn_b2': _L1_ffn_in['b2']}

def reference(x, L0_tok_w, L0_attn_in_proj_w, L0_attn_conv_fwd_w, L0_attn_conv_fwd_b, L0_attn_proj_fwd_w, L0_attn_proj_fwd_b, L0_attn_conv_bwd_w, L0_attn_conv_bwd_b, L0_attn_proj_bwd_w, L0_attn_proj_bwd_b, L0_attn_diag_weight, L0_attn_gate_scale, L0_attn_out_proj_w, L0_attn_ln_g, L0_attn_ln_b, L0_ffn_Ws, L0_ffn_bs, L0_ffn_W1, L0_ffn_b1, L0_ffn_W2, L0_ffn_b2, L1_attn_in_proj_w, L1_attn_conv_w, L1_attn_conv_b, L1_attn_dt_bias, L1_attn_A_log, L1_attn_D_skip, L1_attn_norm_w, L1_attn_ssm_out_w, L1_attn_fuse_w, L1_attn_fuse_b, L1_ffn_gate_w, L1_ffn_gate_b, L1_ffn_w1, L1_ffn_b1, L1_ffn_w2, L1_ffn_b2):
    import jax
    import jax.numpy as jnp

    def _L0_tok_ref(input, w):
        import jax, jax.numpy as jnp
        import numpy as np
        VOCAB = 50257
        UNITS = 128
        return jnp.take(w, input, axis=0)

    def _L0_attn_ref(x, in_proj_w, conv_fwd_w, conv_fwd_b, proj_fwd_w, proj_fwd_b, conv_bwd_w, conv_bwd_b, proj_bwd_w, proj_bwd_b, diag_weight, gate_scale, out_proj_w, ln_g, ln_b):
        import jax, jax.numpy as jnp
        import numpy as np
        B, T, D = (8, 1024, 128)
        EXPAND = 2
        DI = D * EXPAND
        K = 7
        LN_EPS = 1e-05

        def _seq_mixer(x, conv_w, conv_b, proj_w, proj_b):
            C = x.shape[-1]
            xp = jnp.pad(x, ((0, 0), (K - 1, 0), (0, 0)))
            y = jax.lax.conv_general_dilated(xp.transpose(0, 2, 1), conv_w, window_strides=(1,), padding='VALID', dimension_numbers=('NCH', 'OIH', 'NCH'), feature_group_count=C)
            y = y.transpose(0, 2, 1) + conv_b
            y = jnp.einsum('btc,oc->bto', y, proj_w) + proj_b
            return jax.nn.silu(y)

        def _shift_right(x):
            return jnp.pad(x, ((0, 0), (1, 0), (0, 0)))[:, :-1, :]
        residual = x
        xz = jnp.einsum('btd,ed->bte', x, in_proj_w)
        x_proj, z = (xz[..., :DI], xz[..., DI:])
        y_fwd = _shift_right(_seq_mixer(x_proj, conv_fwd_w, conv_fwd_b, proj_fwd_w, proj_fwd_b))
        x_flip = jnp.flip(x_proj, axis=1)
        y_bwd = _shift_right(_seq_mixer(x_flip, conv_bwd_w, conv_bwd_b, proj_bwd_w, proj_bwd_b))
        y_bwd = jnp.flip(y_bwd, axis=1)
        y = y_fwd + y_bwd + x_proj * diag_weight
        y = y * jax.nn.silu(z) * gate_scale
        y = jnp.einsum('bte,de->btd', y, out_proj_w)
        h = residual + y
        mu = jnp.mean(h, axis=-1, keepdims=True)
        var = jnp.var(h, axis=-1, keepdims=True)
        return (h - mu) * jax.lax.rsqrt(var + LN_EPS) * ln_g + ln_b

    def _L0_ffn_ref(x, Ws, bs, W1, b1, W2, b2):
        import jax, jax.numpy as jnp
        import numpy as np
        B, S, D, F, E = (4, 512, 128, 512, 8)
        Bb, Ss, Dd = x.shape
        xt = x.reshape(-1, Dd)
        logits = xt @ Ws + bs
        probs = jax.nn.softmax(logits, axis=-1)
        prob_max = jnp.max(probs, axis=-1)
        routes = jnp.argmax(probs, axis=-1)
        onehot = jax.nn.one_hot(routes, W1.shape[0], dtype=xt.dtype)

        def expert_ffn(w1, bb1, w2, bb2):
            h = jax.nn.gelu(xt @ w1 + bb1, approximate=False)
            return h @ w2 + bb2
        y = jax.vmap(expert_ffn)(W1, b1, W2, b2)
        out = jnp.einsum('te,etd->td', onehot, y)
        out = out * prob_max[:, None]
        return out.reshape(Bb, Ss, Dd)

    def _L1_attn_ref(x, in_proj_w, conv_w, conv_b, dt_bias, A_log, D_skip, norm_w, ssm_out_w, fuse_w, fuse_b):
        import jax, jax.numpy as jnp
        import numpy as np
        D_MODEL = 128
        D_STATE = 128
        D_CONV = 4
        EXPAND = 2
        HEADDIM = 64
        CHUNK = 64
        D_INNER = EXPAND * D_MODEL
        NHEADS = D_INNER // HEADDIM
        CONV_DIM = D_INNER + 2 * D_STATE
        D_IN_PROJ = 2 * D_INNER + 2 * D_STATE + NHEADS
        BATCH, SEQLEN = (2, 2048)

        def segsum(a):
            T = a.shape[-1]
            a = jnp.broadcast_to(a[..., :, None], a.shape + (T,))
            a = jnp.where(jnp.tril(jnp.ones((T, T), bool), -1), a, 0.0)
            a = jnp.cumsum(a, axis=-2)
            return jnp.where(jnp.tril(jnp.ones((T, T), bool), 0), a, -jnp.inf)

        def ssd(x, A, B, C):
            b, l, h, p = x.shape
            c = l // CHUNK
            x = x.reshape(b, c, CHUNK, h, p)
            A = jnp.transpose(A.reshape(b, c, CHUNK, h), (0, 3, 1, 2))
            B = B.reshape(b, c, CHUNK, -1)
            C = C.reshape(b, c, CHUNK, -1)
            A_cumsum = jnp.cumsum(A, axis=-1)
            L = jnp.exp(segsum(A))
            Y_diag = jnp.einsum('bcln,bcsn,bhcls,bcshp->bclhp', C, B, L, x)
            decay_states = jnp.exp(A_cumsum[..., -1:] - A_cumsum)
            states = jnp.einsum('bcln,bhcl,bclhp->bchpn', B, decay_states, x)
            init = jnp.zeros_like(states[:, :1])
            A_pad = jnp.pad(A_cumsum[..., -1], ((0, 0), (0, 0), (1, 0)))
            decay_chunk = jnp.exp(segsum(A_pad))
            new_states = jnp.einsum('bhzc,bchpn->bzhpn', decay_chunk, jnp.concatenate([init, states], axis=1))
            states = new_states[:, :-1]
            state_decay_out = jnp.exp(A_cumsum)
            Y_off = jnp.einsum('bchpn,bcsn,bhcs->bcshp', states, C, state_decay_out)
            return (Y_diag + Y_off).reshape(b, l, h, p)

        def mamba2_block(u, in_proj_w, conv_w, conv_b, dt_bias, A_log, D_skip, norm_w, ssm_out_w):
            b, l, _ = u.shape
            zxbcdt = u @ in_proj_w.T
            z = zxbcdt[..., :D_INNER]
            xBC = zxbcdt[..., D_INNER:D_INNER + CONV_DIM]
            dt = jax.nn.softplus(zxbcdt[..., -NHEADS:] + dt_bias)
            conv = jax.lax.conv_general_dilated(jnp.transpose(xBC, (0, 2, 1)), conv_w, (1,), [(D_CONV - 1, 0)], dimension_numbers=('NCH', 'OIH', 'NCH'), feature_group_count=CONV_DIM)
            xBC = jax.nn.silu(jnp.transpose(conv + conv_b[None, :, None], (0, 2, 1)))
            xh = xBC[..., :D_INNER].reshape(b, l, NHEADS, HEADDIM)
            Bm = xBC[..., D_INNER:D_INNER + D_STATE]
            Cm = xBC[..., -D_STATE:]
            A = -jnp.exp(A_log)
            y = ssd(xh * dt[..., None], A * dt, Bm, Cm)
            y = y + xh * D_skip[None, None, :, None]
            y = y.reshape(b, l, D_INNER)
            y = y * jax.nn.silu(z)
            y = y * jax.lax.rsqrt(jnp.mean(y * y, axis=-1, keepdims=True) + 1e-05) * norm_w
            return y @ ssm_out_w.T
        args = (in_proj_w, conv_w, conv_b, dt_bias, A_log, D_skip, norm_w, ssm_out_w)
        y_fwd = mamba2_block(x, *args)
        y_rev = jnp.flip(mamba2_block(jnp.flip(x, 1), *args), 1)
        y_cat = jnp.concatenate([y_fwd, y_rev], axis=-1)
        return y_cat @ fuse_w.T + fuse_b

    def _L1_ffn_ref(x, gate_w, gate_b, w1, b1, w2, b2):
        import jax, jax.numpy as jnp
        import numpy as np
        B, S, H, E, K = (8, 1024, 128, 8, 2)
        logits = jnp.einsum('bsh,he->bse', x, gate_w) + gate_b
        topk_vals, topk_idx = jax.lax.top_k(logits, K)
        topk_weights = jax.nn.softmax(topk_vals, axis=-1)
        mask = jax.nn.one_hot(topk_idx, E, dtype=topk_weights.dtype)
        weights = jnp.einsum('bske,bsk->bse', mask, topk_weights)
        h = jax.nn.relu(jnp.einsum('bsh,ehf->bsef', x, w1) + b1)
        expert_out = jnp.einsum('bsef,efh->bseh', h, w2) + b2
        return jnp.einsum('bseh,bse->bsh', expert_out, weights)
    h = _L0_tok_ref(x, L0_tok_w)
    h = h + _L0_attn_ref(_layernorm(h, axis=-1), L0_attn_in_proj_w, L0_attn_conv_fwd_w, L0_attn_conv_fwd_b, L0_attn_proj_fwd_w, L0_attn_proj_fwd_b, L0_attn_conv_bwd_w, L0_attn_conv_bwd_b, L0_attn_proj_bwd_w, L0_attn_proj_bwd_b, L0_attn_diag_weight, L0_attn_gate_scale, L0_attn_out_proj_w, L0_attn_ln_g, L0_attn_ln_b)
    h = h + _L0_ffn_ref(_layernorm(h, axis=-1), L0_ffn_Ws, L0_ffn_bs, L0_ffn_W1, L0_ffn_b1, L0_ffn_W2, L0_ffn_b2)
    h = h + _L1_attn_ref(_layernorm(h, axis=-1), L1_attn_in_proj_w, L1_attn_conv_w, L1_attn_conv_b, L1_attn_dt_bias, L1_attn_A_log, L1_attn_D_skip, L1_attn_norm_w, L1_attn_ssm_out_w, L1_attn_fuse_w, L1_attn_fuse_b)
    h = h + _L1_ffn_ref(_layernorm(h, axis=-1), L1_ffn_gate_w, L1_ffn_gate_b, L1_ffn_w1, L1_ffn_b1, L1_ffn_w2, L1_ffn_b2)
    return h

_drawn_inputs = setup_inputs


def setup_inputs(seed=0):
    import zlib

    import numpy as np

    out = dict(_drawn_inputs(seed))
    spreads = {'L0_attn_conv_fwd_b': (0.0, 0.8),
     'L0_attn_proj_fwd_b': (0.0, 0.8),
     'L0_attn_conv_bwd_b': (0.0, 0.8),
     'L0_attn_proj_bwd_b': (0.0, 0.8),
     'L0_attn_diag_weight': (0.10000000149011612, 0.6),
     'L0_attn_ln_g': (1.0, 0.2),
     'L0_attn_ln_b': (0.0, 0.1),
     'L0_ffn_bs': (0.0, 0.437),
     'L0_ffn_b1': (0.0, 0.8),
     'L0_ffn_b2': (0.0, 0.335),
     'L1_attn_conv_b': (0.0, 0.1),
     'L1_attn_D_skip': (1.0, 0.584),
     'L1_attn_norm_w': (1.0, 0.6),
     'L1_attn_fuse_b': (0.0, 0.1)}
    factors = {'L0_attn_in_proj_w': 8.0,
     'L0_attn_conv_fwd_w': 8.0,
     'L0_attn_proj_fwd_w': 8.0,
     'L0_attn_conv_bwd_w': 8.0,
     'L0_attn_proj_bwd_w': 8.0,
     'L0_attn_out_proj_w': 8.0,
     'L0_ffn_W1': 4.195,
     'L0_ffn_W2': 3.65,
     'L1_attn_conv_w': 4.177,
     'L1_attn_dt_bias': 8.0,
     'L1_attn_A_log': 8.0,
     'L1_ffn_b1': 4.261}
    for name, (base, spread) in spreads.items():
        noise = np.random.default_rng([zlib.crc32(name.encode()), seed]).standard_normal(out[name].shape)
        drawn = base * np.exp(spread * noise) if base else spread * noise
        out[name] = jnp.asarray(drawn.astype(out[name].dtype))
    for name, factor in factors.items():
        out[name] = (out[name] * factor).astype(out[name].dtype)
    return out
```

```python
from contextlib import ExitStack

import numpy as np

import concourse.bass as bass
from concourse import mybir

F32 = mybir.dt.float32
I32 = mybir.dt.int32
ALU = mybir.AluOpType
ACT = mybir.ActivationFunctionType
AX = mybir.AxisListType.X

P = 128
D = 128
NSEQ = 8
T = 512
NT = T // P
VOCAB = 50257
EPS = 1e-5
DI = 256
HB = DI // P
TAPS = 7
PAD = TAPS
XW = PAD + T + PAD
E = 8
F0 = 512
F1 = 256
CH = 512
CB = CH // P
MT = 4
NH = 4
HD = 64
PAIRS = NSEQ // 2
EXPERT_LOADS = 5 + NT
LAST_STAGE = "D"


def parts(nc, ctx, stage=""):
    def sb(name, shape, dt=F32):
        return ctx.enter_context(nc.sbuf_tensor(stage + name, shape, dt))

    def pb(name):
        return ctx.enter_context(nc.psum_tensor(stage + name, [P, 512], F32))

    def sem(name):
        return ctx.enter_context(nc.semaphore(stage + name))

    return sb, pb, sem


def slabs(eng, step):
    with eng.Fori(0, PAIRS - 1) as i:
        step(2 * i, 0, False)
        step(2 * i + 1, 1, False)
    step(NSEQ - 2, 0, False)
    step(NSEQ - 1, 1, True)


class Steps:

    def __init__(self, eng, sem, per, ahead=0):
        self.eng, self.sem, self.per, self.ahead = eng, sem, per, ahead
        self.n = 0
        self.base = 0

    def slab(self, s):
        self.n, self.base = 0, self.per * s + self.ahead

    def mark(self, ins):
        ins.then_inc(self.sem, 1)
        self.n += 1
        return self.n

    def need(self, n):
        self.eng.wait_ge(self.sem, self.base + n)

    def end(self):
        assert self.n == self.per, self.n


def expert_tensors(k, sb, n, f):
    k[f"r_w{n}"] = sb(f"r_w{n}", [P, E])
    k[f"r_b{n}"] = sb(f"r_b{n}", [P, E])
    k[f"w1_{n}"] = sb(f"w1_{n}", [P, E, f])
    k[f"b1_{n}"] = sb(f"b1_{n}", [P, E, f // P])
    k[f"w2_{n}"] = sb(f"w2_{n}", [P, E, f // P, D])
    k[f"b2_{n}"] = sb(f"b2_{n}", [NT * E, NT, D])


def expert_loads(w, k, n):
    router_w, router_b, w1, b1, w2, b2 = (w[name] for name in (
        ("L0_ffn_Ws", "L0_ffn_bs", "L0_ffn_W1", "L0_ffn_b1", "L0_ffn_W2", "L0_ffn_b2"),
        ("L1_ffn_gate_w", "L1_ffn_gate_b", "L1_ffn_w1", "L1_ffn_b1", "L1_ffn_w2", "L1_ffn_b2"))[n])
    loads = [(k[f"r_w{n}"][:], router_w), (k[f"r_b{n}"][:], router_b.partition_broadcast(P)),
             (k[f"w1_{n}"][:], w1.rearrange("e d f -> d e f")),
             (k[f"b1_{n}"][:], b1.rearrange("e (g p) -> p e g", p=P)),
             (k[f"w2_{n}"][:], w2.rearrange("e (g p) d -> p e g d", p=P))]
    for j in range(NT):
        loads.append((k[f"b2_{n}"][E * j:E * (j + 1), j, :], b2))
    assert len(loads) == EXPERT_LOADS
    return loads


def build(nc, w, out):
    with ExitStack() as ctx:
        sb, pb, sem = parts(nc, ctx)
        k = {}
        k["h"] = sb("h", [P, NSEQ * NT, D])
        k["ident"] = sb("ident", [P, P])
        k["ones"] = sb("ones", [P, P])
        for name in ("le", "lt", "ge", "gt"):
            k[name] = sb("mask_" + name, [P, P])
        k["mhalf"] = sb("minus_half", [P, 2 * NT])
        k["eps"] = sb("eps", [P, 2 * NT])
        k["held"] = sem("held")
        k["inv_di"] = sb("inv_di", [P, 2 * NT])
        k["euler"] = sb("euler", [P, NT * E])
        k["rank"] = sb("rank", [P, E])
        k["z_w"] = sb("z_w", [P, DI])
        k["dt_w"] = sb("dt_w", [P, NH])
        k["conv_w"] = sb("conv_w", [P, CB, MT, P])
        k["conv_b"] = sb("conv_b", [P, CB])
        k["dt_b"] = sb("dt_b", [P, NH])
        k["a_neg"] = sb("a_neg", [P, NH])
        k["skip"] = sb("skip", [P, HB, P])
        k["fuse_w"] = sb("fuse_w", [P, HB, 2, D])
        k["fuse_b"] = sb("fuse_b", [P, D])
        k["moe0_in"] = sem("moe0_in")
        k["moe1_in"] = sem("moe1_in")
        k["stored"] = sem("stored")
        with ExitStack() as half:
            sb0, _, _ = parts(nc, half)
            k["xz_w"] = sb0("xz_w", [P, 2 * DI])
            k["tap_w"] = sb0("tap_w", [P, 2 * TAPS, DI])
            k["tap_b"] = sb0("tap_b", [P, 2 * HB])
            k["diag"] = sb0("diag", [P, HB])
            k["out_w"] = sb0("out_w", [P, HB, D])
            k["ln_g"] = sb0("ln_g", [P, D])
            k["ln_b"] = sb0("ln_b", [P, D])
            expert_tensors(k, sb0, 0, F0)
            setup(nc, w, k)
            attention0(nc, k)
            mixture(nc, k, 0, F0)
        with ExitStack() as half:
            sb1, _, _ = parts(nc, half)
            expert_tensors(k, sb1, 1, F1)
            attention1(nc, k, expert_loads(w, k, 1))
            if LAST_STAGE >= "D":
                mixture(nc, k, 1, F1)
        with nc.Block() as block:
            @block.sync
            def _(sp):
                sp.wait_ge(k["moe1_in"], 16 * EXPERT_LOADS)
                for s in range(NSEQ):
                    sp.dma_start(out[s].rearrange("(j p) d -> p j d", p=P),
                                 k["h"][:, NT * s:NT * (s + 1), :]).then_inc(k["stored"], 16)
                sp.wait_ge(k["stored"], 16 * NSEQ)


def setup(nc, w, k):
    with ExitStack() as ctx:
        sb, pb, sem = parts(nc, ctx)
        ids = sb("ids", [P, NSEQ * NT], I32)
        xz_nat = sb("xz_nat", [P, 4, D])
        proj_nat = sb("proj_nat", [P, 2, HB, DI])
        tap = sb("tap", [P, 2, HB, TAPS])
        conv_bias = sb("conv_bias", [P, 2, HB])
        proj_bias = sb("proj_bias", [P, 2 * HB])
        gate_scale = sb("gate_scale", [P, 1])
        out_nat = sb("out_nat", [P, DI])
        proj_t = sb("proj_t", [P, 2, HB, DI])
        scaled = sb("scaled", [P, 2 * TAPS, HB, DI])
        in_nat = sb("in_nat", [P, 6, D])
        dt_nat = sb("dt_nat", [NH, D])
        mtap = sb("mtap", [P, CB, MT])
        in_scaled = sb("in_scaled", [P, CB, MT, D])
        a_log = sb("a_log", [P, NH])
        a_exp = sb("a_exp", [P, NH])
        skip_col = sb("skip_col", [P, HB])
        norm_col = sb("norm_col", [P, HB])
        ssm_nat = sb("ssm_nat", [P, DI])
        fuse_nat = sb("fuse_nat", [P, 2, D])
        fuse_t = sb("fuse_t", [P, 2, D])
        bank = [pb(f"setup_bank{i}") for i in range(8)]
        ids_in, weights_in, gathered = sem("ids_in"), sem("weights_in"), sem("gathered")
        consts, b2_zero = sem("consts"), sem("b2_zero")
        group_ready, group_used = sem("group_ready"), sem("group_used")
        scaled_ready, exp_ready = sem("scaled_ready"), sem("exp_ready")

        def row(a):
            return a.partition_broadcast(P)

        def cols(a, n):
            return a.rearrange("(b p) -> p b", p=P)

        early = [
            (xz_nat[:], w["L0_attn_in_proj_w"].rearrange("(g p) d -> p g d", p=P)),
            (proj_nat[:, 0], w["L0_attn_proj_fwd_w"].rearrange("(g p) c -> p g c", p=P)),
            (proj_nat[:, 1], w["L0_attn_proj_bwd_w"].rearrange("(g p) c -> p g c", p=P)),
            (tap[:, 0], w["L0_attn_conv_fwd_w"].rearrange("(g p) o k -> p g (o k)", p=P)),
            (tap[:, 1], w["L0_attn_conv_bwd_w"].rearrange("(g p) o k -> p g (o k)", p=P)),
            (out_nat[:], w["L0_attn_out_proj_w"]),
            (in_nat[:], w["L1_attn_in_proj_w"][0:6 * P].rearrange("(g p) d -> p g d", p=P)),
            (dt_nat[:], w["L1_attn_in_proj_w"][6 * P:6 * P + NH]),
            (mtap[:], w["L1_attn_conv_w"].rearrange("(g p) o k -> p g (o k)", p=P)),
            (ssm_nat[:], w["L1_attn_ssm_out_w"]),
            (fuse_nat[:], w["L1_attn_fuse_w"].rearrange("o (g m) -> o g m", g=2)),
        ]
        small = [
            (gate_scale[:], row(w["L0_attn_gate_scale"])),
            (k["ln_g"][:], row(w["L0_attn_ln_g"])), (k["ln_b"][:], row(w["L0_attn_ln_b"])),
            (k["dt_b"][:], row(w["L1_attn_dt_bias"])), (a_log[:], row(w["L1_attn_A_log"])),
            (k["fuse_b"][:], row(w["L1_attn_fuse_b"])),
        ]
        for d, n in enumerate(("fwd", "bwd")):
            for g in range(HB):
                small.append((conv_bias[:, d, g:g + 1], w[f"L0_attn_conv_{n}_b"][g * P:(g + 1) * P].unsqueeze(1)))
                small.append((proj_bias[:, HB * d + g:HB * d + g + 1],
                              w[f"L0_attn_proj_{n}_b"][g * P:(g + 1) * P].unsqueeze(1)))
        for g in range(HB):
            small.append((k["diag"][:, g:g + 1], w["L0_attn_diag_weight"][g * P:(g + 1) * P].unsqueeze(1)))
            small.append((norm_col[:, g:g + 1], w["L1_attn_norm_w"][g * P:(g + 1) * P].unsqueeze(1)))
            for j in range(2):
                small.append((skip_col[HD * j:HD * (j + 1), g:g + 1],
                              w["L1_attn_D_skip"][2 * g + j:2 * g + j + 1].partition_broadcast(HD)))
        for g in range(CB):
            small.append((k["conv_b"][:, g:g + 1], w["L1_attn_conv_b"][g * P:(g + 1) * P].unsqueeze(1)))
        n_weights = len(early) + len(small)

        block = ctx.enter_context(nc.Block())

        @block.sync
        def _(sp):
            with nc.allow_non_contiguous_dma("bias columns"):
                sp.dma_start(ids[:], w["x"].rearrange("s (j p) -> p (s j)", p=P)).then_inc(ids_in, 16)
                for dst, src in early + small:
                    sp.dma_start(dst, src).then_inc(weights_in, 16)
                sp.wait_ge(b2_zero, 1)
                for dst, src in expert_loads(w, k, 0):
                    sp.dma_start(dst, src).then_inc(k["moe0_in"], 16)

        @block.gpsimd
        def _(pool):
            nc.gpsimd.memset(k["b2_0"][:], 0.0).then_inc(b2_zero, 1)
            for name in ("ident", "ones", "le", "lt", "ge", "gt"):
                nc.gpsimd.memset(k[name][:], 0.0 if name == "ident" else 1.0).then_inc(consts, 1)
            nc.gpsimd.memset(k["mhalf"][:], -0.5).then_inc(consts, 1)
            nc.gpsimd.memset(k["eps"][:], EPS).then_inc(consts, 1)
            nc.gpsimd.memset(k["euler"][:], float(np.e)).then_inc(consts, 1)
            nc.gpsimd.memset(k["inv_di"][:], 1.0 / DI).then_inc(consts, 1)
            for e in range(E):
                nc.gpsimd.memset(k["rank"][:, e:e + 1], float(E - e)).then_inc(consts, 1)
            pool.wait_ge(consts, 10 + E)
            for name, cmp, cm, step, fill in (("ident", ALU.not_equal, 1, -1, 1.0), ("le", ALU.is_ge, -1, 1, 0.0),
                                              ("lt", ALU.is_gt, -1, 1, 0.0), ("ge", ALU.is_ge, 1, -1, 0.0),
                                              ("gt", ALU.is_gt, 1, -1, 0.0)):
                nc.gpsimd.affine_select(out=k[name][:], in_=k[name][:], compare_op=cmp, fill=fill, base=0,
                                        pattern=[[step, P]], channel_multiplier=cm).then_inc(consts, 1)
            pool.wait_ge(ids_in, 16)
            for n in range(NSEQ * NT):
                pool.indirect_dma_start(out=k["h"][:, n, :], out_offset=None, in_=w["L0_tok_w"],
                                        in_offset=bass.IndirectOffsetOnAxis(ap=ids[:, n:n + 1], axis=0),
                                        ).then_inc(gathered, 16)
            pool.wait_ge(gathered, 16 * NSEQ * NT)

        n_consts = 10 + E + 5

        @block.tensor
        def _(pe):
            pe.wait_ge(consts, n_consts)
            pe.wait_ge(weights_in, 16 * n_weights)
            g = [0]

            def group(work):
                if g[0] >= 8:
                    pe.wait_ge(group_used, g[0] - 7)
                last = work(bank[g[0] % 8])
                last.then_inc(group_ready, 1)
                g[0] += 1

            def transposes(sources):
                def work(b):
                    for n, src in enumerate(sources):
                        rows = src.shape[0]
                        last = nc.tensor.transpose(b[:, P * n:P * n + rows], src, k["ident"][0:rows, 0:rows])
                    return last
                return work

            group(transposes([xz_nat[:, n, :] for n in range(4)]))
            for d in range(2):
                group(transposes([proj_nat[:, d, o, P * c:P * (c + 1)] for c in range(HB) for o in range(HB)]))
            group(transposes([out_nat[:, 0:P], out_nat[:, P:DI], fuse_nat[:, 0, :], fuse_nat[:, 1, :]]))
            group(transposes([in_nat[:, 0, :], in_nat[:, 1, :], dt_nat[:, :]]))
            pe.wait_ge(scaled_ready, 1)
            for b in range(CB):
                group(transposes([in_scaled[:, b, t, :] for t in range(MT)]))
            pe.wait_ge(scaled_ready, 2)

            def tap_products(q):
                def work(b):
                    for m in (2 * q, 2 * q + 1):
                        for c in range(HB):
                            last = nc.tensor.matmul(b[:, DI * (m % 2):DI * (m % 2 + 1)], xz_nat[:, c, :],
                                                    scaled[:, m, c, :], start=(c == 0), stop=(c == HB - 1))
                    return last
                return work

            for q in range(TAPS):
                group(tap_products(q))

            def bias_products(b):
                for d in range(2):
                    for o in range(HB):
                        for c in range(HB):
                            last = nc.tensor.matmul(b[:, HB * d + o:HB * d + o + 1],
                                                    proj_t[:, d, c, P * o:P * (o + 1)], conv_bias[:, d, c:c + 1],
                                                    start=(c == 0), stop=(c == HB - 1))
                return last

            group(bias_products)
            pe.wait_ge(group_used, 4)

            def fuse_products(b):
                for c in range(HB):
                    last = nc.tensor.matmul(b[:, 2 * D * c:2 * D * (c + 1)], ssm_nat[:, P * c:P * (c + 1)],
                                            fuse_t[:, :, :].rearrange("m g o -> m (g o)"), start=True, stop=True)
                return last

            group(fuse_products)

        @block.scalar
        def _(act):
            act.wait_ge(weights_in, 16 * n_weights)
            nc.scalar.activation(a_exp[:], a_log[:], ACT.Exp).then_inc(exp_ready, 1)
            g = [0]

            def used(*copies):
                act.wait_ge(group_ready, g[0] + 1)
                for dst, lo, hi, scale in copies:
                    src = bank[g[0] % 8][:, lo:hi]
                    last = nc.scalar.activation(dst, src, ACT.Copy, scale=scale)
                last.then_inc(group_used, 1)
                g[0] += 1

            used((k["xz_w"][:], 0, 512, 1.0))
            for d in range(2):
                used((proj_t[:, d].rearrange("p c o -> p (c o)"), 0, 512, 1.0))
            used((k["out_w"][:].rearrange("p g d -> p (g d)"), 0, DI, gate_scale[:, 0:1]),
                 (fuse_t[:].rearrange("p g d -> p (g d)"), DI, 2 * DI, 1.0))
            used((k["z_w"][:], 0, DI, 1.0), (k["dt_w"][:], DI, DI + NH, 1.0))
            for b in range(CB):
                used((k["conv_w"][:, b].rearrange("p t d -> p (t d)"), 0, 512, 1.0))
            for q in range(TAPS):
                used((k["tap_w"][:, 2 * q:2 * q + 2].rearrange("p t d -> p (t d)"), 0, 512, 1.0))
            act.wait_ge(group_ready, g[0] + 1)
            for n in range(2 * HB):
                last = nc.scalar.activation(k["tap_b"][:, n:n + 1], bank[g[0] % 8][:, n:n + 1], ACT.Identity,
                                            bias=proj_bias[:, n:n + 1])
            last.then_inc(group_used, 1)
            g[0] += 1
            act.wait_ge(group_ready, g[0] + 1)
            for c in range(HB):
                last = nc.scalar.activation(k["fuse_w"][:, c].rearrange("p g d -> p (g d)"),
                                            bank[g[0] % 8][:, 2 * D * c:2 * D * (c + 1)], ACT.Copy,
                                            scale=norm_col[:, c:c + 1])
            last.then_inc(group_used, 1)

        @block.vector
        def _(dve):
            dve.wait_ge(weights_in, 16 * n_weights)
            for b in range(CB):
                for t in range(MT):
                    last = nc.vector.tensor_scalar(in_scaled[:, b, t, :], in_nat[:, 2 + b, :], mtap[:, b, t:t + 1],
                                                   None, ALU.mult)
            last.then_inc(scaled_ready, 1)
            dve.wait_ge(group_used, 3)
            for d in range(2):
                for t in range(TAPS):
                    for c in range(HB):
                        last = nc.vector.tensor_scalar(scaled[:, TAPS * d + t, c, :], proj_t[:, d, c, :],
                                                       tap[:, d, c, t:t + 1], None, ALU.mult)
            last.then_inc(scaled_ready, 1)
            dve.wait_ge(consts, n_consts)
            for c in range(HB):
                nc.vector.tensor_scalar(k["skip"][:, c, :], k["ident"][:], skip_col[:, c:c + 1], None, ALU.mult)
            dve.wait_ge(exp_ready, 1)
            nc.vector.tensor_scalar(k["a_neg"][:], a_exp[:], -1.0, None, ALU.mult)


def front_tensors(sb):
    return {
        "stats": sb("stats", [P, NT, 6]),
        "mv": sb("mv", [P, NT, 2]),
        "var": sb("var", [P, NT]),
        "rstd": sb("rstd", [P, NT]),
        "xn": [sb(f"xn{u}", [P, NT, D]) for u in range(2)],
        "xf": [sb(f"xf{u}", [P, XW]) for u in range(2)],
    }


def stat_steps(nc, k, st, f, src, var_ready):
    for j in range(NT):
        st.mark(nc.vector.bn_stats(f["stats"][:, j, :], src[:, j, :]))
    st.need(st.n)
    nc.vector.sem_inc(k["held"], 1)
    for j in range(NT):
        st.mark(nc.vector.bn_aggr(f["mv"][:, j, :], f["stats"][:, j, :]))
    st.need(st.n)
    nc.vector.tensor_copy(f["var"][:], f["mv"][:, :, 1]).then_inc(var_ready, 1)


def normalise(nc, k, st, f, s, u, var_ready, rstd_ready, xn_ready):
    stat_steps(nc, k, st, f, k["h"][:, bass.ds(NT * s, NT), :], var_ready)
    nc.vector.wait_ge(rstd_ready, s + 1)
    for j in range(NT):
        tile = k["h"][:, bass.ds(NT * s + j, 1), :].rearrange("p a d -> p (a d)")
        last = nc.vector.tensor_scalar(f["xn"][u][:, j, :], tile, f["mv"][:, j, 0:1], f["rstd"][:, j:j + 1],
                                       ALU.subtract, ALU.mult)
    last.then_inc(xn_ready, 1)


def rstd_steps(nc, pool, f, k, var_ready, var_eps, rstd_ready, n):
    pool.wait_ge(var_ready, n)
    nc.gpsimd.tensor_tensor(f["var"][:], f["var"][:], k["eps"][:, 0:NT], ALU.add).then_inc(var_eps, 1)
    pool.wait_ge(var_eps, n)
    nc.gpsimd.tensor_tensor(f["rstd"][:], f["var"][:], k["mhalf"][:, 0:NT], ALU.pow).then_inc(rstd_ready, 1)


def attention0(nc, k):
    with ExitStack() as ctx:
        sb, pb, sem = parts(nc, ctx, "a_")
        f = front_tensors(sb)
        f2 = {"stats": sb("stats2", [P, NT, 6]), "mv": sb("mv2", [P, NT, 2]), "var": sb("var2", [P, NT]),
              "rstd": sb("rstd2", [P, NT])}
        mix = sb("mix", [P, 4, T])
        gate = sb("gate", [P, HB, T])
        both = sb("both", [P, HB, T])
        both_d = sb("both_d", [P, HB, T])
        y = sb("y", [P, HB, T])
        res = sb("res", [P, NT, D])
        nrm = sb("nrm", [P, NT, D])
        nrm_g = sb("nrm_g", [P, NT, D])
        nrm_b = sb("nrm_b", [P, NT, D])
        bank = [pb(f"bank{i}") for i in range(8)]
        edges = sem("edges")
        var_ready, var_eps, rstd_ready = sem("var"), sem("eps"), sem("rstd")
        var2_ready, var2_eps, rstd2_ready = sem("var2"), sem("eps2"), sem("rstd2")
        xn_ready, xt_ready, xf_ready = sem("xn"), sem("xt"), sem("xf")
        conv_ready, silu_ready, xp_used = sem("conv"), sem("silu"), sem("xp_used")
        y_ready, out_ready, out_used = sem("y"), sem("out"), sem("out_used")
        dve_step = sem("dve")

        block = ctx.enter_context(nc.Block())
        h = k["h"]

        PER_SLAB = 2 * NT + 2 * HB + 1 + 2 * NT + NT + 2

        @block.vector
        def _(dve):
            dve.sem_inc(y_ready, 1)
            dve.sem_inc(out_used, 1)
            for u in range(2):
                nc.vector.memset(f["xf"][u][:, 0:PAD], 0.0).then_inc(edges, 1)
                nc.vector.memset(f["xf"][u][:, PAD + T:XW], 0.0).then_inc(edges, 1)
            nc.vector.memset(mix[:, 0:2, 0:1], 0.0).then_inc(edges, 1)
            nc.vector.memset(mix[:, 2:4, T - 1:T], 0.0).then_inc(edges, 1)
            dve.wait_ge(edges, 6)
            st = Steps(dve, dve_step, PER_SLAB, ahead=2 * NT)
            st.n, st.base = 0, 0
            normalise(nc, k, st, f, 0, 0, var_ready, rstd_ready, xn_ready)

            def step(s, u, last_slab):
                st.slab(s)
                if not last_slab:
                    normalise(nc, k, st, f, s + 1, 1 - u, var_ready, rstd_ready, xn_ready)
                for g in range(HB):
                    dve.wait_ge(silu_ready, 6 * s + 4 + g)
                    a = st.mark(nc.vector.tensor_tensor(both[:, g, :], mix[:, g, :], mix[:, 2 + g, :], ALU.add))
                    dve.wait_ge(conv_ready, 8 * s + 7 + g)
                    st.need(a)
                    b = st.mark(nc.vector.scalar_tensor_tensor(both_d[:, g, :], bank[4 + g][:], k["diag"][:, g:g + 1],
                                                               both[:, g, :], ALU.mult, ALU.add))
                    dve.wait_ge(silu_ready, 6 * s + 6 + g)
                    st.need(b)
                    nc.vector.tensor_tensor(y[:, g, :], both_d[:, g, :], gate[:, g, :], ALU.mult).then_inc(y_ready, 1)
                dve.wait_ge(out_ready, s + 1)
                r = st.mark(nc.vector.tensor_tensor(res[:].rearrange("p j d -> p (j d)"), bank[7][:],
                                                    f["xn"][u][:].rearrange("p j d -> p (j d)"), ALU.add))
                st.need(r)
                stat_steps(nc, k, st, f2, res, var2_ready)
                dve.wait_ge(rstd2_ready, s + 1)
                for j in range(NT):
                    n = st.mark(nc.vector.tensor_scalar(nrm[:, j, :], res[:, j, :], f2["mv"][:, j, 0:1],
                                                        f2["rstd"][:, j:j + 1], ALU.subtract, ALU.mult))
                st.need(n)
                n = st.mark(nc.vector.tensor_tensor(nrm_g[:], nrm[:],
                                                    k["ln_g"][:].unsqueeze(1).broadcast_to([P, NT, D]), ALU.mult))
                st.need(n)
                n = st.mark(nc.vector.tensor_tensor(nrm_b[:], nrm_g[:],
                                                    k["ln_b"][:].unsqueeze(1).broadcast_to([P, NT, D]), ALU.add))
                st.need(n)
                hs = h[:, bass.ds(NT * s, NT), :]
                nc.vector.tensor_tensor(hs, hs, nrm_b[:], ALU.add).then_inc(out_used, 1)
                if not last_slab:
                    st.end()

            slabs(dve, step)

        @block.gpsimd
        def _(pool):
            rstd_steps(nc, pool, f, k, var_ready, var_eps, rstd_ready, 1)

            def step(s, u, last_slab):
                if not last_slab:
                    rstd_steps(nc, pool, f, k, var_ready, var_eps, rstd_ready, s + 2)
                rstd_steps(nc, pool, f2, k, var2_ready, var2_eps, rstd2_ready, s + 1)

            slabs(pool, step)

        @block.tensor
        def _(pe):
            def transposes(s, u):
                pe.wait_ge(xn_ready, s + 1)
                pe.wait_ge(xf_ready, s + 1)
                for j in range(NT):
                    last = nc.tensor.transpose(bank[6][:, P * j:P * (j + 1)], f["xn"][u][:, j, :], k["ident"][:])
                last.then_inc(xt_ready, 1)

            pe.wait_ge(edges, 6)
            transposes(0, 0)

            def step(s, u, last_slab):
                x = f["xf"][u]
                pe.wait_ge(xf_ready, s + 2)
                pe.wait_ge(silu_ready, 6 * s + 1)
                for d in range(2):
                    for g in range(HB):
                        for t in range(TAPS):
                            at = t if d == 0 else 2 * PAD - t
                            last = nc.tensor.matmul(bank[2 * d + g][:], k["tap_w"][:, TAPS * d + t, P * g:P * (g + 1)],
                                                    x[:, at:at + T], start=(t == 0), stop=(t == TAPS - 1))
                        last.then_inc(conv_ready, 1)
                for g in range(HB):
                    pe.wait_ge(silu_ready, 6 * s + 2 + g)
                    nc.tensor.matmul(bank[g][:], k["xz_w"][:, DI + P * g:DI + P * (g + 1)], x[:, PAD:PAD + T],
                                     start=True, stop=True).then_inc(conv_ready, 1)
                pe.wait_ge(y_ready, 2 * s + 1)
                for g in range(HB):
                    nc.tensor.matmul(bank[4 + g][:], k["xz_w"][:, P * g:P * (g + 1)], x[:, PAD:PAD + T],
                                     start=True, stop=True).then_inc(conv_ready, 1)
                if not last_slab:
                    transposes(s + 1, 1 - u)
                pe.wait_ge(out_used, s + 1)
                pe.wait_ge(y_ready, 2 * s + 3)
                for j in range(NT):
                    for g in range(HB):
                        last = nc.tensor.matmul(bank[7][:, D * j:D * (j + 1)], y[:, g, P * j:P * (j + 1)],
                                                k["out_w"][:, g, :], start=(g == 0), stop=(g == HB - 1))
                last.then_inc(out_ready, 1)

            slabs(pe, step)

        @block.scalar
        def _(act):
            def xf_copy(s, u):
                act.wait_ge(xt_ready, s + 1)
                nc.scalar.activation(f["xf"][u][:, PAD:PAD + T], bank[6][:], ACT.Copy).then_inc(xf_ready, 1)

            act.sem_inc(xf_ready, 1)
            act.sem_inc(silu_ready, 1)
            xf_copy(0, 0)

            def step(s, u, last_slab):
                act.wait_ge(y_ready, 2 * s + 1)
                for d in range(2):
                    for g in range(HB):
                        lo, hi = (1, T) if d == 0 else (0, T - 1)
                        act.wait_ge(conv_ready, 8 * s + 2 * d + g + 1)
                        nc.scalar.activation(mix[:, 2 * d + g, lo:hi], bank[2 * d + g][:, lo:hi], ACT.Silu,
                                             bias=k["tap_b"][:, 2 * d + g:2 * d + g + 1]).then_inc(silu_ready, 1)
                for g in range(HB):
                    act.wait_ge(conv_ready, 8 * s + 5 + g)
                    nc.scalar.activation(gate[:, g, :], bank[g][:], ACT.Silu).then_inc(silu_ready, 1)
                if not last_slab:
                    xf_copy(s + 1, 1 - u)

            slabs(act, step)


def attention1(nc, k, loads):
    with ExitStack() as ctx:
        sb, pb, sem = parts(nc, ctx, "c_")
        C = 2 * NT
        f = front_tensors(sb)
        act_x = [sb(f"act_x{u}", [P, 2, CB, T]) for u in range(2)]
        zs = [sb(f"zs{u}", [P, NT, DI]) for u in range(2)]
        dt_raw = sb("dt_raw", [P, NT, NH])
        dt_x = sb("dt_x", [P, NT, NH])
        dt_n = sb("dt_n", [P, NT, NH])
        dt_e = sb("dt_e", [P, NT, NH])
        dt_l = sb("dt_l", [P, NT, NH])
        dt = [sb(f"dt{u}", [P, NT, NH]) for u in range(2)]
        da = [sb(f"da{u}", [P, NT, NH]) for u in range(2)]
        dec = [sb(f"dec{u}", [P, 5, NT, NH]) for u in range(2)]
        seg_in = [sb(f"seg_in{i}", [P, NH, P]) for i in range(2)]
        decay = [sb(f"decay{i}", [P, NH, P]) for i in range(2)]
        cb = [sb(f"cb{i}", [P, P]) for i in range(2)]
        mixer = sb("mixer", [P, C, NH, P])
        xdt = sb("xdt", [P, C, DI])
        xdd = sb("xdd", [P, C, DI])
        b_t = sb("b_t", [P, C, P])
        state = [sb(f"state{d}", [P, DI]) for d in range(2)]
        state_d = [sb(f"state_d{d}", [P, DI]) for d in range(2)]
        y_off = [sb(f"y_off{d}", [P, DI]) for d in range(2)]
        y_sum = [sb(f"y_sum{d}", [P, DI]) for d in range(2)]
        y = sb("y", [P, C, DI])
        ss = sb("ss", [P, C])
        ms = sb("ms", [P, C])
        mse = sb("mse", [P, C])
        rr = sb("rr", [P, C])
        yn = sb("yn", [P, C, DI])
        yt = [sb(f"yt{i}", [P, 4, P]) for i in range(2)]
        o = sb("o", [P, NT, D])
        bank = [pb(f"bank{i}") for i in range(8)]
        var_ready, var_eps, rstd_ready = sem("var"), sem("eps"), sem("rstd")
        xn_ready, edges, b2_zero = sem("xn"), sem("edges"), sem("b2_zero")
        front_ready, front_used = sem("front"), sem("front_used")
        dtx_ready, sp_step, sp_ready, da_ready = sem("dtx"), sem("sp_step"), sem("sp"), sem("da")
        tpx_ready, g_ready, seg_ready = sem("tpx"), sem("g"), sem("seg")
        seg_in_ready, seg_in_used = sem("seg_in"), sem("seg_in_used")
        xdt_ready, bt_ready, xdd_ready = sem("xdt"), sem("bt"), sem("xdd")
        cb_ready, decay_ready, mixer_ready = sem("cb"), sem("decay"), sem("mixer")
        y_ready, y_used, st_ready, st_used, y2_ready = sem("y"), sem("y_used"), sem("st"), sem("st_used"), sem("y2")
        ss_ready, ms_step, rr_ready, yn_ready = sem("ss"), sem("ms"), sem("rr"), sem("yn")
        yt_ready, yt_used, out_ready, out_used = sem("yt"), sem("yt_used"), sem("out"), sem("out_used")
        dve_step = sem("dve")
        h = k["h"]

        FRONT = 13

        def chunk(c):
            return c % 2, c // 2 if c % 2 == 0 else NT - 1 - c // 2

        SUMS = (("gt", "le"), ("lt", "ge"))
        INTO, OUT, TOTAL = (0, 3), (1, 4), 2

        block = ctx.enter_context(nc.Block())

        def heads(t):
            return t.rearrange("p (h d) -> p h d", h=NH)

        def per_head(t):
            return t.unsqueeze(2).broadcast_to([P, NH, HD])

        @block.sync
        def _(sp):
            with nc.allow_non_contiguous_dma("bias columns"):
                sp.wait_ge(b2_zero, 1)
                for dst, src in loads:
                    sp.dma_start(dst, src).then_inc(k["moe1_in"], 16)

        @block.vector
        def _(dve):
            nc.vector.memset(k["b2_1"][:], 0.0).then_inc(b2_zero, 1)
            dve.sem_inc(out_used, 1)
            dve.sem_inc(xdt_ready, 2)
            dve.sem_inc(cb_ready, 2)
            dve.sem_inc(mixer_ready, 2)
            dve.sem_inc(y_used, 1)
            dve.sem_inc(st_used, 1)
            for u in range(2):
                nc.vector.memset(f["xf"][u][:, 0:PAD], 0.0).then_inc(edges, 1)
                nc.vector.memset(f["xf"][u][:, PAD + T:XW], 0.0).then_inc(edges, 1)
            dve.wait_ge(edges, 4)
            AHEAD = 2 * NT + 2
            st = Steps(dve, dve_step, AHEAD + 2 * (C - 2) + (C - 4) + 1, ahead=AHEAD)

            def dt_steps(s, u):
                dve.wait_ge(front_used, FRONT * s + 3)
                n = st.mark(nc.vector.tensor_tensor(dt_x[:], dt_raw[:], k["dt_b"][:].unsqueeze(1).broadcast_to([P, NT, NH]), ALU.add))
                st.need(n)
                nc.vector.scalar_tensor_tensor(dt_n[:], dt_x[:], -1.0, dt_x[:], ALU.mult, ALU.min).then_inc(dtx_ready, 1)
                dve.wait_ge(sp_ready, s + 1)
                n = st.mark(nc.vector.scalar_tensor_tensor(dt[u][:], dt_x[:], 0.0, dt_l[:], ALU.max, ALU.add))
                st.need(n)
                nc.vector.tensor_tensor(da[u][:], dt[u][:], k["a_neg"][:].unsqueeze(1).broadcast_to([P, NT, NH]), ALU.mult).then_inc(da_ready, 1)

            st.n, st.base = 0, 0
            normalise(nc, k, st, f, 0, 0, var_ready, rstd_ready, xn_ready)
            dt_steps(0, 0)

            def step(s, u, last_slab):
                st.slab(s)
                if not last_slab:
                    normalise(nc, k, st, f, s + 1, 1 - u, var_ready, rstd_ready, xn_ready)
                for c in range(C):
                    d, j = chunk(c)
                    dve.wait_ge(tpx_ready, C * s + c + 1)
                    nc.vector.tensor_tensor(heads(xdt[:, c, :]), heads(bank[2 + c % 2][:, 0:DI]),
                                            per_head(dt[u][:, j, :]), ALU.mult).then_inc(xdt_ready, 1)
                    dve.wait_ge(g_ready, C * s + c + 1)
                    nc.vector.tensor_tensor(cb[c % 2][:], bank[4 + 2 * (c % 2)][:, 0:P],
                                            k[SUMS[d][1]][:], ALU.mult).then_inc(cb_ready, 1)
                    dve.wait_ge(decay_ready, C * s + c + 3)
                    dve.wait_ge(cb_ready, C * s + c + 3)
                    nc.vector.tensor_tensor(mixer[:, c], decay[c % 2][:],
                                            cb[c % 2][:].unsqueeze(1).broadcast_to([P, NH, P]), ALU.mult).then_inc(mixer_ready, 1)
                if not last_slab:
                    dt_steps(s + 1, 1 - u)
                for c in range(C):
                    d, j = chunk(c)
                    dve.wait_ge(y_ready, C * s + c + 1)
                    if c >= 2:
                        n = st.mark(nc.vector.tensor_tensor(heads(y_off[d][:]), heads(bank[4 + 2 * d][:, DI:2 * DI]),
                                                            per_head(dec[u][:, OUT[d], j, :]), ALU.mult))
                        st.need(n)
                        n = st.mark(nc.vector.tensor_tensor(y_sum[d][:], bank[4 + 2 * d][:, 0:DI], y_off[d][:], ALU.add))
                        st.need(n)
                        dve.sem_inc(y_used, 1)
                        nc.vector.tensor_tensor(y[:, c, :], y_sum[d][:], zs[u][:, j, :], ALU.mult).then_inc(y2_ready, 1)
                    else:
                        nc.vector.tensor_tensor(y[:, c, :], bank[4 + 2 * d][:, 0:DI], zs[u][:, j, :],
                                                ALU.mult).then_inc(y2_ready, 1)
                        dve.wait_ge(y2_ready, C * s + c + 1)
                        dve.sem_inc(y_used, 1)
                    if c < C - 2:
                        if c < 2:
                            dve.wait_ge(st_ready, (C - 2) * s + c + 1)
                            nc.vector.tensor_copy(state[d][:], bank[5 + 2 * d][:, 0:DI]).then_inc(st_used, 1)
                        else:
                            n = st.mark(nc.vector.tensor_tensor(heads(state_d[d][:]), heads(state[d][:]),
                                                                per_head(dec[u][:, TOTAL, j, :]), ALU.mult))
                            st.need(n)
                            dve.wait_ge(st_ready, (C - 2) * s + c + 1)
                            nc.vector.tensor_tensor(state[d][:], state_d[d][:], bank[5 + 2 * d][:, 0:DI],
                                                    ALU.add).then_inc(st_used, 1)
                dve.wait_ge(rr_ready, s + 1)
                for c in range(C):
                    nc.vector.tensor_scalar(yn[:, c, :], y[:, c, :], rr[:, c:c + 1], None, ALU.mult).then_inc(yn_ready, 1)
                dve.wait_ge(out_ready, NT * s + NT + 2)
                n = st.mark(nc.vector.tensor_tensor(o[:], bank[1][:].rearrange("p (j d) -> p j d", d=D),
                                                    k["fuse_b"][:].unsqueeze(1).broadcast_to([P, NT, D]), ALU.add))
                st.need(n)
                hs = h[:, bass.ds(NT * s, NT), :]
                nc.vector.tensor_tensor(hs, hs, o[:], ALU.add).then_inc(out_used, 1)
                if not last_slab:
                    st.end()

            slabs(dve, step)

        @block.gpsimd
        def _(pool):
            rstd_steps(nc, pool, f, k, var_ready, var_eps, rstd_ready, 1)

            def step(s, u, last_slab):
                if not last_slab:
                    rstd_steps(nc, pool, f, k, var_ready, var_eps, rstd_ready, s + 2)
                pool.wait_ge(da_ready, s + 1)
                for c in range(C):
                    d, j = chunk(c)
                    pool.wait_ge(seg_in_used, C * s + c + 1)
                    nc.gpsimd.tensor_tensor(seg_in[c % 2][:], k[SUMS[d][1]][:].unsqueeze(1).broadcast_to([P, NH, P]),
                                            da[u][:, j, :].unsqueeze(2).broadcast_to([P, NH, P]),
                                            ALU.mult).then_inc(seg_in_ready, 1)
                    if c == 0:
                        pool.wait_ge(front_used, FRONT * (s + 1) + 1)
                    if c >= 1:
                        into_state(s, u, c - 1)
                into_state(s, u, C - 1)
                pool.wait_ge(ss_ready, C * s + C)
                nc.gpsimd.tensor_tensor(ms[:], ss[:], k["inv_di"][:], ALU.mult).then_inc(ms_step, 1)
                pool.wait_ge(ms_step, 2 * s + 1)
                nc.gpsimd.tensor_tensor(mse[:], ms[:], k["eps"][:], ALU.add).then_inc(ms_step, 1)
                pool.wait_ge(ms_step, 2 * s + 2)
                nc.gpsimd.tensor_tensor(rr[:], mse[:], k["mhalf"][:], ALU.pow).then_inc(rr_ready, 1)

            def into_state(s, u, c):
                d, j = chunk(c)
                pool.wait_ge(xdt_ready, C * s + c + 3)
                nc.gpsimd.tensor_tensor(heads(xdd[:, c, :]), heads(xdt[:, c, :]), per_head(dec[u][:, INTO[d], j, :]),
                                        ALU.mult).then_inc(xdd_ready, 1)

            slabs(pool, step)

        @block.tensor
        def _(pe):
            pe.sem_inc(seg_in_used, 2)
            pe.sem_inc(out_ready, 2)
            pe.wait_ge(edges, 4)

            def front(s, u):
                x = f["xf"][u]

                def turn(n):
                    pe.wait_ge(front_used, FRONT * s + n)
                    return bank[n % 2]

                pe.wait_ge(xn_ready, s + 1)
                b = bank[0]
                pe.wait_ge(front_used, FRONT * s + 1)
                for j in range(NT):
                    last = nc.tensor.transpose(b[:, P * j:P * (j + 1)], f["xn"][u][:, j, :], k["ident"][:])
                last.then_inc(front_ready, 1)
                pe.wait_ge(front_used, FRONT * s + 2)
                for j in range(NT):
                    last = nc.tensor.matmul(bank[1][:, NH * j:NH * (j + 1)], x[:, PAD + P * j:PAD + P * (j + 1)],
                                            k["dt_w"][:], start=True, stop=True)
                last.then_inc(front_ready, 1)
                for n in range(2 * CB):
                    d, blk = n // CB, n % CB
                    b = turn(2 + n)
                    for t in range(MT):
                        at = PAD - (MT - 1) + t if d == 0 else PAD + (MT - 1) - t
                        last = nc.tensor.matmul(b[:], k["conv_w"][:, blk, t, :], x[:, at:at + T],
                                                start=(t == 0), stop=(t == MT - 1))
                    last.then_inc(front_ready, 1)
                for n in range(2):
                    b = turn(10 + n)
                    for j in (2 * n, 2 * n + 1):
                        last = nc.tensor.matmul(b[:, DI * (j % 2):DI * (j % 2 + 1)],
                                                x[:, PAD + P * j:PAD + P * (j + 1)], k["z_w"][:], start=True, stop=True)
                    last.then_inc(front_ready, 1)
                b = turn(12)
                pe.wait_ge(da_ready, s + 1)
                for n, name in enumerate(("gt", "le", "ones", "lt", "ge")):
                    last = nc.tensor.matmul(b[:, NT * NH * n:NT * NH * (n + 1)], k[name][:],
                                            da[u][:].rearrange("p j h -> p (j h)"), start=True, stop=True)
                last.then_inc(front_ready, 1)

            front(0, 0)

            def step(s, u, last_slab):
                x = act_x[u]
                pe.wait_ge(front_used, FRONT * (s + 1) + 1)
                pe.wait_ge(yt_used, NT * s + 1)
                pe.wait_ge(y_used, C * s + 1)
                pe.wait_ge(st_used, (C - 2) * s + 1)
                for c in range(C):
                    d, j = chunk(c)
                    tile = slice(P * j, P * (j + 1))
                    if c >= 2:
                        pe.wait_ge(xdt_ready, C * s + c + 1)
                        pe.wait_ge(bt_ready, C * s + c - 1)
                    for n in range(3):
                        last = nc.tensor.transpose(bank[2 + c % 2][:, P * n:P * (n + 1)], x[:, d, n, tile], k["ident"][:])
                    last.then_inc(tpx_ready, 1)
                    if c >= 2:
                        pe.wait_ge(cb_ready, C * s + c + 1)
                    nc.tensor.matmul(bank[4 + 2 * (c % 2)][:, 0:P], x[:, d, 2, tile], x[:, d, 3, tile],
                                     start=True, stop=True).then_inc(g_ready, 1)
                    if c >= 2:
                        pe.wait_ge(decay_ready, C * s + c + 1)
                    pe.wait_ge(seg_in_ready, C * s + c + 1)
                    nc.tensor.matmul(bank[5 + 2 * (c % 2)][:], k[SUMS[d][0]][:],
                                     seg_in[c % 2][:].rearrange("p h l -> p (h l)"),
                                     start=True, stop=True).then_inc(seg_in_used, 1)
                if not last_slab:
                    front(s + 1, 1 - u)
                pe.wait_ge(mixer_ready, C * s + C + 2)
                pe.wait_ge(bt_ready, C * s + C)
                for c in range(C):
                    d, j = chunk(c)
                    tile = slice(P * j, P * (j + 1))
                    b = bank[4 + 2 * d]
                    if c >= 2:
                        pe.wait_ge(y_used, C * s + c)
                    for g in range(HB):
                        nc.tensor.matmul(b[:, P * g:P * (g + 1)], x[:, d, g, tile], k["skip"][:, g, :],
                                         start=(g == 0), stop=False, skip_group_check=True)
                    for n in range(NH):
                        last = nc.tensor.matmul(b[:, HD * n:HD * (n + 1)], mixer[:, c, n, :],
                                                xdt[:, c, HD * n:HD * (n + 1)], start=False, stop=(n == NH - 1),
                                                skip_group_check=True)
                    if c >= 2:
                        pe.wait_ge(st_used, (C - 2) * s + c)
                        last = nc.tensor.matmul(b[:, DI:2 * DI], x[:, d, 3, tile], state[d][:], start=False, stop=True,
                                                skip_group_check=True)
                    last.then_inc(y_ready, 1)
                    if c < C - 2:
                        pe.wait_ge(xdd_ready, C * s + c + 1)
                        nc.tensor.matmul(bank[5 + 2 * d][:, 0:DI], b_t[:, c, :], xdd[:, c, :],
                                         start=True, stop=True).then_inc(st_ready, 1)

                def output(j):
                    pe.wait_ge(yt_used, NT * s + j + 2)
                    for n in range(4):
                        last = nc.tensor.matmul(bank[1][:, D * j:D * (j + 1)], yt[j % 2][:, n, :],
                                                k["fuse_w"][:, n % HB, n // HB, :], start=(n == 0), stop=(n == 3))
                    last.then_inc(out_ready, 1)

                for j in range(NT):
                    if j >= 2:
                        pe.wait_ge(yt_used, NT * s + j)
                    pe.wait_ge(yn_ready, C * s + C)
                    for n in range(4):
                        d, g = n // HB, n % HB
                        c = 2 * j if d == 0 else 2 * (NT - 1 - j) + 1
                        last = nc.tensor.transpose(bank[2 + j % 2][:, P * n:P * (n + 1)], yn[:, c, P * g:P * (g + 1)],
                                                   k["ident"][:])
                    last.then_inc(yt_ready, 1)
                    if j >= 1:
                        output(j - 1)
                output(NT - 1)

            slabs(pe, step)

        @block.scalar
        def _(act):
            act.sem_inc(front_used, 1)
            act.sem_inc(decay_ready, 2)
            act.sem_inc(yt_used, 1)

            def front(s, u):
                def take(n):
                    act.wait_ge(front_ready, FRONT * s + n + 1)
                    return bank[n % 2]

                b = take(0)
                nc.scalar.activation(f["xf"][u][:, PAD:PAD + T], b[:], ACT.Copy).then_inc(front_used, 1)
                b = take(1)
                nc.scalar.activation(dt_raw[:].rearrange("p j h -> p (j h)"), b[:, 0:NT * NH], ACT.Copy).then_inc(front_used, 1)
                nc.scalar.preload_act_table_set("natural_log_exp_and_others")
                act.wait_ge(dtx_ready, s + 1)
                nc.scalar.activation(dt_e[:], dt_n[:], ACT.Exp).then_inc(sp_step, 1)
                act.wait_ge(sp_step, s + 1)
                nc.scalar.activation(dt_l[:], dt_e[:], ACT.Ln, bias=1.0).then_inc(sp_ready, 1)
                for n in range(2 * CB):
                    b = take(2 + n)
                    nc.scalar.activation(act_x[u][:, n // CB, n % CB, :], b[:], ACT.Silu,
                                         bias=k["conv_b"][:, n % CB:n % CB + 1]).then_inc(front_used, 1)
                for n in range(2):
                    b = take(10 + n)
                    nc.scalar.activation(zs[u][:, 2 * n:2 * n + 2, :].rearrange("p j c -> p (j c)"), b[:],
                                         ACT.Silu).then_inc(front_used, 1)
                nc.scalar.preload_act_table_set("natural_log_exp_and_others")
                b = take(12)
                nc.scalar.activation(dec[u][:].rearrange("p n j h -> p (n j h)"), b[:, 0:5 * NT * NH],
                                     ACT.Exp).then_inc(front_used, 1)

            front(0, 0)

            def step(s, u, last_slab):
                for c in range(C):
                    act.wait_ge(xdt_ready, C * s + c + 3)
                    nc.scalar.activation(b_t[:, c, :], bank[2 + c % 2][:, DI:DI + P], ACT.Copy).then_inc(bt_ready, 1)
                    act.wait_ge(seg_in_used, C * s + c + 3)
                    act.wait_ge(mixer_ready, C * s + c + 1)
                    nc.scalar.activation(decay[c % 2][:].rearrange("p h l -> p (h l)"), bank[5 + 2 * (c % 2)][:],
                                         ACT.Exp).then_inc(decay_ready, 1)
                if not last_slab:
                    front(s + 1, 1 - u)
                for c in range(C):
                    act.wait_ge(y2_ready, C * s + c + 1)
                    nc.scalar.activation(yn[:, c, :], y[:, c, :], ACT.Square, accum_out=ss[:, c:c + 1]).then_inc(ss_ready, 1)
                for j in range(NT):
                    act.wait_ge(yt_ready, NT * s + j + 1)
                    act.wait_ge(out_ready, NT * s + j + 1)
                    nc.scalar.activation(yt[j % 2][:].rearrange("p n t -> p (n t)"), bank[2 + j % 2][:],
                                         ACT.Copy).then_inc(yt_used, 1)

            slabs(act, step)


def mixture(nc, k, n, width):
    with ExitStack() as ctx:
        sb, pb, sem = parts(nc, ctx, f"m{n}_")
        G = width // P
        HP = E * G
        f = front_tensors(sb)
        hid = [sb(f"hid{e}", [P, G, T]) for e in range(2)]
        rt = {name: sb("rt_" + name, [P, NT, E]) for name in
              ("logit", "shift", "ex", "eq", "rk", "one", "rest", "eq2", "rk2", "two", "g1", "g2", "gate")}
        rs = {name: sb("rs_" + name, [P, NT]) for name in
              ("mx", "sum", "mr", "w1", "mx2", "mr2", "d", "ed", "den", "w2")}
        gate_t = sb("gate_t", [NT * E, P])
        bank = [pb(f"bank{i}") for i in range(8)]
        var_ready, var_eps, rstd_ready = sem("var"), sem("eps"), sem("rstd")
        xn_ready, xt_ready, xf_ready = sem("xn"), sem("xt"), sem("xf")
        logit_ready, shift_ready, ex_ready, gate_ready = sem("logit"), sem("shift"), sem("ex"), sem("gate")
        gt_ready, gts_ready, bias_ready, bias_used = sem("gt"), sem("gts"), sem("bias"), sem("bias_used")
        hid_ready, hid_used, y_ready, y_used = sem("hid"), sem("hid_used"), sem("y"), sem("y_used")
        dve_step = sem("dve")
        func = ACT.Gelu if n == 0 else ACT.Relu
        w1, b1, w2, b2 = k[f"w1_{n}"], k[f"b1_{n}"], k[f"w2_{n}"], k[f"b2_{n}"]
        h = k["h"]

        block = ctx.enter_context(nc.Block())

        def over_e(t):
            return t[:].unsqueeze(2).broadcast_to([P, NT, E])

        def over_j(t):
            return t[:].unsqueeze(1).broadcast_to([P, NT, E])

        PER_SLAB = 2 * NT + (9 if n == 0 else 18) + 1 + NT * E

        @block.vector
        def _(dve):
            dve.sem_inc(bias_used, 1)
            dve.sem_inc(y_used, 2)
            st = Steps(dve, dve_step, PER_SLAB, ahead=2 * NT)
            st.n, st.base = 0, 0
            normalise(nc, k, st, f, 0, 0, var_ready, rstd_ready, xn_ready)

            def do(ins):
                st.need(st.mark(ins))

            def top(eq, rk, mr, one, logit, mx):
                do(nc.vector.tensor_tensor(rt[eq][:], rt[logit][:], over_e(rs[mx]), ALU.is_equal))
                do(nc.vector.tensor_tensor(rt[rk][:], rt[eq][:], over_j(k["rank"]), ALU.mult))
                do(nc.vector.tensor_reduce(rs[mr][:], rt[rk][:], AX, ALU.max))
                do(nc.vector.tensor_tensor(rt[one][:], rt[rk][:], over_e(rs[mr]), ALU.is_equal))

            def step(s, u, last_slab):
                st.slab(s)
                if not last_slab:
                    normalise(nc, k, st, f, s + 1, 1 - u, var_ready, rstd_ready, xn_ready)
                dve.wait_ge(logit_ready, s + 1)
                do(nc.vector.tensor_tensor(rt["logit"][:], bank[1][:, 0:NT * E].rearrange("p (j e) -> p j e", e=E),
                                           over_j(k[f"r_b{n}"]), ALU.add))
                do(nc.vector.tensor_reduce(rs["mx"][:], rt["logit"][:], AX, ALU.max))
                if n == 0:
                    nc.vector.tensor_tensor(rt["shift"][:], rt["logit"][:], over_e(rs["mx"]),
                                            ALU.subtract).then_inc(shift_ready, 1)
                    top("eq", "rk", "mr", "one", "logit", "mx")
                    dve.wait_ge(ex_ready, s + 1)
                    do(nc.vector.tensor_reduce(rs["sum"][:], rt["ex"][:], AX, ALU.add))
                    do(nc.vector.reciprocal(rs["w1"][:], rs["sum"][:]))
                    m = st.mark(nc.vector.tensor_tensor(rt["gate"][:], rt["one"][:], over_e(rs["w1"]), ALU.mult))
                    st.need(m)
                    dve.sem_inc(gate_ready, 1)
                    extra = 2
                else:
                    top("eq", "rk", "mr", "one", "logit", "mx")
                    do(nc.vector.scalar_tensor_tensor(rt["rest"][:], rt["one"][:], -3.0e38, rt["logit"][:],
                                                      ALU.mult, ALU.add))
                    do(nc.vector.tensor_reduce(rs["mx2"][:], rt["rest"][:], AX, ALU.max))
                    nc.vector.tensor_tensor(rs["d"][:], rs["mx2"][:], rs["mx"][:], ALU.subtract).then_inc(shift_ready, 1)
                    top("eq2", "rk2", "mr2", "two", "rest", "mx2")
                    dve.wait_ge(ex_ready, s + 1)
                    do(nc.vector.tensor_scalar(rs["den"][:], rs["ed"][:], 1.0, None, ALU.add))
                    do(nc.vector.reciprocal(rs["w1"][:], rs["den"][:]))
                    do(nc.vector.tensor_tensor(rs["w2"][:], rs["ed"][:], rs["w1"][:], ALU.mult))
                    do(nc.vector.tensor_tensor(rt["g1"][:], rt["one"][:], over_e(rs["w1"]), ALU.mult))
                    do(nc.vector.tensor_tensor(rt["g2"][:], rt["two"][:], over_e(rs["w2"]), ALU.mult))
                    m = st.mark(nc.vector.tensor_tensor(rt["gate"][:], rt["g1"][:], rt["g2"][:], ALU.add))
                    st.need(m)
                    dve.sem_inc(gate_ready, 1)
                    extra = 2
                dve.wait_ge(gt_ready, s + 1)
                nc.vector.tensor_copy(gate_t[:], bank[1][0:NT * E, 0:P]).then_inc(gts_ready, 1)
                dve.wait_ge(bias_ready, s + 1)
                hs = h[:, bass.ds(NT * s, NT), :]
                before = st.mark(nc.vector.tensor_tensor(hs, bank[1][:].rearrange("p (j d) -> p j d", d=D), hs, ALU.add))
                st.need(before)
                dve.sem_inc(bias_used, 1)
                done = [before] * NT
                for e in range(E):
                    dve.wait_ge(y_ready, E * s + e + 3)
                    for j in range(NT):
                        tile = h[:, bass.ds(NT * s + j, 1), :].rearrange("p a d -> p (a d)")
                        st.need(done[j])
                        done[j] = st.mark(nc.vector.scalar_tensor_tensor(
                            tile, bank[6 + e % 2][:, D * j:D * (j + 1)], rt["gate"][:, j, e:e + 1], tile,
                            ALU.mult, ALU.add))
                    st.need(done[NT - 1])
                    dve.sem_inc(y_used, 1)
                if not last_slab:
                    st.end()

            slabs(dve, step)

        @block.gpsimd
        def _(pool):
            rstd_steps(nc, pool, f, k, var_ready, var_eps, rstd_ready, 1)

            def step(s, u, last_slab):
                if not last_slab:
                    rstd_steps(nc, pool, f, k, var_ready, var_eps, rstd_ready, s + 2)
                if n == 0:
                    pool.wait_ge(shift_ready, s + 1)
                    nc.gpsimd.tensor_tensor(rt["ex"][:].rearrange("p j e -> p (j e)"), k["euler"][:],
                                            rt["shift"][:].rearrange("p j e -> p (j e)"),
                                            ALU.pow).then_inc(ex_ready, 1)

            slabs(pool, step)

        @block.tensor
        def _(pe):
            def transposes(s, u):
                pe.wait_ge(xn_ready, s + 1)
                pe.wait_ge(xf_ready, s + 1)
                for j in range(NT):
                    last = nc.tensor.transpose(bank[0][:, P * j:P * (j + 1)], f["xn"][u][:, j, :], k["ident"][:])
                last.then_inc(xt_ready, 1)

            pe.sem_inc(y_ready, 2)
            pe.wait_ge(k[f"moe{n}_in"], 16 * EXPERT_LOADS)
            transposes(0, 0)

            def step(s, u, last_slab):
                x = f["xf"][u]
                pe.wait_ge(xf_ready, s + 2)
                pe.wait_ge(bias_used, s + 1)
                for j in range(NT):
                    last = nc.tensor.matmul(bank[1][:, E * j:E * (j + 1)], x[:, PAD + P * j:PAD + P * (j + 1)],
                                            k[f"r_w{n}"][:], start=True, stop=True)
                last.then_inc(logit_ready, 1)

                def hidden(e):
                    for g in range(G):
                        m = e * G + g
                        pe.wait_ge(hid_used, HP * s + m + 1)
                        nc.tensor.matmul(bank[2 + m % 4][:], w1[:, e, P * g:P * (g + 1)], x[:, PAD:PAD + T],
                                         start=True, stop=True).then_inc(hid_ready, 1)

                def output(e):
                    pe.wait_ge(hid_used, HP * s + 4 + G * (e + 1))
                    pe.wait_ge(y_used, E * s + e + 1)
                    for j in range(NT):
                        for g in range(G):
                            last = nc.tensor.matmul(bank[6 + e % 2][:, D * j:D * (j + 1)],
                                                    hid[e % 2][:, g, P * j:P * (j + 1)], w2[:, e, g, :],
                                                    start=(g == 0), stop=(g == G - 1))
                    last.then_inc(y_ready, 1)

                hidden(0)
                for e in range(E):
                    if e + 1 < E:
                        hidden(e + 1)
                    if e == 0:
                        pe.wait_ge(gate_ready, s + 1)
                        nc.tensor.transpose(bank[1][0:NT * E, 0:P], rt["gate"][:].rearrange("p j e -> p (j e)"),
                                            k["ident"][:]).then_inc(gt_ready, 1)
                    if e == 1:
                        pe.wait_ge(gts_ready, s + 1)
                        nc.tensor.matmul(bank[1][:], gate_t[:], b2[:].rearrange("r j d -> r (j d)"),
                                         start=True, stop=True).then_inc(bias_ready, 1)
                    output(e)
                    if e == 3 and not last_slab:
                        transposes(s + 1, 1 - u)

            slabs(pe, step)

        @block.scalar
        def _(act):
            def xf_copy(s, u):
                act.wait_ge(xt_ready, s + 1)
                nc.scalar.activation(f["xf"][u][:, PAD:PAD + T], bank[0][:], ACT.Copy).then_inc(xf_ready, 1)

            act.sem_inc(xf_ready, 1)
            act.sem_inc(hid_used, 4)
            xf_copy(0, 0)

            def step(s, u, last_slab):
                for e in range(E):
                    act.wait_ge(y_ready, E * s + e + 1)
                    for g in range(G):
                        m = e * G + g
                        act.wait_ge(hid_ready, HP * s + m + 1)
                        nc.scalar.activation(hid[e % 2][:, g, :], bank[2 + m % 4][:], func,
                                             bias=b1[:, e, g:g + 1]).then_inc(hid_used, 1)
                    if e == 0 and n == 1:
                        act.wait_ge(shift_ready, s + 1)
                        nc.scalar.activation(rs["ed"][:], rs["d"][:], ACT.Exp).then_inc(ex_ready, 1)
                    if e == 4 and not last_slab:
                        xf_copy(s + 1, 1 - u)

            slabs(act, step)


_INS = ['x', 'L0_tok_w', 'L0_attn_in_proj_w', 'L0_attn_conv_fwd_w', 'L0_attn_conv_fwd_b', 'L0_attn_proj_fwd_w',
        'L0_attn_proj_fwd_b', 'L0_attn_conv_bwd_w', 'L0_attn_conv_bwd_b', 'L0_attn_proj_bwd_w', 'L0_attn_proj_bwd_b',
        'L0_attn_diag_weight', 'L0_attn_gate_scale', 'L0_attn_out_proj_w', 'L0_attn_ln_g', 'L0_attn_ln_b',
        'L0_ffn_Ws', 'L0_ffn_bs', 'L0_ffn_W1', 'L0_ffn_b1', 'L0_ffn_W2', 'L0_ffn_b2', 'L1_attn_in_proj_w',
        'L1_attn_conv_w', 'L1_attn_conv_b', 'L1_attn_dt_bias', 'L1_attn_A_log', 'L1_attn_D_skip', 'L1_attn_norm_w',
        'L1_attn_ssm_out_w', 'L1_attn_fuse_w', 'L1_attn_fuse_b', 'L1_ffn_gate_w', 'L1_ffn_gate_b', 'L1_ffn_w1',
        'L1_ffn_b1', 'L1_ffn_w2', 'L1_ffn_b2']


def kernel(**inputs):
    import numpy as _np
    import concourse.bacc as _bacc
    from concourse import mybir as _mybir
    from concourse.bass_utils import run_bass_kernel_spmd as _run

    nc = _bacc.Bacc("TRN2", target_bir_lowering=False, num_devices=1)
    arrays, aps = {}, {}
    for name in _INS:
        a = _np.ascontiguousarray(inputs[name])
        arrays[f"in_{name}"] = a
        aps[name] = nc.dram_tensor(f"in_{name}", a.shape, _mybir.dt.from_np(a.dtype), kind="ExternalInput").ap()
    out = nc.dram_tensor("out", (NSEQ, T, D), _mybir.dt.float32, kind="ExternalOutput").ap()
    build(nc, aps, out)
    r = _run(nc, [arrays], core_ids=[0])
    return r.results[0]["out"]
```

```python
from contextlib import ExitStack

import numpy as np

import concourse.bass as bass
from concourse import mybir

F32 = mybir.dt.float32
I32 = mybir.dt.int32
ALU = mybir.AluOpType
ACT = mybir.ActivationFunctionType
AX = mybir.AxisListType.X

P = 128
D = 128
NSEQ = 8
T = 512
NT = T // P
VOCAB = 50257
EPS = 1e-5
DI = 256
HB = DI // P
TAPS = 7
PAD = TAPS
XW = PAD + T + PAD
E = 8
F0 = 512
F1 = 256
CH = 512
CB = CH // P
MT = 4
NH = 4
HD = 64
PAIRS = NSEQ // 2
EXPERT_LOADS = 5 + NT
GROUPS = 2
SORTED = (0, 1)
LAST_STAGE = "D"


def parts(nc, ctx, stage=""):
    def sb(name, shape, dt=F32):
        return ctx.enter_context(nc.sbuf_tensor(stage + name, shape, dt))

    def pb(name):
        return ctx.enter_context(nc.psum_tensor(stage + name, [P, 512], F32))

    def sem(name):
        return ctx.enter_context(nc.semaphore(stage + name))

    return sb, pb, sem


def slabs(eng, step):
    with eng.Fori(0, PAIRS - 1) as i:
        step(2 * i, 0, False)
        step(2 * i + 1, 1, False)
    step(NSEQ - 2, 0, False)
    step(NSEQ - 1, 1, True)


class Steps:

    def __init__(self, eng, sem, per, ahead=0):
        self.eng, self.sem, self.per, self.ahead = eng, sem, per, ahead
        self.n = 0
        self.base = 0

    def slab(self, s):
        self.n, self.base = 0, self.per * s + self.ahead

    def mark(self, ins):
        ins.then_inc(self.sem, 1)
        self.n += 1
        return self.n

    def need(self, n):
        self.eng.wait_ge(self.sem, self.base + n)

    def end(self):
        assert self.n == self.per, self.n


def expert_tensors(k, sb, n, f):
    k[f"r_w{n}"] = sb(f"r_w{n}", [P, E])
    k[f"r_b{n}"] = sb(f"r_b{n}", [P, E])
    k[f"w1_{n}"] = sb(f"w1_{n}", [P, E, f])
    k[f"b1_{n}"] = sb(f"b1_{n}", [P, E, f // P])
    k[f"w2_{n}"] = sb(f"w2_{n}", [P, E, f // P, D])
    if n in SORTED:
        k[f"b2_{n}"] = sb(f"b2_{n}", [P, E, D])
    else:
        k[f"b2_{n}"] = sb(f"b2_{n}", [NT * E, NT, D])


def expert_loads(w, k, n):
    router_w, router_b, w1, b1, w2, b2 = (w[name] for name in (
        ("L0_ffn_Ws", "L0_ffn_bs", "L0_ffn_W1", "L0_ffn_b1", "L0_ffn_W2", "L0_ffn_b2"),
        ("L1_ffn_gate_w", "L1_ffn_gate_b", "L1_ffn_w1", "L1_ffn_b1", "L1_ffn_w2", "L1_ffn_b2"))[n])
    loads = [(k[f"r_w{n}"][:], router_w), (k[f"r_b{n}"][:], router_b.partition_broadcast(P)),
             (k[f"w1_{n}"][:], w1.rearrange("e d f -> d e f")),
             (k[f"b1_{n}"][:], b1.rearrange("e (g p) -> p e g", p=P)),
             (k[f"w2_{n}"][:], w2.rearrange("e (g p) d -> p e g d", p=P))]
    for j in range(NT):
        loads.append((k[f"b2_{n}"][P // NT * j:P // NT * (j + 1)], b2.partition_broadcast(P // NT)) if n in SORTED
                     else (k[f"b2_{n}"][E * j:E * (j + 1), j, :], b2))
    assert len(loads) == EXPERT_LOADS
    return loads


def sorted_tiles(picks):
    return GROUPS * (picks * NSEQ * NT // GROUPS + E - 1)


def build(nc, w, out):
    rows_in = nc.dram_tensor("rows_in", (sorted_tiles(2) * P, D), F32, kind="Internal").ap()
    rows_out = nc.dram_tensor("rows_out", (sorted_tiles(2) * P, D), F32, kind="Internal").ap()
    with ExitStack() as ctx:
        sb, pb, sem = parts(nc, ctx)
        k = {}
        k["h"] = sb("h", [P, NSEQ * NT, D])
        k["ident"] = sb("ident", [P, P])
        k["ones"] = sb("ones", [P, P])
        for name in ("le", "lt", "ge", "gt"):
            k[name] = sb("mask_" + name, [P, P])
        k["mhalf"] = sb("minus_half", [P, 2 * NT])
        k["eps"] = sb("eps", [P, 2 * NT])
        k["held"] = sem("held")
        k["inv_di"] = sb("inv_di", [P, 2 * NT])
        k["euler"] = sb("euler", [P, NT * E])
        k["zeros"] = sb("zeros", [P, D])
        k["rank"] = sb("rank", [P, E])
        k["z_w"] = sb("z_w", [P, DI])
        k["dt_w"] = sb("dt_w", [P, NH])
        k["conv_w"] = sb("conv_w", [P, CB, MT, P])
        k["conv_b"] = sb("conv_b", [P, CB])
        k["dt_b"] = sb("dt_b", [P, NH])
        k["a_neg"] = sb("a_neg", [P, NH])
        k["skip"] = sb("skip", [P, HB, P])
        k["fuse_w"] = sb("fuse_w", [P, HB, 2, D])
        k["fuse_b"] = sb("fuse_b", [P, D])
        k["moe0_in"] = sem("moe0_in")
        k["moe1_in"] = sem("moe1_in")
        k["stored"] = sem("stored")
        k["blank"] = sem("blank")
        with ExitStack() as half:
            sb0, _, _ = parts(nc, half)
            k["xz_w"] = sb0("xz_w", [P, 2 * DI])
            k["tap_w"] = sb0("tap_w", [P, 2 * TAPS, DI])
            k["tap_b"] = sb0("tap_b", [P, 2 * HB])
            k["diag"] = sb0("diag", [P, HB])
            k["out_w"] = sb0("out_w", [P, HB, D])
            k["ln_g"] = sb0("ln_g", [P, D])
            k["ln_b"] = sb0("ln_b", [P, D])
            expert_tensors(k, sb0, 0, F0)
            setup(nc, w, k, rows_in)
            attention0(nc, k)
            sorted_mixture(nc, k, 0, F0, 1, rows_in, rows_out)
        with ExitStack() as half:
            sb1, _, _ = parts(nc, half)
            expert_tensors(k, sb1, 1, F1)
            attention1(nc, k, expert_loads(w, k, 1))
            if LAST_STAGE >= "D":
                sorted_mixture(nc, k, 1, F1, 2, rows_in, rows_out)
        with nc.Block() as block:
            @block.sync
            def _(sp):
                sp.wait_ge(k["moe1_in"], 16 * EXPERT_LOADS)
                for s in range(NSEQ):
                    sp.dma_start(out[s].rearrange("(j p) d -> p j d", p=P),
                                 k["h"][:, NT * s:NT * (s + 1), :]).then_inc(k["stored"], 16)
                sp.wait_ge(k["stored"], 16 * NSEQ)


def setup(nc, w, k, rows_in):
    with ExitStack() as ctx:
        sb, pb, sem = parts(nc, ctx)
        ids = sb("ids", [P, NSEQ * NT], I32)
        xz_nat = sb("xz_nat", [P, 4, D])
        proj_nat = sb("proj_nat", [P, 2, HB, DI])
        tap = sb("tap", [P, 2, HB, TAPS])
        conv_bias = sb("conv_bias", [P, 2, HB])
        proj_bias = sb("proj_bias", [P, 2 * HB])
        gate_scale = sb("gate_scale", [P, 1])
        out_nat = sb("out_nat", [P, DI])
        proj_t = sb("proj_t", [P, 2, HB, DI])
        scaled = sb("scaled", [P, 2 * TAPS, HB, DI])
        in_nat = sb("in_nat", [P, 6, D])
        dt_nat = sb("dt_nat", [NH, D])
        mtap = sb("mtap", [P, CB, MT])
        in_scaled = sb("in_scaled", [P, CB, MT, D])
        a_log = sb("a_log", [P, NH])
        a_exp = sb("a_exp", [P, NH])
        skip_col = sb("skip_col", [P, HB])
        norm_col = sb("norm_col", [P, HB])
        ssm_nat = sb("ssm_nat", [P, DI])
        fuse_nat = sb("fuse_nat", [P, 2, D])
        fuse_t = sb("fuse_t", [P, 2, D])
        bank = [pb(f"setup_bank{i}") for i in range(8)]
        ids_in, weights_in, gathered = sem("ids_in"), sem("weights_in"), sem("gathered")
        consts, b2_zero = sem("consts"), sem("b2_zero")
        group_ready, group_used = sem("group_ready"), sem("group_used")
        scaled_ready, exp_ready = sem("scaled_ready"), sem("exp_ready")

        def row(a):
            return a.partition_broadcast(P)

        def cols(a, n):
            return a.rearrange("(b p) -> p b", p=P)

        early = [
            (xz_nat[:], w["L0_attn_in_proj_w"].rearrange("(g p) d -> p g d", p=P)),
            (proj_nat[:, 0], w["L0_attn_proj_fwd_w"].rearrange("(g p) c -> p g c", p=P)),
            (proj_nat[:, 1], w["L0_attn_proj_bwd_w"].rearrange("(g p) c -> p g c", p=P)),
            (tap[:, 0], w["L0_attn_conv_fwd_w"].rearrange("(g p) o k -> p g (o k)", p=P)),
            (tap[:, 1], w["L0_attn_conv_bwd_w"].rearrange("(g p) o k -> p g (o k)", p=P)),
            (out_nat[:], w["L0_attn_out_proj_w"]),
            (in_nat[:], w["L1_attn_in_proj_w"][0:6 * P].rearrange("(g p) d -> p g d", p=P)),
            (dt_nat[:], w["L1_attn_in_proj_w"][6 * P:6 * P + NH]),
            (mtap[:], w["L1_attn_conv_w"].rearrange("(g p) o k -> p g (o k)", p=P)),
            (ssm_nat[:], w["L1_attn_ssm_out_w"]),
            (fuse_nat[:], w["L1_attn_fuse_w"].rearrange("o (g m) -> o g m", g=2)),
        ]
        small = [
            (gate_scale[:], row(w["L0_attn_gate_scale"])),
            (k["ln_g"][:], row(w["L0_attn_ln_g"])), (k["ln_b"][:], row(w["L0_attn_ln_b"])),
            (k["dt_b"][:], row(w["L1_attn_dt_bias"])), (a_log[:], row(w["L1_attn_A_log"])),
            (k["fuse_b"][:], row(w["L1_attn_fuse_b"])),
        ]
        for d, n in enumerate(("fwd", "bwd")):
            for g in range(HB):
                small.append((conv_bias[:, d, g:g + 1], w[f"L0_attn_conv_{n}_b"][g * P:(g + 1) * P].unsqueeze(1)))
                small.append((proj_bias[:, HB * d + g:HB * d + g + 1],
                              w[f"L0_attn_proj_{n}_b"][g * P:(g + 1) * P].unsqueeze(1)))
        for g in range(HB):
            small.append((k["diag"][:, g:g + 1], w["L0_attn_diag_weight"][g * P:(g + 1) * P].unsqueeze(1)))
            small.append((norm_col[:, g:g + 1], w["L1_attn_norm_w"][g * P:(g + 1) * P].unsqueeze(1)))
            for j in range(2):
                small.append((skip_col[HD * j:HD * (j + 1), g:g + 1],
                              w["L1_attn_D_skip"][2 * g + j:2 * g + j + 1].partition_broadcast(HD)))
        for g in range(CB):
            small.append((k["conv_b"][:, g:g + 1], w["L1_attn_conv_b"][g * P:(g + 1) * P].unsqueeze(1)))
        n_weights = len(early) + len(small)

        block = ctx.enter_context(nc.Block())

        @block.sync
        def _(sp):
            with nc.allow_non_contiguous_dma("bias columns"):
                sp.dma_start(ids[:], w["x"].rearrange("s (j p) -> p (s j)", p=P)).then_inc(ids_in, 16)
                for dst, src in early + small:
                    sp.dma_start(dst, src).then_inc(weights_in, 16)
                sp.wait_ge(b2_zero, 1)
                n_rows = sorted_tiles(2)
                sp.dma_start(rows_in.rearrange("(p n) d -> p n d", n=n_rows),
                             k["zeros"][:].unsqueeze(1).broadcast_to([P, n_rows, D])).then_inc(k["blank"], 16)
                for dst, src in expert_loads(w, k, 0):
                    sp.dma_start(dst, src).then_inc(k["moe0_in"], 16)

        @block.gpsimd
        def _(pool):
            nc.gpsimd.memset(k["zeros"][:], 0.0).then_inc(b2_zero, 1)
            for name in ("ident", "ones", "le", "lt", "ge", "gt"):
                nc.gpsimd.memset(k[name][:], 0.0 if name == "ident" else 1.0).then_inc(consts, 1)
            nc.gpsimd.memset(k["mhalf"][:], -0.5).then_inc(consts, 1)
            nc.gpsimd.memset(k["eps"][:], EPS).then_inc(consts, 1)
            nc.gpsimd.memset(k["euler"][:], float(np.e)).then_inc(consts, 1)
            nc.gpsimd.memset(k["inv_di"][:], 1.0 / DI).then_inc(consts, 1)
            for e in range(E):
                nc.gpsimd.memset(k["rank"][:, e:e + 1], float(E - e)).then_inc(consts, 1)
            pool.wait_ge(consts, 10 + E)
            for name, cmp, cm, step, fill in (("ident", ALU.not_equal, 1, -1, 1.0), ("le", ALU.is_ge, -1, 1, 0.0),
                                              ("lt", ALU.is_gt, -1, 1, 0.0), ("ge", ALU.is_ge, 1, -1, 0.0),
                                              ("gt", ALU.is_gt, 1, -1, 0.0)):
                nc.gpsimd.affine_select(out=k[name][:], in_=k[name][:], compare_op=cmp, fill=fill, base=0,
                                        pattern=[[step, P]], channel_multiplier=cm).then_inc(consts, 1)
            pool.wait_ge(ids_in, 16)
            for n in range(NSEQ * NT):
                pool.indirect_dma_start(out=k["h"][:, n, :], out_offset=None, in_=w["L0_tok_w"],
                                        in_offset=bass.IndirectOffsetOnAxis(ap=ids[:, n:n + 1], axis=0),
                                        ).then_inc(gathered, 16)
            pool.wait_ge(gathered, 16 * NSEQ * NT)

        n_consts = 10 + E + 5

        @block.tensor
        def _(pe):
            pe.wait_ge(consts, n_consts)
            pe.wait_ge(weights_in, 16 * n_weights)
            g = [0]

            def group(work):
                if g[0] >= 8:
                    pe.wait_ge(group_used, g[0] - 7)
                last = work(bank[g[0] % 8])
                last.then_inc(group_ready, 1)
                g[0] += 1

            def transposes(sources):
                def work(b):
                    for n, src in enumerate(sources):
                        rows = src.shape[0]
                        last = nc.tensor.transpose(b[:, P * n:P * n + rows], src, k["ident"][0:rows, 0:rows])
                    return last
                return work

            group(transposes([xz_nat[:, n, :] for n in range(4)]))
            for d in range(2):
                group(transposes([proj_nat[:, d, o, P * c:P * (c + 1)] for c in range(HB) for o in range(HB)]))
            group(transposes([out_nat[:, 0:P], out_nat[:, P:DI], fuse_nat[:, 0, :], fuse_nat[:, 1, :]]))
            group(transposes([in_nat[:, 0, :], in_nat[:, 1, :], dt_nat[:, :]]))
            pe.wait_ge(scaled_ready, 1)
            for b in range(CB):
                group(transposes([in_scaled[:, b, t, :] for t in range(MT)]))
            pe.wait_ge(scaled_ready, 2)

            def tap_products(q):
                def work(b):
                    for m in (2 * q, 2 * q + 1):
                        for c in range(HB):
                            last = nc.tensor.matmul(b[:, DI * (m % 2):DI * (m % 2 + 1)], xz_nat[:, c, :],
                                                    scaled[:, m, c, :], start=(c == 0), stop=(c == HB - 1))
                    return last
                return work

            for q in range(TAPS):
                group(tap_products(q))

            def bias_products(b):
                for d in range(2):
                    for o in range(HB):
                        for c in range(HB):
                            last = nc.tensor.matmul(b[:, HB * d + o:HB * d + o + 1],
                                                    proj_t[:, d, c, P * o:P * (o + 1)], conv_bias[:, d, c:c + 1],
                                                    start=(c == 0), stop=(c == HB - 1))
                return last

            group(bias_products)
            pe.wait_ge(group_used, 4)

            def fuse_products(b):
                for c in range(HB):
                    last = nc.tensor.matmul(b[:, 2 * D * c:2 * D * (c + 1)], ssm_nat[:, P * c:P * (c + 1)],
                                            fuse_t[:, :, :].rearrange("m g o -> m (g o)"), start=True, stop=True)
                return last

            group(fuse_products)

        @block.scalar
        def _(act):
            act.wait_ge(weights_in, 16 * n_weights)
            nc.scalar.activation(a_exp[:], a_log[:], ACT.Exp).then_inc(exp_ready, 1)
            g = [0]

            def used(*copies):
                act.wait_ge(group_ready, g[0] + 1)
                for dst, lo, hi, scale in copies:
                    src = bank[g[0] % 8][:, lo:hi]
                    last = nc.scalar.activation(dst, src, ACT.Copy, scale=scale)
                last.then_inc(group_used, 1)
                g[0] += 1

            used((k["xz_w"][:], 0, 512, 1.0))
            for d in range(2):
                used((proj_t[:, d].rearrange("p c o -> p (c o)"), 0, 512, 1.0))
            used((k["out_w"][:].rearrange("p g d -> p (g d)"), 0, DI, gate_scale[:, 0:1]),
                 (fuse_t[:].rearrange("p g d -> p (g d)"), DI, 2 * DI, 1.0))
            used((k["z_w"][:], 0, DI, 1.0), (k["dt_w"][:], DI, DI + NH, 1.0))
            for b in range(CB):
                used((k["conv_w"][:, b].rearrange("p t d -> p (t d)"), 0, 512, 1.0))
            for q in range(TAPS):
                used((k["tap_w"][:, 2 * q:2 * q + 2].rearrange("p t d -> p (t d)"), 0, 512, 1.0))
            act.wait_ge(group_ready, g[0] + 1)
            for n in range(2 * HB):
                last = nc.scalar.activation(k["tap_b"][:, n:n + 1], bank[g[0] % 8][:, n:n + 1], ACT.Identity,
                                            bias=proj_bias[:, n:n + 1])
            last.then_inc(group_used, 1)
            g[0] += 1
            act.wait_ge(group_ready, g[0] + 1)
            for c in range(HB):
                last = nc.scalar.activation(k["fuse_w"][:, c].rearrange("p g d -> p (g d)"),
                                            bank[g[0] % 8][:, 2 * D * c:2 * D * (c + 1)], ACT.Copy,
                                            scale=norm_col[:, c:c + 1])
            last.then_inc(group_used, 1)

        @block.vector
        def _(dve):
            dve.wait_ge(weights_in, 16 * n_weights)
            for b in range(CB):
                for t in range(MT):
                    last = nc.vector.tensor_scalar(in_scaled[:, b, t, :], in_nat[:, 2 + b, :], mtap[:, b, t:t + 1],
                                                   None, ALU.mult)
            last.then_inc(scaled_ready, 1)
            dve.wait_ge(group_used, 3)
            for d in range(2):
                for t in range(TAPS):
                    for c in range(HB):
                        last = nc.vector.tensor_scalar(scaled[:, TAPS * d + t, c, :], proj_t[:, d, c, :],
                                                       tap[:, d, c, t:t + 1], None, ALU.mult)
            last.then_inc(scaled_ready, 1)
            dve.wait_ge(consts, n_consts)
            for c in range(HB):
                nc.vector.tensor_scalar(k["skip"][:, c, :], k["ident"][:], skip_col[:, c:c + 1], None, ALU.mult)
            dve.wait_ge(exp_ready, 1)
            nc.vector.tensor_scalar(k["a_neg"][:], a_exp[:], -1.0, None, ALU.mult)


def front_tensors(sb):
    return {
        "stats": sb("stats", [P, NT, 6]),
        "mv": sb("mv", [P, NT, 2]),
        "var": sb("var", [P, NT]),
        "rstd": sb("rstd", [P, NT]),
        "xn": [sb(f"xn{u}", [P, NT, D]) for u in range(2)],
        "xf": [sb(f"xf{u}", [P, XW]) for u in range(2)],
    }


def stat_steps(nc, k, st, f, src, var_ready):
    for j in range(NT):
        st.mark(nc.vector.bn_stats(f["stats"][:, j, :], src[:, j, :]))
    st.need(st.n)
    nc.vector.sem_inc(k["held"], 1)
    for j in range(NT):
        st.mark(nc.vector.bn_aggr(f["mv"][:, j, :], f["stats"][:, j, :]))
    st.need(st.n)
    nc.vector.tensor_copy(f["var"][:], f["mv"][:, :, 1]).then_inc(var_ready, 1)


def normalise(nc, k, st, f, s, u, var_ready, rstd_ready, xn_ready):
    stat_steps(nc, k, st, f, k["h"][:, bass.ds(NT * s, NT), :], var_ready)
    nc.vector.wait_ge(rstd_ready, s + 1)
    for j in range(NT):
        tile = k["h"][:, bass.ds(NT * s + j, 1), :].rearrange("p a d -> p (a d)")
        last = nc.vector.tensor_scalar(f["xn"][u][:, j, :], tile, f["mv"][:, j, 0:1], f["rstd"][:, j:j + 1],
                                       ALU.subtract, ALU.mult)
    last.then_inc(xn_ready, 1)


def rstd_steps(nc, pool, f, k, var_ready, var_eps, rstd_ready, n):
    pool.wait_ge(var_ready, n)
    nc.gpsimd.tensor_tensor(f["var"][:], f["var"][:], k["eps"][:, 0:NT], ALU.add).then_inc(var_eps, 1)
    pool.wait_ge(var_eps, n)
    nc.gpsimd.tensor_tensor(f["rstd"][:], f["var"][:], k["mhalf"][:, 0:NT], ALU.pow).then_inc(rstd_ready, 1)


def attention0(nc, k):
    with ExitStack() as ctx:
        sb, pb, sem = parts(nc, ctx, "a_")
        f = front_tensors(sb)
        f2 = {"stats": sb("stats2", [P, NT, 6]), "mv": sb("mv2", [P, NT, 2]), "var": sb("var2", [P, NT]),
              "rstd": sb("rstd2", [P, NT])}
        mix = sb("mix", [P, 4, T])
        gate = sb("gate", [P, HB, T])
        both = sb("both", [P, HB, T])
        both_d = sb("both_d", [P, HB, T])
        y = sb("y", [P, HB, T])
        res = sb("res", [P, NT, D])
        nrm = sb("nrm", [P, NT, D])
        nrm_g = sb("nrm_g", [P, NT, D])
        nrm_b = sb("nrm_b", [P, NT, D])
        bank = [pb(f"bank{i}") for i in range(8)]
        edges = sem("edges")
        var_ready, var_eps, rstd_ready = sem("var"), sem("eps"), sem("rstd")
        var2_ready, var2_eps, rstd2_ready = sem("var2"), sem("eps2"), sem("rstd2")
        xn_ready, xt_ready, xf_ready = sem("xn"), sem("xt"), sem("xf")
        conv_ready, silu_ready, xp_used = sem("conv"), sem("silu"), sem("xp_used")
        y_ready, out_ready, out_used = sem("y"), sem("out"), sem("out_used")
        dve_step = sem("dve")

        block = ctx.enter_context(nc.Block())
        h = k["h"]

        PER_SLAB = 2 * NT + 2 * HB + 1 + 2 * NT + NT + 2

        @block.vector
        def _(dve):
            dve.sem_inc(y_ready, 1)
            dve.sem_inc(out_used, 1)
            for u in range(2):
                nc.vector.memset(f["xf"][u][:, 0:PAD], 0.0).then_inc(edges, 1)
                nc.vector.memset(f["xf"][u][:, PAD + T:XW], 0.0).then_inc(edges, 1)
            nc.vector.memset(mix[:, 0:2, 0:1], 0.0).then_inc(edges, 1)
            nc.vector.memset(mix[:, 2:4, T - 1:T], 0.0).then_inc(edges, 1)
            dve.wait_ge(edges, 6)
            st = Steps(dve, dve_step, PER_SLAB, ahead=2 * NT)
            st.n, st.base = 0, 0
            normalise(nc, k, st, f, 0, 0, var_ready, rstd_ready, xn_ready)

            def step(s, u, last_slab):
                st.slab(s)
                if not last_slab:
                    normalise(nc, k, st, f, s + 1, 1 - u, var_ready, rstd_ready, xn_ready)
                for g in range(HB):
                    dve.wait_ge(silu_ready, 6 * s + 4 + g)
                    a = st.mark(nc.vector.tensor_tensor(both[:, g, :], mix[:, g, :], mix[:, 2 + g, :], ALU.add))
                    dve.wait_ge(conv_ready, 8 * s + 7 + g)
                    st.need(a)
                    b = st.mark(nc.vector.scalar_tensor_tensor(both_d[:, g, :], bank[4 + g][:], k["diag"][:, g:g + 1],
                                                               both[:, g, :], ALU.mult, ALU.add))
                    dve.wait_ge(silu_ready, 6 * s + 6 + g)
                    st.need(b)
                    nc.vector.tensor_tensor(y[:, g, :], both_d[:, g, :], gate[:, g, :], ALU.mult).then_inc(y_ready, 1)
                dve.wait_ge(out_ready, s + 1)
                r = st.mark(nc.vector.tensor_tensor(res[:].rearrange("p j d -> p (j d)"), bank[7][:],
                                                    f["xn"][u][:].rearrange("p j d -> p (j d)"), ALU.add))
                st.need(r)
                stat_steps(nc, k, st, f2, res, var2_ready)
                dve.wait_ge(rstd2_ready, s + 1)
                for j in range(NT):
                    n = st.mark(nc.vector.tensor_scalar(nrm[:, j, :], res[:, j, :], f2["mv"][:, j, 0:1],
                                                        f2["rstd"][:, j:j + 1], ALU.subtract, ALU.mult))
                st.need(n)
                n = st.mark(nc.vector.tensor_tensor(nrm_g[:], nrm[:],
                                                    k["ln_g"][:].unsqueeze(1).broadcast_to([P, NT, D]), ALU.mult))
                st.need(n)
                n = st.mark(nc.vector.tensor_tensor(nrm_b[:], nrm_g[:],
                                                    k["ln_b"][:].unsqueeze(1).broadcast_to([P, NT, D]), ALU.add))
                st.need(n)
                hs = h[:, bass.ds(NT * s, NT), :]
                nc.vector.tensor_tensor(hs, hs, nrm_b[:], ALU.add).then_inc(out_used, 1)
                if not last_slab:
                    st.end()

            slabs(dve, step)

        @block.gpsimd
        def _(pool):
            rstd_steps(nc, pool, f, k, var_ready, var_eps, rstd_ready, 1)

            def step(s, u, last_slab):
                if not last_slab:
                    rstd_steps(nc, pool, f, k, var_ready, var_eps, rstd_ready, s + 2)
                rstd_steps(nc, pool, f2, k, var2_ready, var2_eps, rstd2_ready, s + 1)

            slabs(pool, step)

        @block.tensor
        def _(pe):
            def transposes(s, u):
                pe.wait_ge(xn_ready, s + 1)
                pe.wait_ge(xf_ready, s + 1)
                for j in range(NT):
                    last = nc.tensor.transpose(bank[6][:, P * j:P * (j + 1)], f["xn"][u][:, j, :], k["ident"][:])
                last.then_inc(xt_ready, 1)

            pe.wait_ge(edges, 6)
            transposes(0, 0)

            def step(s, u, last_slab):
                x = f["xf"][u]
                pe.wait_ge(xf_ready, s + 2)
                pe.wait_ge(silu_ready, 6 * s + 1)
                for d in range(2):
                    for g in range(HB):
                        for t in range(TAPS):
                            at = t if d == 0 else 2 * PAD - t
                            last = nc.tensor.matmul(bank[2 * d + g][:], k["tap_w"][:, TAPS * d + t, P * g:P * (g + 1)],
                                                    x[:, at:at + T], start=(t == 0), stop=(t == TAPS - 1))
                        last.then_inc(conv_ready, 1)
                for g in range(HB):
                    pe.wait_ge(silu_ready, 6 * s + 2 + g)
                    nc.tensor.matmul(bank[g][:], k["xz_w"][:, DI + P * g:DI + P * (g + 1)], x[:, PAD:PAD + T],
                                     start=True, stop=True).then_inc(conv_ready, 1)
                pe.wait_ge(y_ready, 2 * s + 1)
                for g in range(HB):
                    nc.tensor.matmul(bank[4 + g][:], k["xz_w"][:, P * g:P * (g + 1)], x[:, PAD:PAD + T],
                                     start=True, stop=True).then_inc(conv_ready, 1)
                if not last_slab:
                    transposes(s + 1, 1 - u)
                pe.wait_ge(out_used, s + 1)
                pe.wait_ge(y_ready, 2 * s + 3)
                for j in range(NT):
                    for g in range(HB):
                        last = nc.tensor.matmul(bank[7][:, D * j:D * (j + 1)], y[:, g, P * j:P * (j + 1)],
                                                k["out_w"][:, g, :], start=(g == 0), stop=(g == HB - 1))
                last.then_inc(out_ready, 1)

            slabs(pe, step)

        @block.scalar
        def _(act):
            def xf_copy(s, u):
                act.wait_ge(xt_ready, s + 1)
                nc.scalar.activation(f["xf"][u][:, PAD:PAD + T], bank[6][:], ACT.Copy).then_inc(xf_ready, 1)

            act.sem_inc(xf_ready, 1)
            act.sem_inc(silu_ready, 1)
            xf_copy(0, 0)

            def step(s, u, last_slab):
                act.wait_ge(y_ready, 2 * s + 1)
                for d in range(2):
                    for g in range(HB):
                        lo, hi = (1, T) if d == 0 else (0, T - 1)
                        act.wait_ge(conv_ready, 8 * s + 2 * d + g + 1)
                        nc.scalar.activation(mix[:, 2 * d + g, lo:hi], bank[2 * d + g][:, lo:hi], ACT.Silu,
                                             bias=k["tap_b"][:, 2 * d + g:2 * d + g + 1]).then_inc(silu_ready, 1)
                for g in range(HB):
                    act.wait_ge(conv_ready, 8 * s + 5 + g)
                    nc.scalar.activation(gate[:, g, :], bank[g][:], ACT.Silu).then_inc(silu_ready, 1)
                if not last_slab:
                    xf_copy(s + 1, 1 - u)

            slabs(act, step)


def attention1(nc, k, loads):
    with ExitStack() as ctx:
        sb, pb, sem = parts(nc, ctx, "c_")
        C = 2 * NT
        f = front_tensors(sb)
        act_x = [sb(f"act_x{u}", [P, 2, CB, T]) for u in range(2)]
        zs = [sb(f"zs{u}", [P, NT, DI]) for u in range(2)]
        dt_raw = sb("dt_raw", [P, NT, NH])
        dt_x = sb("dt_x", [P, NT, NH])
        dt_n = sb("dt_n", [P, NT, NH])
        dt_e = sb("dt_e", [P, NT, NH])
        dt_l = sb("dt_l", [P, NT, NH])
        dt = [sb(f"dt{u}", [P, NT, NH]) for u in range(2)]
        da = [sb(f"da{u}", [P, NT, NH]) for u in range(2)]
        dec = [sb(f"dec{u}", [P, 5, NT, NH]) for u in range(2)]
        seg_in = [sb(f"seg_in{i}", [P, NH, P]) for i in range(2)]
        decay = [sb(f"decay{i}", [P, NH, P]) for i in range(2)]
        cb = [sb(f"cb{i}", [P, P]) for i in range(2)]
        mixer = sb("mixer", [P, C, NH, P])
        xdt = sb("xdt", [P, C, DI])
        xdd = sb("xdd", [P, C, DI])
        b_t = sb("b_t", [P, C, P])
        state = [sb(f"state{d}", [P, DI]) for d in range(2)]
        state_d = [sb(f"state_d{d}", [P, DI]) for d in range(2)]
        y_off = [sb(f"y_off{d}", [P, DI]) for d in range(2)]
        y_sum = [sb(f"y_sum{d}", [P, DI]) for d in range(2)]
        y = sb("y", [P, C, DI])
        ss = sb("ss", [P, C])
        ms = sb("ms", [P, C])
        mse = sb("mse", [P, C])
        rr = sb("rr", [P, C])
        yn = sb("yn", [P, C, DI])
        yt = [sb(f"yt{i}", [P, 4, P]) for i in range(2)]
        o = sb("o", [P, NT, D])
        bank = [pb(f"bank{i}") for i in range(8)]
        var_ready, var_eps, rstd_ready = sem("var"), sem("eps"), sem("rstd")
        xn_ready, edges, b2_zero = sem("xn"), sem("edges"), sem("b2_zero")
        front_ready, front_used = sem("front"), sem("front_used")
        dtx_ready, sp_step, sp_ready, da_ready = sem("dtx"), sem("sp_step"), sem("sp"), sem("da")
        tpx_ready, g_ready, seg_ready = sem("tpx"), sem("g"), sem("seg")
        seg_in_ready, seg_in_used = sem("seg_in"), sem("seg_in_used")
        xdt_ready, bt_ready, xdd_ready = sem("xdt"), sem("bt"), sem("xdd")
        cb_ready, decay_ready, mixer_ready = sem("cb"), sem("decay"), sem("mixer")
        y_ready, y_used, st_ready, st_used, y2_ready = sem("y"), sem("y_used"), sem("st"), sem("st_used"), sem("y2")
        ss_ready, ms_step, rr_ready, yn_ready = sem("ss"), sem("ms"), sem("rr"), sem("yn")
        yt_ready, yt_used, out_ready, out_used = sem("yt"), sem("yt_used"), sem("out"), sem("out_used")
        dve_step = sem("dve")
        h = k["h"]

        FRONT = 13

        def chunk(c):
            return c % 2, c // 2 if c % 2 == 0 else NT - 1 - c // 2

        SUMS = (("gt", "le"), ("lt", "ge"))
        INTO, OUT, TOTAL = (0, 3), (1, 4), 2

        block = ctx.enter_context(nc.Block())

        def heads(t):
            return t.rearrange("p (h d) -> p h d", h=NH)

        def per_head(t):
            return t.unsqueeze(2).broadcast_to([P, NH, HD])

        @block.sync
        def _(sp):
            with nc.allow_non_contiguous_dma("bias columns"):
                sp.wait_ge(b2_zero, 1)
                for dst, src in loads:
                    sp.dma_start(dst, src).then_inc(k["moe1_in"], 16)

        @block.vector
        def _(dve):
            nc.vector.memset(k["b2_1"][:], 0.0).then_inc(b2_zero, 1)
            dve.sem_inc(out_used, 1)
            dve.sem_inc(xdt_ready, 2)
            dve.sem_inc(cb_ready, 2)
            dve.sem_inc(mixer_ready, 2)
            dve.sem_inc(y_used, 1)
            dve.sem_inc(st_used, 1)
            for u in range(2):
                nc.vector.memset(f["xf"][u][:, 0:PAD], 0.0).then_inc(edges, 1)
                nc.vector.memset(f["xf"][u][:, PAD + T:XW], 0.0).then_inc(edges, 1)
            dve.wait_ge(edges, 4)
            AHEAD = 2 * NT + 2
            st = Steps(dve, dve_step, AHEAD + 2 * (C - 2) + (C - 4) + 1, ahead=AHEAD)

            def dt_steps(s, u):
                dve.wait_ge(front_used, FRONT * s + 3)
                n = st.mark(nc.vector.tensor_tensor(dt_x[:], dt_raw[:], k["dt_b"][:].unsqueeze(1).broadcast_to([P, NT, NH]), ALU.add))
                st.need(n)
                nc.vector.scalar_tensor_tensor(dt_n[:], dt_x[:], -1.0, dt_x[:], ALU.mult, ALU.min).then_inc(dtx_ready, 1)
                dve.wait_ge(sp_ready, s + 1)
                n = st.mark(nc.vector.scalar_tensor_tensor(dt[u][:], dt_x[:], 0.0, dt_l[:], ALU.max, ALU.add))
                st.need(n)
                nc.vector.tensor_tensor(da[u][:], dt[u][:], k["a_neg"][:].unsqueeze(1).broadcast_to([P, NT, NH]), ALU.mult).then_inc(da_ready, 1)

            st.n, st.base = 0, 0
            normalise(nc, k, st, f, 0, 0, var_ready, rstd_ready, xn_ready)
            dt_steps(0, 0)

            def step(s, u, last_slab):
                st.slab(s)
                if not last_slab:
                    normalise(nc, k, st, f, s + 1, 1 - u, var_ready, rstd_ready, xn_ready)
                for c in range(C):
                    d, j = chunk(c)
                    dve.wait_ge(tpx_ready, C * s + c + 1)
                    nc.vector.tensor_tensor(heads(xdt[:, c, :]), heads(bank[2 + c % 2][:, 0:DI]),
                                            per_head(dt[u][:, j, :]), ALU.mult).then_inc(xdt_ready, 1)
                    dve.wait_ge(g_ready, C * s + c + 1)
                    nc.vector.tensor_tensor(cb[c % 2][:], bank[4 + 2 * (c % 2)][:, 0:P],
                                            k[SUMS[d][1]][:], ALU.mult).then_inc(cb_ready, 1)
                    dve.wait_ge(decay_ready, C * s + c + 3)
                    dve.wait_ge(cb_ready, C * s + c + 3)
                    nc.vector.tensor_tensor(mixer[:, c], decay[c % 2][:],
                                            cb[c % 2][:].unsqueeze(1).broadcast_to([P, NH, P]), ALU.mult).then_inc(mixer_ready, 1)
                if not last_slab:
                    dt_steps(s + 1, 1 - u)
                for c in range(C):
                    d, j = chunk(c)
                    dve.wait_ge(y_ready, C * s + c + 1)
                    if c >= 2:
                        n = st.mark(nc.vector.tensor_tensor(heads(y_off[d][:]), heads(bank[4 + 2 * d][:, DI:2 * DI]),
                                                            per_head(dec[u][:, OUT[d], j, :]), ALU.mult))
                        st.need(n)
                        n = st.mark(nc.vector.tensor_tensor(y_sum[d][:], bank[4 + 2 * d][:, 0:DI], y_off[d][:], ALU.add))
                        st.need(n)
                        dve.sem_inc(y_used, 1)
                        nc.vector.tensor_tensor(y[:, c, :], y_sum[d][:], zs[u][:, j, :], ALU.mult).then_inc(y2_ready, 1)
                    else:
                        nc.vector.tensor_tensor(y[:, c, :], bank[4 + 2 * d][:, 0:DI], zs[u][:, j, :],
                                                ALU.mult).then_inc(y2_ready, 1)
                        dve.wait_ge(y2_ready, C * s + c + 1)
                        dve.sem_inc(y_used, 1)
                    if c < C - 2:
                        if c < 2:
                            dve.wait_ge(st_ready, (C - 2) * s + c + 1)
                            nc.vector.tensor_copy(state[d][:], bank[5 + 2 * d][:, 0:DI]).then_inc(st_used, 1)
                        else:
                            n = st.mark(nc.vector.tensor_tensor(heads(state_d[d][:]), heads(state[d][:]),
                                                                per_head(dec[u][:, TOTAL, j, :]), ALU.mult))
                            st.need(n)
                            dve.wait_ge(st_ready, (C - 2) * s + c + 1)
                            nc.vector.tensor_tensor(state[d][:], state_d[d][:], bank[5 + 2 * d][:, 0:DI],
                                                    ALU.add).then_inc(st_used, 1)
                dve.wait_ge(rr_ready, s + 1)
                for c in range(C):
                    nc.vector.tensor_scalar(yn[:, c, :], y[:, c, :], rr[:, c:c + 1], None, ALU.mult).then_inc(yn_ready, 1)
                dve.wait_ge(out_ready, NT * s + NT + 2)
                n = st.mark(nc.vector.tensor_tensor(o[:], bank[1][:].rearrange("p (j d) -> p j d", d=D),
                                                    k["fuse_b"][:].unsqueeze(1).broadcast_to([P, NT, D]), ALU.add))
                st.need(n)
                hs = h[:, bass.ds(NT * s, NT), :]
                nc.vector.tensor_tensor(hs, hs, o[:], ALU.add).then_inc(out_used, 1)
                if not last_slab:
                    st.end()

            slabs(dve, step)

        @block.gpsimd
        def _(pool):
            rstd_steps(nc, pool, f, k, var_ready, var_eps, rstd_ready, 1)

            def step(s, u, last_slab):
                if not last_slab:
                    rstd_steps(nc, pool, f, k, var_ready, var_eps, rstd_ready, s + 2)
                pool.wait_ge(da_ready, s + 1)
                for c in range(C):
                    d, j = chunk(c)
                    pool.wait_ge(seg_in_used, C * s + c + 1)
                    nc.gpsimd.tensor_tensor(seg_in[c % 2][:], k[SUMS[d][1]][:].unsqueeze(1).broadcast_to([P, NH, P]),
                                            da[u][:, j, :].unsqueeze(2).broadcast_to([P, NH, P]),
                                            ALU.mult).then_inc(seg_in_ready, 1)
                    if c == 0:
                        pool.wait_ge(front_used, FRONT * (s + 1) + 1)
                    if c >= 1:
                        into_state(s, u, c - 1)
                into_state(s, u, C - 1)
                pool.wait_ge(ss_ready, C * s + C)
                nc.gpsimd.tensor_tensor(ms[:], ss[:], k["inv_di"][:], ALU.mult).then_inc(ms_step, 1)
                pool.wait_ge(ms_step, 2 * s + 1)
                nc.gpsimd.tensor_tensor(mse[:], ms[:], k["eps"][:], ALU.add).then_inc(ms_step, 1)
                pool.wait_ge(ms_step, 2 * s + 2)
                nc.gpsimd.tensor_tensor(rr[:], mse[:], k["mhalf"][:], ALU.pow).then_inc(rr_ready, 1)

            def into_state(s, u, c):
                d, j = chunk(c)
                pool.wait_ge(xdt_ready, C * s + c + 3)
                nc.gpsimd.tensor_tensor(heads(xdd[:, c, :]), heads(xdt[:, c, :]), per_head(dec[u][:, INTO[d], j, :]),
                                        ALU.mult).then_inc(xdd_ready, 1)

            slabs(pool, step)

        @block.tensor
        def _(pe):
            pe.sem_inc(seg_in_used, 2)
            pe.sem_inc(out_ready, 2)
            pe.wait_ge(edges, 4)

            def front(s, u):
                x = f["xf"][u]

                def turn(n):
                    pe.wait_ge(front_used, FRONT * s + n)
                    return bank[n % 2]

                pe.wait_ge(xn_ready, s + 1)
                b = bank[0]
                pe.wait_ge(front_used, FRONT * s + 1)
                for j in range(NT):
                    last = nc.tensor.transpose(b[:, P * j:P * (j + 1)], f["xn"][u][:, j, :], k["ident"][:])
                last.then_inc(front_ready, 1)
                pe.wait_ge(front_used, FRONT * s + 2)
                for j in range(NT):
                    last = nc.tensor.matmul(bank[1][:, NH * j:NH * (j + 1)], x[:, PAD + P * j:PAD + P * (j + 1)],
                                            k["dt_w"][:], start=True, stop=True)
                last.then_inc(front_ready, 1)
                for n in range(2 * CB):
                    d, blk = n // CB, n % CB
                    b = turn(2 + n)
                    for t in range(MT):
                        at = PAD - (MT - 1) + t if d == 0 else PAD + (MT - 1) - t
                        last = nc.tensor.matmul(b[:], k["conv_w"][:, blk, t, :], x[:, at:at + T],
                                                start=(t == 0), stop=(t == MT - 1))
                    last.then_inc(front_ready, 1)
                for n in range(2):
                    b = turn(10 + n)
                    for j in (2 * n, 2 * n + 1):
                        last = nc.tensor.matmul(b[:, DI * (j % 2):DI * (j % 2 + 1)],
                                                x[:, PAD + P * j:PAD + P * (j + 1)], k["z_w"][:], start=True, stop=True)
                    last.then_inc(front_ready, 1)
                b = turn(12)
                pe.wait_ge(da_ready, s + 1)
                for n, name in enumerate(("gt", "le", "ones", "lt", "ge")):
                    last = nc.tensor.matmul(b[:, NT * NH * n:NT * NH * (n + 1)], k[name][:],
                                            da[u][:].rearrange("p j h -> p (j h)"), start=True, stop=True)
                last.then_inc(front_ready, 1)

            front(0, 0)

            def step(s, u, last_slab):
                x = act_x[u]
                pe.wait_ge(front_used, FRONT * (s + 1) + 1)
                pe.wait_ge(yt_used, NT * s + 1)
                pe.wait_ge(y_used, C * s + 1)
                pe.wait_ge(st_used, (C - 2) * s + 1)
                for c in range(C):
                    d, j = chunk(c)
                    tile = slice(P * j, P * (j + 1))
                    if c >= 2:
                        pe.wait_ge(xdt_ready, C * s + c + 1)
                        pe.wait_ge(bt_ready, C * s + c - 1)
                    for n in range(3):
                        last = nc.tensor.transpose(bank[2 + c % 2][:, P * n:P * (n + 1)], x[:, d, n, tile], k["ident"][:])
                    last.then_inc(tpx_ready, 1)
                    if c >= 2:
                        pe.wait_ge(cb_ready, C * s + c + 1)
                    nc.tensor.matmul(bank[4 + 2 * (c % 2)][:, 0:P], x[:, d, 2, tile], x[:, d, 3, tile],
                                     start=True, stop=True).then_inc(g_ready, 1)
                    if c >= 2:
                        pe.wait_ge(decay_ready, C * s + c + 1)
                    pe.wait_ge(seg_in_ready, C * s + c + 1)
                    nc.tensor.matmul(bank[5 + 2 * (c % 2)][:], k[SUMS[d][0]][:],
                                     seg_in[c % 2][:].rearrange("p h l -> p (h l)"),
                                     start=True, stop=True).then_inc(seg_in_used, 1)
                if not last_slab:
                    front(s + 1, 1 - u)
                pe.wait_ge(mixer_ready, C * s + C + 2)
                pe.wait_ge(bt_ready, C * s + C)
                for c in range(C):
                    d, j = chunk(c)
                    tile = slice(P * j, P * (j + 1))
                    b = bank[4 + 2 * d]
                    if c >= 2:
                        pe.wait_ge(y_used, C * s + c)
                    for g in range(HB):
                        nc.tensor.matmul(b[:, P * g:P * (g + 1)], x[:, d, g, tile], k["skip"][:, g, :],
                                         start=(g == 0), stop=False, skip_group_check=True)
                    for n in range(NH):
                        last = nc.tensor.matmul(b[:, HD * n:HD * (n + 1)], mixer[:, c, n, :],
                                                xdt[:, c, HD * n:HD * (n + 1)], start=False, stop=(n == NH - 1),
                                                skip_group_check=True)
                    if c >= 2:
                        pe.wait_ge(st_used, (C - 2) * s + c)
                        last = nc.tensor.matmul(b[:, DI:2 * DI], x[:, d, 3, tile], state[d][:], start=False, stop=True,
                                                skip_group_check=True)
                    last.then_inc(y_ready, 1)
                    if c < C - 2:
                        pe.wait_ge(xdd_ready, C * s + c + 1)
                        nc.tensor.matmul(bank[5 + 2 * d][:, 0:DI], b_t[:, c, :], xdd[:, c, :],
                                         start=True, stop=True).then_inc(st_ready, 1)

                def output(j):
                    pe.wait_ge(yt_used, NT * s + j + 2)
                    for n in range(4):
                        last = nc.tensor.matmul(bank[1][:, D * j:D * (j + 1)], yt[j % 2][:, n, :],
                                                k["fuse_w"][:, n % HB, n // HB, :], start=(n == 0), stop=(n == 3))
                    last.then_inc(out_ready, 1)

                for j in range(NT):
                    if j >= 2:
                        pe.wait_ge(yt_used, NT * s + j)
                    pe.wait_ge(yn_ready, C * s + C)
                    for n in range(4):
                        d, g = n // HB, n % HB
                        c = 2 * j if d == 0 else 2 * (NT - 1 - j) + 1
                        last = nc.tensor.transpose(bank[2 + j % 2][:, P * n:P * (n + 1)], yn[:, c, P * g:P * (g + 1)],
                                                   k["ident"][:])
                    last.then_inc(yt_ready, 1)
                    if j >= 1:
                        output(j - 1)
                output(NT - 1)

            slabs(pe, step)

        @block.scalar
        def _(act):
            act.sem_inc(front_used, 1)
            act.sem_inc(decay_ready, 2)
            act.sem_inc(yt_used, 1)

            def front(s, u):
                def take(n):
                    act.wait_ge(front_ready, FRONT * s + n + 1)
                    return bank[n % 2]

                b = take(0)
                nc.scalar.activation(f["xf"][u][:, PAD:PAD + T], b[:], ACT.Copy).then_inc(front_used, 1)
                b = take(1)
                nc.scalar.activation(dt_raw[:].rearrange("p j h -> p (j h)"), b[:, 0:NT * NH], ACT.Copy).then_inc(front_used, 1)
                nc.scalar.preload_act_table_set("natural_log_exp_and_others")
                act.wait_ge(dtx_ready, s + 1)
                nc.scalar.activation(dt_e[:], dt_n[:], ACT.Exp).then_inc(sp_step, 1)
                act.wait_ge(sp_step, s + 1)
                nc.scalar.activation(dt_l[:], dt_e[:], ACT.Ln, bias=1.0).then_inc(sp_ready, 1)
                for n in range(2 * CB):
                    b = take(2 + n)
                    nc.scalar.activation(act_x[u][:, n // CB, n % CB, :], b[:], ACT.Silu,
                                         bias=k["conv_b"][:, n % CB:n % CB + 1]).then_inc(front_used, 1)
                for n in range(2):
                    b = take(10 + n)
                    nc.scalar.activation(zs[u][:, 2 * n:2 * n + 2, :].rearrange("p j c -> p (j c)"), b[:],
                                         ACT.Silu).then_inc(front_used, 1)
                nc.scalar.preload_act_table_set("natural_log_exp_and_others")
                b = take(12)
                nc.scalar.activation(dec[u][:].rearrange("p n j h -> p (n j h)"), b[:, 0:5 * NT * NH],
                                     ACT.Exp).then_inc(front_used, 1)

            front(0, 0)

            def step(s, u, last_slab):
                for c in range(C):
                    act.wait_ge(xdt_ready, C * s + c + 3)
                    nc.scalar.activation(b_t[:, c, :], bank[2 + c % 2][:, DI:DI + P], ACT.Copy).then_inc(bt_ready, 1)
                    act.wait_ge(seg_in_used, C * s + c + 3)
                    act.wait_ge(mixer_ready, C * s + c + 1)
                    nc.scalar.activation(decay[c % 2][:].rearrange("p h l -> p (h l)"), bank[5 + 2 * (c % 2)][:],
                                         ACT.Exp).then_inc(decay_ready, 1)
                if not last_slab:
                    front(s + 1, 1 - u)
                for c in range(C):
                    act.wait_ge(y2_ready, C * s + c + 1)
                    nc.scalar.activation(yn[:, c, :], y[:, c, :], ACT.Square, accum_out=ss[:, c:c + 1]).then_inc(ss_ready, 1)
                for j in range(NT):
                    act.wait_ge(yt_ready, NT * s + j + 1)
                    act.wait_ge(out_ready, NT * s + j + 1)
                    nc.scalar.activation(yt[j % 2][:].rearrange("p n t -> p (n t)"), bank[2 + j % 2][:],
                                         ACT.Copy).then_inc(yt_used, 1)

            slabs(act, step)


def mixture(nc, k, n, width):
    with ExitStack() as ctx:
        sb, pb, sem = parts(nc, ctx, f"m{n}_")
        G = width // P
        HP = E * G
        f = front_tensors(sb)
        hid = [sb(f"hid{e}", [P, G, T]) for e in range(2)]
        rt = {name: sb("rt_" + name, [P, NT, E]) for name in
              ("logit", "shift", "ex", "eq", "rk", "one", "rest", "eq2", "rk2", "two", "g1", "g2", "gate")}
        rs = {name: sb("rs_" + name, [P, NT]) for name in
              ("mx", "sum", "mr", "w1", "mx2", "mr2", "d", "ed", "den", "w2")}
        gate_t = sb("gate_t", [NT * E, P])
        bank = [pb(f"bank{i}") for i in range(8)]
        var_ready, var_eps, rstd_ready = sem("var"), sem("eps"), sem("rstd")
        xn_ready, xt_ready, xf_ready = sem("xn"), sem("xt"), sem("xf")
        logit_ready, shift_ready, ex_ready, gate_ready = sem("logit"), sem("shift"), sem("ex"), sem("gate")
        gt_ready, gts_ready, bias_ready, bias_used = sem("gt"), sem("gts"), sem("bias"), sem("bias_used")
        hid_ready, hid_used, y_ready, y_used = sem("hid"), sem("hid_used"), sem("y"), sem("y_used")
        dve_step = sem("dve")
        func = ACT.Gelu if n == 0 else ACT.Relu
        w1, b1, w2, b2 = k[f"w1_{n}"], k[f"b1_{n}"], k[f"w2_{n}"], k[f"b2_{n}"]
        h = k["h"]

        block = ctx.enter_context(nc.Block())

        def over_e(t):
            return t[:].unsqueeze(2).broadcast_to([P, NT, E])

        def over_j(t):
            return t[:].unsqueeze(1).broadcast_to([P, NT, E])

        PER_SLAB = 2 * NT + (9 if n == 0 else 18) + 1 + NT * E

        @block.vector
        def _(dve):
            dve.sem_inc(bias_used, 1)
            dve.sem_inc(y_used, 2)
            st = Steps(dve, dve_step, PER_SLAB, ahead=2 * NT)
            st.n, st.base = 0, 0
            normalise(nc, k, st, f, 0, 0, var_ready, rstd_ready, xn_ready)

            def do(ins):
                st.need(st.mark(ins))

            def top(eq, rk, mr, one, logit, mx):
                do(nc.vector.tensor_tensor(rt[eq][:], rt[logit][:], over_e(rs[mx]), ALU.is_equal))
                do(nc.vector.tensor_tensor(rt[rk][:], rt[eq][:], over_j(k["rank"]), ALU.mult))
                do(nc.vector.tensor_reduce(rs[mr][:], rt[rk][:], AX, ALU.max))
                do(nc.vector.tensor_tensor(rt[one][:], rt[rk][:], over_e(rs[mr]), ALU.is_equal))

            def step(s, u, last_slab):
                st.slab(s)
                if not last_slab:
                    normalise(nc, k, st, f, s + 1, 1 - u, var_ready, rstd_ready, xn_ready)
                dve.wait_ge(logit_ready, s + 1)
                do(nc.vector.tensor_tensor(rt["logit"][:], bank[1][:, 0:NT * E].rearrange("p (j e) -> p j e", e=E),
                                           over_j(k[f"r_b{n}"]), ALU.add))
                do(nc.vector.tensor_reduce(rs["mx"][:], rt["logit"][:], AX, ALU.max))
                if n == 0:
                    nc.vector.tensor_tensor(rt["shift"][:], rt["logit"][:], over_e(rs["mx"]),
                                            ALU.subtract).then_inc(shift_ready, 1)
                    top("eq", "rk", "mr", "one", "logit", "mx")
                    dve.wait_ge(ex_ready, s + 1)
                    do(nc.vector.tensor_reduce(rs["sum"][:], rt["ex"][:], AX, ALU.add))
                    do(nc.vector.reciprocal(rs["w1"][:], rs["sum"][:]))
                    m = st.mark(nc.vector.tensor_tensor(rt["gate"][:], rt["one"][:], over_e(rs["w1"]), ALU.mult))
                    st.need(m)
                    dve.sem_inc(gate_ready, 1)
                    extra = 2
                else:
                    top("eq", "rk", "mr", "one", "logit", "mx")
                    do(nc.vector.scalar_tensor_tensor(rt["rest"][:], rt["one"][:], -3.0e38, rt["logit"][:],
                                                      ALU.mult, ALU.add))
                    do(nc.vector.tensor_reduce(rs["mx2"][:], rt["rest"][:], AX, ALU.max))
                    nc.vector.tensor_tensor(rs["d"][:], rs["mx2"][:], rs["mx"][:], ALU.subtract).then_inc(shift_ready, 1)
                    top("eq2", "rk2", "mr2", "two", "rest", "mx2")
                    dve.wait_ge(ex_ready, s + 1)
                    do(nc.vector.tensor_scalar(rs["den"][:], rs["ed"][:], 1.0, None, ALU.add))
                    do(nc.vector.reciprocal(rs["w1"][:], rs["den"][:]))
                    do(nc.vector.tensor_tensor(rs["w2"][:], rs["ed"][:], rs["w1"][:], ALU.mult))
                    do(nc.vector.tensor_tensor(rt["g1"][:], rt["one"][:], over_e(rs["w1"]), ALU.mult))
                    do(nc.vector.tensor_tensor(rt["g2"][:], rt["two"][:], over_e(rs["w2"]), ALU.mult))
                    m = st.mark(nc.vector.tensor_tensor(rt["gate"][:], rt["g1"][:], rt["g2"][:], ALU.add))
                    st.need(m)
                    dve.sem_inc(gate_ready, 1)
                    extra = 2
                dve.wait_ge(gt_ready, s + 1)
                nc.vector.tensor_copy(gate_t[:], bank[1][0:NT * E, 0:P]).then_inc(gts_ready, 1)
                dve.wait_ge(bias_ready, s + 1)
                hs = h[:, bass.ds(NT * s, NT), :]
                before = st.mark(nc.vector.tensor_tensor(hs, bank[1][:].rearrange("p (j d) -> p j d", d=D), hs, ALU.add))
                st.need(before)
                dve.sem_inc(bias_used, 1)
                done = [before] * NT
                for e in range(E):
                    dve.wait_ge(y_ready, E * s + e + 3)
                    for j in range(NT):
                        tile = h[:, bass.ds(NT * s + j, 1), :].rearrange("p a d -> p (a d)")
                        st.need(done[j])
                        done[j] = st.mark(nc.vector.scalar_tensor_tensor(
                            tile, bank[6 + e % 2][:, D * j:D * (j + 1)], rt["gate"][:, j, e:e + 1], tile,
                            ALU.mult, ALU.add))
                    st.need(done[NT - 1])
                    dve.sem_inc(y_used, 1)
                if not last_slab:
                    st.end()

            slabs(dve, step)

        @block.gpsimd
        def _(pool):
            rstd_steps(nc, pool, f, k, var_ready, var_eps, rstd_ready, 1)

            def step(s, u, last_slab):
                if not last_slab:
                    rstd_steps(nc, pool, f, k, var_ready, var_eps, rstd_ready, s + 2)
                if n == 0:
                    pool.wait_ge(shift_ready, s + 1)
                    nc.gpsimd.tensor_tensor(rt["ex"][:].rearrange("p j e -> p (j e)"), k["euler"][:],
                                            rt["shift"][:].rearrange("p j e -> p (j e)"),
                                            ALU.pow).then_inc(ex_ready, 1)

            slabs(pool, step)

        @block.tensor
        def _(pe):
            def transposes(s, u):
                pe.wait_ge(xn_ready, s + 1)
                pe.wait_ge(xf_ready, s + 1)
                for j in range(NT):
                    last = nc.tensor.transpose(bank[0][:, P * j:P * (j + 1)], f["xn"][u][:, j, :], k["ident"][:])
                last.then_inc(xt_ready, 1)

            pe.sem_inc(y_ready, 2)
            pe.wait_ge(k[f"moe{n}_in"], 16 * EXPERT_LOADS)
            transposes(0, 0)

            def step(s, u, last_slab):
                x = f["xf"][u]
                pe.wait_ge(xf_ready, s + 2)
                pe.wait_ge(bias_used, s + 1)
                for j in range(NT):
                    last = nc.tensor.matmul(bank[1][:, E * j:E * (j + 1)], x[:, PAD + P * j:PAD + P * (j + 1)],
                                            k[f"r_w{n}"][:], start=True, stop=True)
                last.then_inc(logit_ready, 1)

                def hidden(e):
                    for g in range(G):
                        m = e * G + g
                        pe.wait_ge(hid_used, HP * s + m + 1)
                        nc.tensor.matmul(bank[2 + m % 4][:], w1[:, e, P * g:P * (g + 1)], x[:, PAD:PAD + T],
                                         start=True, stop=True).then_inc(hid_ready, 1)

                def output(e):
                    pe.wait_ge(hid_used, HP * s + 4 + G * (e + 1))
                    pe.wait_ge(y_used, E * s + e + 1)
                    for j in range(NT):
                        for g in range(G):
                            last = nc.tensor.matmul(bank[6 + e % 2][:, D * j:D * (j + 1)],
                                                    hid[e % 2][:, g, P * j:P * (j + 1)], w2[:, e, g, :],
                                                    start=(g == 0), stop=(g == G - 1))
                    last.then_inc(y_ready, 1)

                hidden(0)
                for e in range(E):
                    if e + 1 < E:
                        hidden(e + 1)
                    if e == 0:
                        pe.wait_ge(gate_ready, s + 1)
                        nc.tensor.transpose(bank[1][0:NT * E, 0:P], rt["gate"][:].rearrange("p j e -> p (j e)"),
                                            k["ident"][:]).then_inc(gt_ready, 1)
                    if e == 1:
                        pe.wait_ge(gts_ready, s + 1)
                        nc.tensor.matmul(bank[1][:], gate_t[:], b2[:].rearrange("r j d -> r (j d)"),
                                         start=True, stop=True).then_inc(bias_ready, 1)
                    output(e)
                    if e == 3 and not last_slab:
                        transposes(s + 1, 1 - u)

            slabs(pe, step)

        @block.scalar
        def _(act):
            def xf_copy(s, u):
                act.wait_ge(xt_ready, s + 1)
                nc.scalar.activation(f["xf"][u][:, PAD:PAD + T], bank[0][:], ACT.Copy).then_inc(xf_ready, 1)

            act.sem_inc(xf_ready, 1)
            act.sem_inc(hid_used, 4)
            xf_copy(0, 0)

            def step(s, u, last_slab):
                for e in range(E):
                    act.wait_ge(y_ready, E * s + e + 1)
                    for g in range(G):
                        m = e * G + g
                        act.wait_ge(hid_ready, HP * s + m + 1)
                        nc.scalar.activation(hid[e % 2][:, g, :], bank[2 + m % 4][:], func,
                                             bias=b1[:, e, g:g + 1]).then_inc(hid_used, 1)
                    if e == 0 and n == 1:
                        act.wait_ge(shift_ready, s + 1)
                        nc.scalar.activation(rs["ed"][:], rs["d"][:], ACT.Exp).then_inc(ex_ready, 1)
                    if e == 4 and not last_slab:
                        xf_copy(s + 1, 1 - u)

            slabs(act, step)


def sorted_mixture(nc, k, n, width, picks, rows_in, rows_out):
    with ExitStack() as ctx:
        sb, pb, sem = parts(nc, ctx, f"s{n}_")
        G = width // P
        NTT = NSEQ * NT
        NA = picks * NTT
        GT = NTT // GROUPS
        GA = picks * GT
        TILES = sorted_tiles(picks)
        GTILES = TILES // GROUPS
        RING = 4
        rows_in, rows_out = rows_in[0:P * TILES, :], rows_out[0:P * TILES, :]
        f = front_tensors(sb)
        xn_all = sb("xn_all", [P, NTT, D])
        back = sb("back", [P, NA, D])
        logit = sb("logit", [P, NTT, E])
        picked = sb("picked", [P, NA, E])
        weight = sb("weight", [P, NA])
        big = {name: sb(name, [P, NTT, E]) for name in ("shift", "ex", "eq", "rk", "rest")}
        col = {name: sb("col_" + name, [P, NTT]) for name in ("mx", "sum", "mr", "mx2", "d", "ed", "den")}
        cnt = sb("cnt", [P, GROUPS, E])
        tot_i, pad_i = sb("tot_i", [P, GROUPS, E], I32), sb("pad_i", [P, GROUPS, E], I32)
        pad_f, end, start, init = (sb(name, [P, GROUPS, E]) for name in ("pad_f", "end", "start", "init"))
        run = sb("run", [P, GROUPS, E, GA])
        sel = sb("sel", [P, NA, E])
        pos_f = sb("pos_f", [P, NA])
        pos = sb("pos", [P, NA], I32)
        first_i = sb("first_i", [P, TILES], I32)
        first = sb("first", [P, TILES])
        past = sb("past", [P, TILES, E])
        tile_e = sb("tile_e", [P, TILES])
        tile_ec = sb("tile_ec", [P, TILES])
        expert = sb("expert", [P, TILES], I32)
        xs = [sb(f"xs{u}", [P, D]) for u in range(RING)]
        xt = [sb(f"xt{u}", [P, P]) for u in range(RING)]
        w1 = [sb(f"w1{u}", [P, width]) for u in range(RING)]
        w2 = [sb(f"w2{u}", [P, G, D]) for u in range(RING)]
        b1 = [sb(f"b1{u}", [P, G]) for u in range(RING)]
        b2 = [sb(f"b2{u}", [P, D]) for u in range(RING)]
        hid = [sb(f"hid{u}", [P, G, P]) for u in range(2)]
        ys = [sb(f"ys{u}", [P, D]) for u in range(RING)]
        bank = [pb(f"bank{i}") for i in range(8)]
        var_ready, var_eps, rstd_ready = sem("var"), sem("eps"), sem("rstd")
        xn_ready, xt_ready, xf_ready, kept = sem("xn"), sem("xt_slab"), sem("xf"), sem("kept")
        logit_ready, logit_used = sem("logit_ready"), sem("logit_used")
        pool_const, shift_ready, ex_ready = sem("pool_const"), sem("shift_ready"), sem("ex_ready")
        cnt_ready, sums_ready, pos_ready, expert_ready = sem("cnt_ready"), sem("sums"), sem("pos_ready"), sem("expert_ready")
        scattered, gathered = ([sem(f"{name}{g}") for g in range(GROUPS)] for name in ("scattered", "gathered"))
        xs_in = [sem(f"xs_in{u}") for u in range(RING)]
        ys_out = [sem(f"ys_out{u}") for u in range(RING)]
        tr_ready, xt_copied, w_copied = sem("tr"), sem("xt_copied"), sem("w_copied")
        hid_ready, hid_done, y_ready, ys_ready = sem("hid_ready"), sem("hid_done"), sem("y_ready"), sem("ys_ready")
        slab_step, seq_step, add_step = sem("slab_step"), sem("seq_step"), sem("add_step")
        func = ACT.Gelu if n == 0 else ACT.Relu
        w1_all, b1_all, w2_all, b2_all = k[f"w1_{n}"], k[f"b1_{n}"], k[f"w2_{n}"], k[f"b2_{n}"]
        h = k["h"]

        block = ctx.enter_context(nc.Block())

        def lagged(eng, step):
            for i in range(2 * RING):
                step(i, i % RING)
            with eng.Fori(2, TILES // RING) as q:
                for u in range(RING):
                    step(RING * q + u, u)
            for i in range(TILES // RING * RING, TILES + RING):
                step(i, i % RING)

        def since(i, lag):
            return not isinstance(i, int) or i >= lag

        def turns(i, u):
            return i // RING + 1 if isinstance(i, int) else (i - u) // RING + 1

        def is_tile(i, lag):
            return not isinstance(i, int) or 0 <= i - lag < TILES

        def pick_of(pick):
            return picked[:].rearrange("p (g q t) e -> p g q t e", g=GROUPS, q=picks)[:, :, pick]

        def weight_of(pick):
            return weight[:].rearrange("p (g q t) -> p g q t", g=GROUPS, q=picks)[:, :, pick]

        def by_group(t):
            return t.rearrange("p (g t) ... -> p g t ...".replace(" ...", " e" if len(t.shape) == 3 else ""), g=GROUPS)

        @block.vector
        def _(dve):
            dve.sem_inc(logit_used, 1)
            st = Steps(dve, slab_step, 2 * NT, ahead=2 * NT)
            st.n, st.base = 0, 0
            normalise(nc, k, st, f, 0, 0, var_ready, rstd_ready, xn_ready)

            def slab(s, u, last_slab):
                st.slab(s)
                if not last_slab:
                    normalise(nc, k, st, f, s + 1, 1 - u, var_ready, rstd_ready, xn_ready)
                dve.wait_ge(logit_ready, s + 1)
                nc.vector.tensor_tensor(logit[:, bass.ds(NT * s, NT), :],
                                        bank[1][:, 0:NT * E].rearrange("p (j e) -> p j e", e=E),
                                        k[f"r_b{n}"][:].unsqueeze(1).broadcast_to([P, NT, E]),
                                        ALU.add).then_inc(logit_used, 1)

            slabs(dve, slab)
            dve.wait_ge(logit_used, NSEQ + 1)
            seq = [0]

            def do(ins):
                ins.then_inc(seq_step, 1)
                seq[0] += 1
                dve.wait_ge(seq_step, seq[0])

            def over_e(t, m=NTT):
                return t.unsqueeze(2).broadcast_to([P, m, E])

            def top(pick, logits, mx):
                do(nc.vector.tensor_tensor(big["eq"][:], logits[:], over_e(mx[:]), ALU.is_equal))
                do(nc.vector.tensor_tensor(big["rk"][:], big["eq"][:],
                                           k["rank"][:].unsqueeze(1).broadcast_to([P, NTT, E]), ALU.mult))
                do(nc.vector.tensor_reduce(col["mr"][:], big["rk"][:], AX, ALU.max))
                do(nc.vector.tensor_tensor(pick_of(pick), by_group(big["rk"][:]),
                                           by_group(col["mr"][:]).unsqueeze(3).broadcast_to([P, GROUPS, GT, E]),
                                           ALU.is_equal))

            do(nc.vector.tensor_reduce(col["mx"][:], logit[:], AX, ALU.max))
            if picks == 1:
                nc.vector.tensor_tensor(big["shift"][:], logit[:], over_e(col["mx"][:]),
                                        ALU.subtract).then_inc(shift_ready, 1)
            top(0, logit, col["mx"])
            if picks == 2:
                for g in range(GROUPS):
                    do(nc.vector.scalar_tensor_tensor(by_group(big["rest"][:])[:, g], pick_of(0)[:, g], -3.0e38,
                                                      by_group(logit[:])[:, g], ALU.mult, ALU.add))
                do(nc.vector.tensor_reduce(col["mx2"][:], big["rest"][:], AX, ALU.max))
                nc.vector.tensor_tensor(col["d"][:], col["mx2"][:], col["mx"][:], ALU.subtract).then_inc(shift_ready, 1)
                top(1, big["rest"], col["mx2"])

            for g in range(GROUPS):
                last = nc.vector.tensor_reduce(cnt[:, g, :], picked[:, GA * g:GA * (g + 1), :].rearrange("p n e -> p e n"),
                                               AX, ALU.add)
            last.then_inc(cnt_ready, 1)
            dve.wait_ge(sums_ready, 1)
            before, total = (bank[0][:, GROUPS * E * n:GROUPS * E * (n + 1)].rearrange("p (g e) -> p g e", e=E)
                             for n in range(2))
            do(nc.vector.tensor_scalar(tot_i[:], total, float(P - 1), None, ALU.add))
            do(nc.vector.tensor_scalar(pad_i[:], tot_i[:], 7, 7, ALU.arith_shift_right, ALU.logical_shift_left))
            do(nc.vector.tensor_copy(pad_f[:], pad_i[:]))
            for g in range(GROUPS):
                do(nc.vector.tensor_tensor_scan(end[:, g, :], k["ones"][:, 0:E], pad_f[:, g, :],
                                                float(P * GTILES * g), ALU.mult, ALU.add))
            do(nc.vector.tensor_tensor(start[:], end[:], pad_f[:], ALU.subtract))
            do(nc.vector.scalar_tensor_tensor(init[:], start[:], -1.0, before, ALU.add, ALU.add))
            for g in range(GROUPS):
                for e in range(E):
                    nc.vector.tensor_tensor_scan(run[:, g, e, :], k["ones"][:, 0:GA], picked[:, GA * g:GA * (g + 1), e],
                                                 init[:, g, e:e + 1], ALU.mult, ALU.add).then_inc(seq_step, 1)
            seq[0] += GROUPS * E
            dve.wait_ge(seq_step, seq[0])
            for g in range(GROUPS):
                nc.vector.tensor_tensor(sel[:, GA * g:GA * (g + 1), :], run[:, g].rearrange("p e n -> p n e"),
                                        picked[:, GA * g:GA * (g + 1), :], ALU.mult).then_inc(seq_step, 1)
            seq[0] += GROUPS
            dve.wait_ge(seq_step, seq[0])
            do(nc.vector.tensor_reduce(pos_f[:], sel[:], AX, ALU.add))
            nc.vector.tensor_copy(pos[:], pos_f[:]).then_inc(pos_ready, 1)

            dve.wait_ge(pool_const, 1)
            do(nc.vector.tensor_copy(first[:], first_i[:]))
            for g in range(GROUPS):
                tiles = slice(GTILES * g, GTILES * (g + 1))
                do(nc.vector.tensor_tensor(past[:, tiles], over_e(first[:, tiles], GTILES),
                                           end[:, g].unsqueeze(1).broadcast_to([P, GTILES, E]), ALU.is_ge))
            do(nc.vector.tensor_reduce(tile_e[:], past[:], AX, ALU.add))
            do(nc.vector.tensor_scalar(tile_ec[:], tile_e[:], float(E - 1), None, ALU.min))
            do(nc.vector.tensor_copy(expert[:], tile_ec[:]))

            dve.wait_ge(ex_ready, 1)
            if picks == 1:
                do(nc.vector.tensor_reduce(col["sum"][:], big["ex"][:], AX, ALU.add))
                do(nc.vector.reciprocal(weight_of(0), by_group(col["sum"][:])))
            else:
                do(nc.vector.tensor_scalar(col["den"][:], col["ed"][:], 1.0, None, ALU.add))
                do(nc.vector.reciprocal(weight_of(0), by_group(col["den"][:])))
                do(nc.vector.tensor_tensor(weight_of(1), by_group(col["ed"][:]), weight_of(0), ALU.mult))

            dve.wait_ge(k[f"moe{n}_in"], 16 * EXPERT_LOADS)

            def tile_round(i, u):
                if is_tile(i, 0):
                    if since(i, RING):
                        dve.wait_ge(ys_ready, i - RING + 1)
                    e = dve.value_load(expert[0:1, bass.ds(i, 1)], min_val=0, max_val=E - 1)
                    nc.vector.tensor_copy(w1[u][:], w1_all[:, bass.ds(e, 1), :].rearrange("p a f -> p (a f)"))
                    nc.vector.tensor_copy(w2[u][:], w2_all[:, bass.ds(e, 1), :, :].rearrange("p a g d -> p (a g) d"))
                    nc.vector.tensor_copy(b1[u][:], b1_all[:, bass.ds(e, 1), :].rearrange("p a g -> p (a g)"))
                    nc.vector.tensor_copy(b2[u][:], b2_all[:, bass.ds(e, 1), :].rearrange("p a d -> p (a d)")
                                          ).then_inc(w_copied, 1)
                    dve.wait_ge(tr_ready, i + 1)
                    nc.vector.tensor_copy(xt[u][:], bank[u % 2][:, 0:P]).then_inc(xt_copied, 1)
                if is_tile(i, 2):
                    v = (u - 2) % RING
                    dve.wait_ge(y_ready, i - 1)
                    if since(i, 2 + RING):
                        dve.wait_ge(ys_out[v], 16 * (turns(i - 2, v) - 1))
                    dve.wait_ge(w_copied, i - 1)
                    nc.vector.tensor_tensor(ys[v][:], bank[4 + v % 2][:, 0:D], b2[v][:], ALU.add).then_inc(ys_ready, 1)

            lagged(dve, tile_round)

            adds = 0
            for g in range(GROUPS):
                dve.wait_ge(gathered[g], 16 * GA)
                for a in range(GA):
                    t, at = GT * g + a % GT, GA * g + a
                    if a >= GT:
                        dve.wait_ge(add_step, adds - GT + 1)
                    nc.vector.scalar_tensor_tensor(h[:, t, :], back[:, at, :], weight[:, at:at + 1], h[:, t, :],
                                                   ALU.mult, ALU.add).then_inc(add_step, 1)
                    adds += 1

        @block.gpsimd
        def _(pool):
            nc.gpsimd.iota(first_i[:], pattern=[[P, TILES]], base=0, channel_multiplier=0).then_inc(pool_const, 1)
            rstd_steps(nc, pool, f, k, var_ready, var_eps, rstd_ready, 1)

            def slab(s, u, last_slab):
                if not last_slab:
                    rstd_steps(nc, pool, f, k, var_ready, var_eps, rstd_ready, s + 2)

            slabs(pool, slab)
            pool.wait_ge(kept, NSEQ)
            pool.wait_ge(pos_ready, 1)
            pool.wait_ge(k["blank"], 16)
            for g in range(GROUPS):
                for a in range(GA):
                    at = GA * g + a
                    pool.indirect_dma_start(out=rows_in, in_=xn_all[:, GT * g + a % GT, :], in_offset=None,
                                            out_offset=bass.IndirectOffsetOnAxis(ap=pos[:, at:at + 1], axis=0)
                                            ).then_inc(scattered[g], 16)
            for g in range(GROUPS):
                for u in range(RING):
                    pool.wait_ge(ys_out[u], 16 * len(range(u, GTILES * (g + 1), RING)))
                for a in range(GA):
                    at = GA * g + a
                    pool.indirect_dma_start(out=back[:, at, :], out_offset=None,
                                            in_=rows_out[0:P * GTILES * (g + 1), :],
                                            in_offset=bass.IndirectOffsetOnAxis(ap=pos[:, at:at + 1], axis=0)
                                            ).then_inc(gathered[g], 16)

        @block.sync
        def _(sp):
            def tile_round(i, u):
                if is_tile(i, 0):
                    if isinstance(i, int) and i % GTILES == 0:
                        sp.wait_ge(scattered[i // GTILES], 16 * GA)
                    if since(i, RING):
                        sp.wait_ge(tr_ready, i - RING + 1)
                    sp.dma_start(xs[u][:], rows_in[bass.ds(P * i, P), :]).then_inc(xs_in[u], 16)
                if is_tile(i, RING):
                    sp.wait_ge(ys_ready, i - RING + 1)
                    sp.dma_start(rows_out[bass.ds(P * (i - RING), P), :], ys[u][:]).then_inc(ys_out[u], 16)

            assert GROUPS == 2
            for i in range(2 * RING):
                tile_round(i, i % RING)
            with sp.Fori(2, GTILES // RING) as q:
                for u in range(RING):
                    tile_round(RING * q + u, u)
            for i in range(GTILES // RING * RING, (GTILES // RING + 1) * RING):
                tile_round(i, i % RING)
            with sp.Fori(GTILES // RING + 1, TILES // RING) as q:
                for u in range(RING):
                    tile_round(RING * q + u, u)
            for i in range(TILES // RING * RING, TILES + RING):
                tile_round(i, i % RING)

        @block.tensor
        def _(pe):
            pe.wait_ge(k[f"moe{n}_in"], 16 * EXPERT_LOADS)

            def slab(s, u, last_slab):
                x = f["xf"][u]
                pe.wait_ge(xn_ready, s + 1)
                for j in range(NT):
                    last = nc.tensor.transpose(bank[2 * u][:, P * j:P * (j + 1)], f["xn"][u][:, j, :], k["ident"][:])
                last.then_inc(xt_ready, 1)
                pe.wait_ge(xf_ready, s + 1)
                pe.wait_ge(logit_used, s + 1)
                for j in range(NT):
                    last = nc.tensor.matmul(bank[1][:, E * j:E * (j + 1)], x[:, PAD + P * j:PAD + P * (j + 1)],
                                            k[f"r_w{n}"][:], start=True, stop=True)
                last.then_inc(logit_ready, 1)

            slabs(pe, slab)
            pe.wait_ge(cnt_ready, 1)
            for m, name in enumerate(("lt", "ones")):
                last = nc.tensor.matmul(bank[0][:, GROUPS * E * m:GROUPS * E * (m + 1)], k[name][:],
                                        cnt[:].rearrange("p g e -> p (g e)"), start=True, stop=True)
            last.then_inc(sums_ready, 1)

            def tile_round(i, u):
                if is_tile(i, 0):
                    pe.wait_ge(xs_in[u], 16 * turns(i, u))
                    if since(i, 2):
                        pe.wait_ge(xt_copied, i - 1)
                    nc.tensor.transpose(bank[u % 2][:, 0:P], xs[u][:], k["ident"][:]).then_inc(tr_ready, 1)
                if is_tile(i, 1):
                    v = (u - 1) % RING
                    pe.wait_ge(xt_copied, i)
                    pe.wait_ge(w_copied, i)
                    if since(i, 3):
                        pe.wait_ge(hid_done, i - 2)
                    for g in range(G):
                        last = nc.tensor.matmul(bank[2 + v % 2][:, P * g:P * (g + 1)], w1[v][:, P * g:P * (g + 1)],
                                                xt[v][:], start=True, stop=True)
                    last.then_inc(hid_ready, 1)
                if is_tile(i, 2):
                    v = (u - 2) % RING
                    pe.wait_ge(hid_done, i - 1)
                    if since(i, 4):
                        pe.wait_ge(ys_ready, i - 3)
                    for g in range(G):
                        last = nc.tensor.matmul(bank[4 + v % 2][:, 0:D], hid[v % 2][:, g, :], w2[v][:, g, :],
                                                start=(g == 0), stop=(g == G - 1))
                    last.then_inc(y_ready, 1)

            lagged(pe, tile_round)

        @block.scalar
        def _(act):
            def slab(s, u, last_slab):
                act.wait_ge(xn_ready, s + 1)
                nc.scalar.activation(xn_all[:, bass.ds(NT * s, NT), :], f["xn"][u][:], ACT.Copy).then_inc(kept, 1)
                act.wait_ge(xt_ready, s + 1)
                nc.scalar.activation(f["xf"][u][:, PAD:PAD + T], bank[2 * u][:], ACT.Copy).then_inc(xf_ready, 1)

            slabs(act, slab)
            act.wait_ge(shift_ready, 1)
            nc.scalar.activation(*((big["ex"][:], big["shift"][:]) if picks == 1 else (col["ed"][:], col["d"][:])),
                                 ACT.Exp).then_inc(ex_ready, 1)

            def tile_round(i, u):
                if is_tile(i, 1):
                    v = (u - 1) % RING
                    act.wait_ge(hid_ready, i)
                    for g in range(G):
                        last = nc.scalar.activation(hid[v % 2][:, g, :], bank[2 + v % 2][:, P * g:P * (g + 1)], func,
                                                    bias=b1[v][:, g:g + 1])
                    last.then_inc(hid_done, 1)

            lagged(act, tile_round)


_INS = ['x', 'L0_tok_w', 'L0_attn_in_proj_w', 'L0_attn_conv_fwd_w', 'L0_attn_conv_fwd_b', 'L0_attn_proj_fwd_w',
        'L0_attn_proj_fwd_b', 'L0_attn_conv_bwd_w', 'L0_attn_conv_bwd_b', 'L0_attn_proj_bwd_w', 'L0_attn_proj_bwd_b',
        'L0_attn_diag_weight', 'L0_attn_gate_scale', 'L0_attn_out_proj_w', 'L0_attn_ln_g', 'L0_attn_ln_b',
        'L0_ffn_Ws', 'L0_ffn_bs', 'L0_ffn_W1', 'L0_ffn_b1', 'L0_ffn_W2', 'L0_ffn_b2', 'L1_attn_in_proj_w',
        'L1_attn_conv_w', 'L1_attn_conv_b', 'L1_attn_dt_bias', 'L1_attn_A_log', 'L1_attn_D_skip', 'L1_attn_norm_w',
        'L1_attn_ssm_out_w', 'L1_attn_fuse_w', 'L1_attn_fuse_b', 'L1_ffn_gate_w', 'L1_ffn_gate_b', 'L1_ffn_w1',
        'L1_ffn_b1', 'L1_ffn_w2', 'L1_ffn_b2']


def kernel(**inputs):
    import numpy as _np
    import concourse.bacc as _bacc
    from concourse import mybir as _mybir
    from concourse.bass_utils import run_bass_kernel_spmd as _run

    nc = _bacc.Bacc("TRN2", target_bir_lowering=False, num_devices=1)
    arrays, aps = {}, {}
    for name in _INS:
        a = _np.ascontiguousarray(inputs[name])
        arrays[f"in_{name}"] = a
        aps[name] = nc.dram_tensor(f"in_{name}", a.shape, _mybir.dt.from_np(a.dtype), kind="ExternalInput").ap()
    out = nc.dram_tensor("out", (NSEQ, T, D), _mybir.dt.float32, kind="ExternalOutput").ap()
    build(nc, aps, out)
    r = _run(nc, [arrays], core_ids=[0])
    return r.results[0]["out"]
```

```python
from contextlib import ExitStack

import numpy as np

import concourse.bass as bass
from concourse import mybir

F32 = mybir.dt.float32
I32 = mybir.dt.int32
ALU = mybir.AluOpType
ACT = mybir.ActivationFunctionType
AX = mybir.AxisListType.X

P = 128
D = 128
NSEQ = 8
T = 512
NT = T // P
VOCAB = 50257
EPS = 1e-5
DI = 256
HB = DI // P
TAPS = 7
PAD = TAPS
XW = PAD + T + PAD
E = 8
F0 = 512
F1 = 256
CH = 512
CB = CH // P
MT = 4
NH = 4
HD = 64
PAIRS = NSEQ // 2
EXPERT_LOADS = [3 + 2 * f // P + NT for f in (F0, F1)]
EARLY = 4
GROUPS = 2


def parts(nc, ctx, stage=""):
    def sb(name, shape, dt=F32):
        return ctx.enter_context(nc.sbuf_tensor(stage + name, shape, dt))

    def pb(name):
        return ctx.enter_context(nc.psum_tensor(stage + name, [P, 512], F32))

    def sem(name):
        return ctx.enter_context(nc.semaphore(stage + name))

    return sb, pb, sem


def slabs(eng, step):
    with eng.Fori(0, PAIRS - 1) as i:
        step(2 * i, 0, 2)
        step(2 * i + 1, 1, 2)
    step(NSEQ - 2, 0, 1)
    step(NSEQ - 1, 1, 0)


class Steps:

    def __init__(self, eng, sem, per, ahead=0):
        self.eng, self.sem, self.per, self.ahead = eng, sem, per, ahead
        self.n = 0
        self.base = 0

    def slab(self, s):
        self.n, self.base = 0, self.per * s + self.ahead

    def mark(self, ins):
        ins.then_inc(self.sem, 1)
        self.n += 1
        return self.n

    def need(self, n):
        self.eng.wait_ge(self.sem, self.base + n)

    def end(self):
        assert self.n == self.per, self.n


def expert_tensors(k, sb, n, f):
    k[f"r_w{n}"] = sb(f"r_w{n}", [P, E])
    k[f"r_b{n}"] = sb(f"r_b{n}", [P, E])
    k[f"experts{n}"] = sb(f"experts{n}", [P, E, expert_parts(f)[-1].stop])


def expert_parts(f):
    stops = np.cumsum([0, f, f // P * D, f // P, D])
    return [slice(int(a), int(b)) for a, b in zip(stops[:-1], stops[1:])]


def expert_loads(w, k, n):
    router_w, router_b, w1, b1, w2, b2 = (w[name] for name in (
        ("L0_ffn_Ws", "L0_ffn_bs", "L0_ffn_W1", "L0_ffn_b1", "L0_ffn_W2", "L0_ffn_b2"),
        ("L1_ffn_gate_w", "L1_ffn_gate_b", "L1_ffn_w1", "L1_ffn_b1", "L1_ffn_w2", "L1_ffn_b2"))[n])
    f = (F0, F1)[n]
    all_w1, all_w2, all_b1, all_b2 = (k[f"experts{n}"][:, :, part] for part in expert_parts(f))
    loads = [(k[f"r_w{n}"][:], router_w), (k[f"r_b{n}"][:], router_b.partition_broadcast(P)),
             (all_w1, w1.rearrange("e d f -> d e f"))]
    for g in range(f // P):
        loads.append((all_w2[:, :, D * g:D * (g + 1)], w2[:, P * g:P * (g + 1), :].rearrange("e p d -> p e d")))
        loads.append((all_b1[:, :, g], b1.rearrange("e (g p) -> p g e", p=P)[:, g]))
    for j in range(NT):
        loads.append((all_b2[P // NT * j:P // NT * (j + 1)], b2.partition_broadcast(P // NT)))
    assert len(loads) == EXPERT_LOADS[n]
    return loads


def sorted_tiles(picks):
    return GROUPS * (picks * NSEQ * NT // GROUPS + E - 1)


def build(nc, w, out):
    rows_in = nc.dram_tensor("rows_in", (sorted_tiles(2) * P, D), F32, kind="Internal").ap()
    rows_out = nc.dram_tensor("rows_out", (sorted_tiles(2) * P, D), F32, kind="Internal").ap()
    with ExitStack() as ctx:
        sb, pb, sem = parts(nc, ctx)
        k = {}
        k["h"] = sb("h", [P, NSEQ * NT, D])
        k["ident"] = sb("ident", [P, P])
        k["ones"] = sb("ones", [P, P])
        for name in ("le", "lt", "ge", "gt"):
            k[name] = sb("mask_" + name, [P, P])
        k["mhalf"] = sb("minus_half", [P, 2 * NT])
        k["eps"] = sb("eps", [P, 2 * NT])
        k["held"] = sem("held")
        k["inv_di"] = sb("inv_di", [P, 2 * NT])
        k["rank"] = sb("rank", [P, E])
        k["z_w"] = sb("z_w", [P, DI])
        k["dt_w"] = sb("dt_w", [P, NH])
        k["xbc_w"] = sb("xbc_w", [P, CH])
        k["mtap"] = sb("mtap", [P, CB, MT])
        k["conv_b"] = sb("conv_b", [P, CB])
        k["dt_b"] = sb("dt_b", [P, NH])
        k["a_neg"] = sb("a_neg", [P, NH])
        k["skip"] = sb("skip", [P, HB, P])
        k["fuse_w"] = sb("fuse_w", [P, HB, 2, D])
        k["fuse_b"] = sb("fuse_b", [P, D])
        k["pos0"] = sb("pos0", [P, NSEQ * NT], I32)
        k["weight0"] = sb("weight0", [P, NSEQ * NT])
        k["moe0_in"] = sem("moe0_in")
        k["moe1_in"] = sem("moe1_in")
        k["stored"] = sem("stored")
        k["blank"] = sem("blank")
        k["gathered"] = sem("rows_gathered")
        with ExitStack() as half:
            sb0, _, _ = parts(nc, half)
            k["ids"] = sb0("ids", [P, NSEQ * NT], I32)
            k["zeros"] = sb0("zeros", [P, D])
            k["xz_w"] = sb0("xz_w", [P, 2 * DI])
            k["tap"] = sb0("tap", [P, 2, HB, TAPS])
            k["proj_w"] = sb0("proj_w", [P, 2, HB, DI])
            k["tap_b"] = sb0("tap_b", [P, 2 * HB])
            k["diag"] = sb0("diag", [P, HB])
            k["out_w"] = sb0("out_w", [P, HB, D])
            k["ln_g"] = sb0("ln_g", [P, D])
            k["ln_b"] = sb0("ln_b", [P, D])
            expert_tensors(k, sb0, 0, F0)
            setup(nc, w, k)
            attention0(nc, w, k, expert_loads(w, k, 0), rows_in)
            sorted_mixture(nc, k, 0, F0, 1, rows_in, rows_out)
        with ExitStack() as half:
            sb1, _, _ = parts(nc, half)
            expert_tensors(k, sb1, 1, F1)
            attention1(nc, k, expert_loads(w, k, 1), rows_out)
            sorted_mixture(nc, k, 1, F1, 2, rows_in, rows_out, out)


def gather(pool, w, k, tiles):
    for n in tiles:
        pool.indirect_dma_start(out=k["h"][:, n, :], out_offset=None, in_=w["L0_tok_w"],
                                in_offset=bass.IndirectOffsetOnAxis(ap=k["ids"][:, n:n + 1], axis=0),
                                ).then_inc(k["gathered"], 16)


def setup(nc, w, k):
    with ExitStack() as ctx:
        sb, pb, sem = parts(nc, ctx)
        xz_nat = sb("xz_nat", [P, 4, D])
        proj_nat = sb("proj_nat", [P, 2, HB, DI])
        conv_bias = sb("conv_bias", [P, 2, HB])
        proj_bias = sb("proj_bias", [P, 2 * HB])
        gate_scale = sb("gate_scale", [P, 1])
        out_nat = sb("out_nat", [P, DI])
        in_nat = sb("in_nat", [P, 6, D])
        dt_nat = sb("dt_nat", [NH, D])
        a_log = sb("a_log", [P, NH])
        a_exp = sb("a_exp", [P, NH])
        skip_col = sb("skip_col", [P, HB])
        norm_col = sb("norm_col", [P, HB])
        ssm_nat = sb("ssm_nat", [P, DI])
        fuse_nat = sb("fuse_nat", [P, 2, D])
        fuse_t = sb("fuse_t", [P, 2, D])
        bank = [pb(f"setup_bank{i}") for i in range(8)]
        ids_in, weights_in = sem("ids_in"), sem("weights_in")
        consts = sem("consts")
        group_ready, group_used = sem("group_ready"), sem("group_used")
        exp_ready = sem("exp_ready")

        def row(a):
            return a.partition_broadcast(P)

        def cols(a):
            return a.rearrange("(b p) -> p b", p=P)

        early = [
            (xz_nat[:], w["L0_attn_in_proj_w"].rearrange("(g p) d -> p g d", p=P)),
            (proj_nat[:, 0], w["L0_attn_proj_fwd_w"].rearrange("(g p) c -> p g c", p=P)),
            (proj_nat[:, 1], w["L0_attn_proj_bwd_w"].rearrange("(g p) c -> p g c", p=P)),
            (k["tap"][:, 0], w["L0_attn_conv_fwd_w"].rearrange("(g p) o k -> p g (o k)", p=P)),
            (k["tap"][:, 1], w["L0_attn_conv_bwd_w"].rearrange("(g p) o k -> p g (o k)", p=P)),
            (out_nat[:], w["L0_attn_out_proj_w"]),
            (in_nat[:], w["L1_attn_in_proj_w"][0:6 * P].rearrange("(g p) d -> p g d", p=P)),
            (dt_nat[:], w["L1_attn_in_proj_w"][6 * P:6 * P + NH]),
            (k["mtap"][:], w["L1_attn_conv_w"].rearrange("(g p) o k -> p g (o k)", p=P)),
            (ssm_nat[:], w["L1_attn_ssm_out_w"]),
            (fuse_nat[:], w["L1_attn_fuse_w"].rearrange("o (g m) -> o g m", g=2)),
        ]
        small = [
            (gate_scale[:], row(w["L0_attn_gate_scale"])),
            (k["ln_g"][:], row(w["L0_attn_ln_g"])), (k["ln_b"][:], row(w["L0_attn_ln_b"])),
            (k["dt_b"][:], row(w["L1_attn_dt_bias"])), (a_log[:], row(w["L1_attn_A_log"])),
            (k["fuse_b"][:], row(w["L1_attn_fuse_b"])),
        ]
        for d, n in enumerate(("fwd", "bwd")):
            small.append((conv_bias[:, d], cols(w[f"L0_attn_conv_{n}_b"])))
            small.append((proj_bias[:, HB * d:HB * (d + 1)], cols(w[f"L0_attn_proj_{n}_b"])))
        small += [(k["diag"][:], cols(w["L0_attn_diag_weight"])), (norm_col[:], cols(w["L1_attn_norm_w"])),
                  (k["conv_b"][:], cols(w["L1_attn_conv_b"]))]
        for g in range(HB):
            for j in range(2):
                small.append((skip_col[HD * j:HD * (j + 1), g:g + 1],
                              w["L1_attn_D_skip"][2 * g + j:2 * g + j + 1].partition_broadcast(HD)))
        n_weights = len(early) + len(small)

        block = ctx.enter_context(nc.Block())

        @block.sync
        def _(sp):
            with nc.allow_non_contiguous_dma("bias columns"):
                sp.dma_start(k["ids"][:], w["x"].rearrange("s (j p) -> p (s j)", p=P)).then_inc(ids_in, 16)
                for dst, src in early + small:
                    sp.dma_start(dst, src).then_inc(weights_in, 16)

        @block.gpsimd
        def _(pool):
            for name in ("zeros", "ident", "ones", "le", "lt", "ge", "gt"):
                nc.gpsimd.memset(k[name][:], 0.0 if name in ("zeros", "ident") else 1.0).then_inc(consts, 1)
            nc.gpsimd.memset(k["mhalf"][:], -0.5).then_inc(consts, 1)
            nc.gpsimd.memset(k["eps"][:], EPS).then_inc(consts, 1)
            nc.gpsimd.memset(k["inv_di"][:], 1.0 / DI).then_inc(consts, 1)
            for e in range(E):
                nc.gpsimd.memset(k["rank"][:, e:e + 1], float(E - e)).then_inc(consts, 1)
            pool.wait_ge(consts, 10 + E)
            for name, cmp, cm, step, fill in (("ident", ALU.not_equal, 1, -1, 1.0), ("le", ALU.is_ge, -1, 1, 0.0),
                                              ("lt", ALU.is_gt, -1, 1, 0.0), ("ge", ALU.is_ge, 1, -1, 0.0),
                                              ("gt", ALU.is_gt, 1, -1, 0.0)):
                nc.gpsimd.affine_select(out=k[name][:], in_=k[name][:], compare_op=cmp, fill=fill, base=0,
                                        pattern=[[step, P]], channel_multiplier=cm).then_inc(consts, 1)
            pool.wait_ge(ids_in, 16)
            gather(pool, w, k, range(EARLY * NT))
            pool.wait_ge(k["gathered"], 16 * EARLY * NT)

        n_consts = 10 + E + 5

        @block.tensor
        def _(pe):
            pe.wait_ge(consts, n_consts)
            pe.wait_ge(weights_in, 16 * n_weights)
            g = [0]

            def group(work):
                if g[0] >= 8:
                    pe.wait_ge(group_used, g[0] - 7)
                last = work(bank[g[0] % 8])
                last.then_inc(group_ready, 1)
                g[0] += 1

            def transposes(sources):
                def work(b):
                    for n, src in enumerate(sources):
                        rows = src.shape[0]
                        last = nc.tensor.transpose(b[:, P * n:P * n + rows], src, k["ident"][0:rows, 0:rows])
                    return last
                return work

            group(transposes([xz_nat[:, n, :] for n in range(4)]))
            for d in range(2):
                group(transposes([proj_nat[:, d, o, P * c:P * (c + 1)] for c in range(HB) for o in range(HB)]))
            group(transposes([out_nat[:, 0:P], out_nat[:, P:DI], fuse_nat[:, 0, :], fuse_nat[:, 1, :]]))
            group(transposes([in_nat[:, 0, :], in_nat[:, 1, :], dt_nat[:, :]]))
            group(transposes([in_nat[:, 2 + b, :] for b in range(CB)]))
            pe.wait_ge(group_used, 3)

            def bias_products(b):
                for d in range(2):
                    for o in range(HB):
                        for c in range(HB):
                            last = nc.tensor.matmul(b[:, HB * d + o:HB * d + o + 1],
                                                    k["proj_w"][:, d, c, P * o:P * (o + 1)], conv_bias[:, d, c:c + 1],
                                                    start=(c == 0), stop=(c == HB - 1))
                return last

            group(bias_products)
            pe.wait_ge(group_used, 4)

            def fuse_products(b):
                for c in range(HB):
                    last = nc.tensor.matmul(b[:, 2 * D * c:2 * D * (c + 1)], ssm_nat[:, P * c:P * (c + 1)],
                                            fuse_t[:, :, :].rearrange("m g o -> m (g o)"), start=True, stop=True)
                return last

            group(fuse_products)

        @block.scalar
        def _(act):
            act.wait_ge(weights_in, 16 * n_weights)
            nc.scalar.activation(a_exp[:], a_log[:], ACT.Exp).then_inc(exp_ready, 1)
            g = [0]

            def used(*copies):
                act.wait_ge(group_ready, g[0] + 1)
                for dst, lo, hi, scale in copies:
                    src = bank[g[0] % 8][:, lo:hi]
                    last = nc.scalar.activation(dst, src, ACT.Copy, scale=scale)
                last.then_inc(group_used, 1)
                g[0] += 1

            used((k["xz_w"][:], 0, 512, 1.0))
            for d in range(2):
                used((k["proj_w"][:, d].rearrange("p c o -> p (c o)"), 0, 512, 1.0))
            used((k["out_w"][:].rearrange("p g d -> p (g d)"), 0, DI, gate_scale[:, 0:1]),
                 (fuse_t[:].rearrange("p g d -> p (g d)"), DI, 2 * DI, 1.0))
            used((k["z_w"][:], 0, DI, 1.0), (k["dt_w"][:], DI, DI + NH, 1.0))
            used((k["xbc_w"][:], 0, 512, 1.0))
            act.wait_ge(group_ready, g[0] + 1)
            for n in range(2 * HB):
                last = nc.scalar.activation(k["tap_b"][:, n:n + 1], bank[g[0] % 8][:, n:n + 1], ACT.Identity,
                                            bias=proj_bias[:, n:n + 1])
            last.then_inc(group_used, 1)
            g[0] += 1
            act.wait_ge(group_ready, g[0] + 1)
            for c in range(HB):
                last = nc.scalar.activation(k["fuse_w"][:, c].rearrange("p g d -> p (g d)"),
                                            bank[g[0] % 8][:, 2 * D * c:2 * D * (c + 1)], ACT.Copy,
                                            scale=norm_col[:, c:c + 1])
            last.then_inc(group_used, 1)

        @block.vector
        def _(dve):
            dve.wait_ge(weights_in, 16 * n_weights)
            dve.wait_ge(consts, n_consts)
            for c in range(HB):
                nc.vector.tensor_scalar(k["skip"][:, c, :], k["ident"][:], skip_col[:, c:c + 1], None, ALU.mult)
            dve.wait_ge(exp_ready, 1)
            nc.vector.tensor_scalar(k["a_neg"][:], a_exp[:], -1.0, None, ALU.mult)


def front_tensors(sb):
    return {
        "stats": sb("stats", [P, NT, 6]),
        "mv": sb("mv", [P, NT, 2]),
        "var": sb("var", [P, NT]),
        "rstd": sb("rstd", [P, NT]),
        "xn": [sb(f"xn{u}", [P, NT, D]) for u in range(2)],
        "xf": [sb(f"xf{u}", [P, XW]) for u in range(2)],
    }


def stat_steps(nc, k, st, f, src, var_ready):
    for j in range(NT):
        st.mark(nc.vector.bn_stats(f["stats"][:, j, :], src[:, j, :]))
    st.need(st.n)
    nc.vector.sem_inc(k["held"], 1)
    for j in range(NT):
        st.mark(nc.vector.bn_aggr(f["mv"][:, j, :], f["stats"][:, j, :]))
    st.need(st.n)
    nc.vector.tensor_copy(f["var"][:], f["mv"][:, :, 1]).then_inc(var_ready, 1)


def rstd_steps(nc, pool, f, k, var_ready, var_eps, rstd_ready, n):
    pool.wait_ge(var_ready, n)
    nc.gpsimd.tensor_tensor(f["var"][:], f["var"][:], k["eps"][:, 0:NT], ALU.add).then_inc(var_eps, 1)
    pool.wait_ge(var_eps, n)
    nc.gpsimd.tensor_tensor(f["rstd"][:], f["var"][:], k["mhalf"][:, 0:NT], ALU.pow).then_inc(rstd_ready, 1)


def attention0(nc, w, k, loads, rows_in):
    with ExitStack() as ctx:
        sb, pb, sem = parts(nc, ctx, "a_")
        f = front_tensors(sb)
        f2 = {"stats": sb("stats2", [P, NT, 6]), "mv": sb("mv2", [P, NT, 2]), "var": sb("var2", [P, NT]),
              "rstd": sb("rstd2", [P, NT])}
        xp = [sb(f"xp{u}", [P, HB, XW]) for u in range(2)]
        conved = [sb(f"conved{u}", [P, 2, HB, T]) for u in range(2)]
        RING = 8
        prod = [sb(f"prod{i}", [P, T]) for i in range(RING)]
        mix = sb("mix", [P, 4, T])
        gate = [sb(f"gate{u}", [P, HB, T]) for u in range(2)]
        both = sb("both", [P, HB, T])
        both_d = sb("both_d", [P, HB, T])
        y = sb("y", [P, HB, T])
        nrm_g = sb("nrm_g", [P, NT, D])
        nrm_b = sb("nrm_b", [P, NT, D])
        bank = [pb(f"bank{i}") for i in range(8)]
        edges = sem("edges")
        var_ready, var_eps, rstd_ready = sem("var"), sem("eps"), sem("rstd")
        var2_ready, var2_eps, rstd2_ready = sem("var2"), sem("eps2"), sem("rstd2")
        xn_ready, front_ready, front_used = sem("xn"), sem("front"), sem("front_used")
        prod_ready, sum_ready, fwd_ready = sem("prod"), sem("sum"), sem("fwd")
        proj_ready, silu_ready = sem("proj"), sem("silu")
        y_ready, out_ready, out_used = sem("y"), sem("out"), sem("out_used")
        dve_step = sem("dve")

        block = ctx.enter_context(nc.Block())
        h = k["h"]

        FRONT = 5
        FRONT_BANK = (bank[6], bank[4], bank[5], bank[6], bank[4])
        UNIT = 1 + TAPS - 2
        SUMS = TAPS - 1

        def span(d, t):
            at = t if d == 0 else 2 * PAD - t
            return slice(at, at + T)

        @block.sync
        def _(sp):
            sp.wait_ge(k["gathered"], 16 * NSEQ * NT)
            n_rows = sorted_tiles(2)
            sp.dma_start(rows_in.rearrange("(p n) d -> p n d", n=n_rows),
                         k["zeros"][:].unsqueeze(1).broadcast_to([P, n_rows, D])).then_inc(k["blank"], 16)
            with nc.allow_non_contiguous_dma("bias columns"):
                for dst, src in loads:
                    sp.dma_start(dst, src).then_inc(k["moe0_in"], 16)

        @block.vector
        def _(dve):
            dve.sem_inc(y_ready, 1)
            dve.sem_inc(out_used, 1)
            for u in range(2):
                nc.vector.memset(xp[u][:, :, 0:PAD], 0.0).then_inc(edges, 1)
                nc.vector.memset(xp[u][:, :, PAD + T:XW], 0.0).then_inc(edges, 1)
            nc.vector.memset(mix[:, 0:2, 0:1], 0.0).then_inc(edges, 1)
            nc.vector.memset(mix[:, 2:4, T - 1:T], 0.0).then_inc(edges, 1)
            dve.wait_ge(edges, 6)
            AHEAD = 2 * 2 * NT + 2 * HB * UNIT
            st = Steps(dve, dve_step, 2 * NT + HB * UNIT + 2 * HB + 2 * NT + 2 * NT, ahead=AHEAD)

            def stats(s):
                stat_steps(nc, k, st, f, h[:, bass.ds(NT * s, NT), :], var_ready)

            def scale(s, u):
                dve.wait_ge(rstd_ready, s + 1)
                for j in range(NT):
                    tile = h[:, bass.ds(NT * s + j, 1), :].rearrange("p a d -> p (a d)")
                    last = nc.vector.tensor_scalar(f["xn"][u][:, j, :], tile, f["mv"][:, j, 0:1],
                                                   f["rstd"][:, j:j + 1], ALU.subtract, ALU.mult)
                last.then_inc(xn_ready, 1)

            def conv(s, u, g, d=0):
                dve.wait_ge(front_used, FRONT * s + 2 + g)
                out = conved[u][:, d, g, :]
                for t in range(TAPS):
                    w = k["tap"][:, d, g, t:t + 1]
                    if t == 0:
                        ins = nc.vector.tensor_scalar(out, xp[u][:, g, span(d, t)], w, None, ALU.mult)
                    else:
                        st.need(st.n)
                        ins = nc.vector.scalar_tensor_tensor(out, xp[u][:, g, span(d, t)], w, out, ALU.mult, ALU.add)
                    if t < TAPS - 1:
                        st.mark(ins)
                    elif d == 0:
                        ins.then_inc(fwd_ready, 1)
                    else:
                        ins.then_inc(sum_ready, SUMS)

            st.n, st.base = 0, 0
            stats(0)
            scale(0, 0)
            stats(1)
            scale(1, 1)
            for g in range(HB):
                for d in range(2):
                    conv(0, 0, g, d)
            assert st.n == AHEAD
            dve.wait_ge(k["gathered"], 16 * NSEQ * NT)

            def step(s, u, left):
                if left:
                    st.slab(s)
                if left == 2:
                    stats(s + 2)
                if left:
                    conv(s + 1, 1 - u, 0)
                if left == 2:
                    scale(s + 2, u)
                for g in range(HB):
                    dve.wait_ge(silu_ready, 4 * s + 4 + g)
                    a = st.mark(nc.vector.tensor_tensor(both[:, g, :], mix[:, g, :], mix[:, 2 + g, :], ALU.add))
                    st.need(a)
                    b = st.mark(nc.vector.scalar_tensor_tensor(both_d[:, g, :], xp[u][:, g, PAD:PAD + T],
                                                               k["diag"][:, g:g + 1], both[:, g, :],
                                                               ALU.mult, ALU.add))
                    dve.wait_ge(front_used, FRONT * s + 4 + g)
                    st.need(b)
                    nc.vector.tensor_tensor(y[:, g, :], both_d[:, g, :], gate[u][:, g, :], ALU.mult).then_inc(y_ready, 1)
                if left:
                    conv(s + 1, 1 - u, 1)
                dve.wait_ge(out_ready, s + 1)
                res = bank[7][:].rearrange("p (j d) -> p j d", d=D)
                stat_steps(nc, k, st, f2, res, var2_ready)
                for j in range(NT):
                    n = st.mark(nc.vector.scalar_tensor_tensor(nrm_g[:, j, :], res[:, j, :], f2["mv"][:, j, 0:1],
                                                               k["ln_g"][:], ALU.subtract, ALU.mult))
                dve.wait_ge(rstd2_ready, s + 1)
                st.need(n)
                for j in range(NT):
                    n = st.mark(nc.vector.scalar_tensor_tensor(nrm_b[:, j, :], nrm_g[:, j, :], f2["rstd"][:, j:j + 1],
                                                               k["ln_b"][:], ALU.mult, ALU.add))
                st.need(n)
                hs = h[:, bass.ds(NT * s, NT), :]
                nc.vector.tensor_tensor(hs, hs, nrm_b[:], ALU.add).then_inc(out_used, 1)
                if left == 2:
                    st.end()

            slabs(dve, step)

        @block.gpsimd
        def _(pool):
            def sums(s, u, g):
                out = conved[u][:, 1, g, :]
                for t in range(1, TAPS):
                    n = TAPS * g + t
                    pool.wait_ge(prod_ready, HB * TAPS * s + n + 1)
                    if t == 1:
                        first = prod[(n - 1) % RING][:]
                    else:
                        first = out
                        pool.wait_ge(sum_ready, HB * SUMS * s + SUMS * g + t - 1)
                    nc.gpsimd.tensor_tensor(out, first, prod[n % RING][:], ALU.add).then_inc(sum_ready, 1)

            rstd_steps(nc, pool, f, k, var_ready, var_eps, rstd_ready, 1)
            rstd_steps(nc, pool, f, k, var_ready, var_eps, rstd_ready, 2)
            gather(pool, w, k, range(EARLY * NT, NSEQ * NT))

            def step(s, u, left):
                if left == 2:
                    rstd_steps(nc, pool, f, k, var_ready, var_eps, rstd_ready, s + 3)
                if left:
                    for g in range(HB):
                        sums(s + 1, 1 - u, g)
                rstd_steps(nc, pool, f2, k, var2_ready, var2_eps, rstd2_ready, s + 1)

            slabs(pool, step)

        @block.tensor
        def _(pe):
            pe.wait_ge(edges, 6)

            def front(s, u):
                x = f["xf"][u][:, PAD:PAD + T]
                pe.wait_ge(xn_ready, s + 1)
                for j in range(NT):
                    last = nc.tensor.transpose(bank[6][:, P * j:P * (j + 1)], f["xn"][u][:, j, :], k["ident"][:])
                last.then_inc(front_ready, 1)
                pe.wait_ge(front_used, FRONT * s + 1)
                for g in range(HB):
                    nc.tensor.matmul(FRONT_BANK[1 + g][:], k["xz_w"][:, P * g:P * (g + 1)], x,
                                     start=True, stop=True).then_inc(front_ready, 1)
                for g in range(HB):
                    pe.wait_ge(front_used, FRONT * s + 1 + g)
                    nc.tensor.matmul(FRONT_BANK[3 + g][:], k["xz_w"][:, DI + P * g:DI + P * (g + 1)], x,
                                     start=True, stop=True).then_inc(front_ready, 1)

            front(0, 0)
            pe.wait_ge(front_used, FRONT)
            front(1, 1)

            def step(s, u, left):
                pe.wait_ge(silu_ready, 4 * s + 1)
                for d in range(2):
                    if d == 0:
                        pe.wait_ge(fwd_ready, HB * (s + 1))
                    else:
                        pe.wait_ge(sum_ready, HB * SUMS * (s + 1))
                    for g in range(HB):
                        for c in range(HB):
                            last = nc.tensor.matmul(bank[2 * d + g][:], k["proj_w"][:, d, c, P * g:P * (g + 1)],
                                                    conved[u][:, d, c, :], start=(c == 0), stop=(c == HB - 1))
                        last.then_inc(proj_ready, 1)
                pe.wait_ge(out_used, s + 1)
                pe.wait_ge(y_ready, 2 * s + 3)
                for j in range(NT):
                    b = bank[7][:, D * j:D * (j + 1)]
                    for g in range(HB):
                        nc.tensor.matmul(b, y[:, g, P * j:P * (j + 1)], k["out_w"][:, g, :], start=(g == 0), stop=False)
                    last = nc.tensor.matmul(b, f["xf"][u][:, PAD + P * j:PAD + P * (j + 1)], k["ident"][:],
                                            start=False, stop=True)
                last.then_inc(out_ready, 1)
                if left == 2:
                    pe.wait_ge(front_used, FRONT * (s + 2))
                    front(s + 2, u)

            slabs(pe, step)

        @block.scalar
        def _(act):
            act.wait_ge(edges, 6)
            act.sem_inc(silu_ready, 1)

            def take(s, n):
                act.wait_ge(front_ready, FRONT * s + n + 1)
                return FRONT_BANK[n][:]

            def front_x(s, u):
                nc.scalar.activation(f["xf"][u][:, PAD:PAD + T], take(s, 0), ACT.Copy).then_inc(front_used, 1)
                for g in range(HB):
                    nc.scalar.activation(xp[u][:, g, PAD:PAD + T], take(s, 1 + g), ACT.Copy).then_inc(front_used, 1)

            def front_z(s, u):
                for g in range(HB):
                    nc.scalar.activation(gate[u][:, g, :], take(s, 3 + g), ACT.Silu).then_inc(front_used, 1)

            def products(s, u, numbers):
                for n in numbers:
                    g, t = n // TAPS, n % TAPS
                    if n >= RING:
                        before = n - RING
                        sums = SUMS * (before // TAPS) + max(before % TAPS, 1)
                        act.wait_ge(sum_ready, HB * SUMS * s + sums)
                    nc.scalar.activation(prod[n % RING][:], xp[u][:, g, span(1, t)], ACT.Copy,
                                         scale=k["tap"][:, 1, g, t:t + 1]).then_inc(prod_ready, 1)

            ALL = HB * TAPS
            front_x(0, 0)
            front_z(0, 0)
            act.wait_ge(front_used, FRONT)
            act.sem_inc(prod_ready, ALL)
            front_x(1, 1)
            front_z(1, 1)

            def step(s, u, left):
                if left:
                    act.wait_ge(sum_ready, HB * SUMS * (s + 1))
                    act.wait_ge(front_used, FRONT * (s + 2))
                act.wait_ge(y_ready, 2 * s + 1)
                turn = 0
                for d in range(2):
                    for g in range(HB):
                        if left:
                            products(s + 1, 1 - u, range(turn, turn + 2))
                            turn += 2
                        lo, hi = (1, T) if d == 0 else (0, T - 1)
                        act.wait_ge(proj_ready, 4 * s + 2 * d + g + 1)
                        nc.scalar.activation(mix[:, 2 * d + g, lo:hi], bank[2 * d + g][:, lo:hi], ACT.Silu,
                                             bias=k["tap_b"][:, 2 * d + g:2 * d + g + 1]).then_inc(silu_ready, 1)
                if left:
                    products(s + 1, 1 - u, range(turn, ALL))
                if left == 2:
                    act.wait_ge(y_ready, 2 * s + 3)
                    act.wait_ge(out_ready, s + 1)
                    front_x(s + 2, u)
                    front_z(s + 2, u)

            slabs(act, step)


LATE = NSEQ * NT // GROUPS
FIRST_LATE = 9


def late_gather(nc, pool, k, tiles, back, rows_out, gathered):
    for t in tiles:
        pool.indirect_dma_start(out=back[:, t, :], out_offset=None, in_=rows_out[0:P * sorted_tiles(1), :],
                                in_offset=bass.IndirectOffsetOnAxis(
                                    ap=k["pos0"][:, NSEQ * NT - LATE + t:NSEQ * NT - LATE + t + 1], axis=0)
                                ).then_inc(gathered, 16)


def attention1(nc, k, loads, rows_out):
    with ExitStack() as ctx:
        sb, pb, sem = parts(nc, ctx, "c_")
        C = 2 * NT
        CS = C - 2
        LEAD = 2
        REACH = MT - 1
        f = front_tensors(sb)
        xbc = sb("xbc", [P, CB, REACH + T + REACH])
        centre = [sb(f"centre{i}", [P, T]) for i in range(2)]
        prod = [sb(f"prod{b}", [P, 1 + (2 - b) * REACH, T]) for b in range(HB)]
        act_x = [sb(f"act_x{u}", [P, 2, CB, T]) for u in range(2)]
        zs = [sb(f"zs{u}", [P, NT, DI]) for u in range(2)]
        dt_raw = sb("dt_raw", [P, NT, NH])
        dt_x = sb("dt_x", [P, NT, NH])
        dt_n = sb("dt_n", [P, NT, NH])
        dt_e = sb("dt_e", [P, NT, NH])
        dt_l = sb("dt_l", [P, NT, NH])
        dt = [sb(f"dt{u}", [P, NT, NH]) for u in range(2)]
        da = [sb(f"da{u}", [P, NT, NH]) for u in range(2)]
        dec = [sb(f"dec{u}", [P, 5, NT, NH]) for u in range(2)]
        seg_in = [sb(f"seg_in{i}", [P, NH, P]) for i in range(2)]
        decay = [sb(f"decay{i}", [P, NH, P]) for i in range(2)]
        cb = [sb(f"cb{i}", [P, P]) for i in range(2)]
        mixer = sb("mixer", [P, C, NH, P])
        xdt = sb("xdt", [P, C, DI])
        xdd = sb("xdd", [P, CS, DI])
        b_t = sb("b_t", [P, CS, P])
        state = [sb(f"state{d}", [P, DI]) for d in range(2)]
        state_d = [sb(f"state_d{d}", [P, DI]) for d in range(2)]
        y_off = [sb(f"y_off{d}", [P, DI]) for d in range(2)]
        y_sum = [sb(f"y_sum{d}", [P, DI]) for d in range(2)]
        y = sb("y", [P, C, DI])
        ss = sb("ss", [P, C])
        ms = sb("ms", [P, C])
        mse = sb("mse", [P, C])
        rr = sb("rr", [P, C])
        yn = sb("yn", [P, C, DI])
        yt = [sb(f"yt{i}", [P, 4, P]) for i in range(2)]
        o = sb("o", [P, NT, D])
        bank = [pb(f"bank{i}") for i in range(8)]
        Y, ST, OWN, SEG = bank[0:2], bank[2:4], bank[4:6], bank[6:8]
        YT, OUT_BANK, SUM_BANK, FRONT_BANK = bank[0:2], bank[2], bank[6], (bank[4], bank[6], bank[5], bank[7])
        var_ready, var_eps, rstd_ready = sem("var"), sem("eps"), sem("rstd")
        xn_ready, edges = sem("xn"), sem("edges")
        front_ready, front_used = sem("front"), sem("front_used")
        dtx_ready, sp_step, sp_ready, da_ready = sem("dtx"), sem("sp_step"), sem("sp"), sem("da")
        prod_ready, conv_sum = [sem(f"prod_ready{b}") for b in range(HB)], sem("conv_sum")
        sums_ready, dec_ready, conv_ready, silu_ready = sem("sums"), sem("dec"), sem("conv"), sem("silu")
        own_ready, seg_in_ready, seg_ready = sem("own"), sem("seg_in"), sem("seg")
        xdt_ready, bt_ready, xdd_ready = sem("xdt"), sem("bt"), sem("xdd")
        cb_ready, decay_ready, mixer_ready = sem("cb"), sem("decay"), sem("mixer")
        y_ready, y_used, y2_ready = sem("y"), sem("y_used"), sem("y2")
        st_ready, sd_ready, st_used = sem("st"), sem("sd"), sem("st_used")
        ss_ready, ms_step, rr_ready, yn_ready = sem("ss"), sem("ms"), sem("rr"), sem("yn")
        yt_ready, yt_used, out_ready, out_used = sem("yt"), sem("yt_used"), sem("out"), sem("out_used")
        dve_step = sem("dve")
        late_gathered, late_added = sem("late_rows"), sem("late_added")
        h = k["h"]
        back = yn[:].rearrange("p c (a d) -> p (c a) d", d=D)

        FRONT = 8
        TERMS = [(t, d) for t in range(REACH - 1, -1, -1) for d in range(2)]

        SUMMED = (TERMS, [(t, d) for t, d in TERMS if d == 0])
        ADDS = len(SUMMED[0]) + len(SUMMED[1])
        CONVED = 1 + 2 * (CB - HB)

        def block_step(blk):
            return 1 if blk == 0 else 2 + blk

        def span(t, d):
            at = t if d == 0 else 2 * REACH - t
            return slice(at, at + T)

        def chunk(c):
            return c % 2, c // 2 if c % 2 == 0 else NT - 1 - c // 2

        SUMS = (("gt", "le"), ("lt", "ge"))
        INTO, OUT, TOTAL = (0, 3), (1, 4), 2

        block = ctx.enter_context(nc.Block())

        def heads(t):
            return t.rearrange("p (h d) -> p h d", h=NH)

        def per_head(t):
            return t.unsqueeze(2).broadcast_to([P, NH, HD])

        @block.sync
        def _(sp):
            with nc.allow_non_contiguous_dma("bias columns"):
                for dst, src in loads:
                    sp.dma_start(dst, src).then_inc(k["moe1_in"], 16)

        @block.vector
        def _(dve):
            dve.sem_inc(out_used, 1)
            for u in range(2):
                nc.vector.memset(f["xf"][u][:, 0:PAD], 0.0).then_inc(edges, 1)
                nc.vector.memset(f["xf"][u][:, PAD + T:XW], 0.0).then_inc(edges, 1)
            nc.vector.memset(xbc[:, :, 0:REACH], 0.0).then_inc(edges, 1)
            nc.vector.memset(xbc[:, :, REACH + T:], 0.0).then_inc(edges, 1)
            dve.wait_ge(edges, 6)
            CONV = (CB - HB) * (1 + 2 * (MT - 2)) + MT - 2
            AHEAD = 2 * (2 * NT + 2 + CONV)
            st = Steps(dve, dve_step, AHEAD // 2 + C + 1, ahead=AHEAD)

            def tap_of(blk, t):
                return k["mtap"][:, blk, t:t + 1]

            def stats(s):
                stat_steps(nc, k, st, f, h[:, bass.ds(NT * s, NT), :], var_ready)

            def scale(s, u):
                dve.wait_ge(rstd_ready, s + 1)
                for j in range(NT):
                    tile = h[:, bass.ds(NT * s + j, 1), :].rearrange("p a d -> p (a d)")
                    last = nc.vector.tensor_scalar(f["xn"][u][:, j, :], tile, f["mv"][:, j, 0:1],
                                                   f["rstd"][:, j:j + 1], ALU.subtract, ALU.mult)
                last.then_inc(xn_ready, 1)

            def dt_in(s):
                dve.wait_ge(front_used, FRONT * s + 3)
                n = st.mark(nc.vector.tensor_tensor(dt_x[:], dt_raw[:],
                                                    k["dt_b"][:].unsqueeze(1).broadcast_to([P, NT, NH]), ALU.add))
                st.need(n)
                nc.vector.scalar_tensor_tensor(dt_n[:], dt_x[:], -1.0, dt_x[:], ALU.mult, ALU.min).then_inc(dtx_ready, 1)

            def dt_out(s, u):
                dve.wait_ge(sp_ready, s + 1)
                n = st.mark(nc.vector.scalar_tensor_tensor(dt[u][:], dt_x[:], 0.0, dt_l[:], ALU.max, ALU.add))
                st.need(n)
                nc.vector.tensor_tensor(da[u][:], dt[u][:], k["a_neg"][:].unsqueeze(1).broadcast_to([P, NT, NH]),
                                        ALU.mult).then_inc(da_ready, 1)

            def block1(s, u, first=False):
                if not first:
                    dve.wait_ge(conv_sum, ADDS * s)
                dve.wait_ge(front_used, FRONT * s + block_step(1) + 1)
                for n, (t, d) in enumerate([(REACH, 0)] + SUMMED[1]):
                    nc.vector.tensor_scalar(prod[1][:, n, :], xbc[:, 1, span(t, d)], tap_of(1, t), None,
                                            ALU.mult).then_inc(prod_ready[1], 1)
                to, acc = act_x[u][:, 1, 1, :], prod[1][:, 0, :]
                dve.wait_ge(prod_ready[1], MT * s + 1)
                for t in range(REACH - 1, -1, -1):
                    if t < REACH - 1:
                        st.need(st.n)
                    ins = nc.vector.scalar_tensor_tensor(to, xbc[:, 1, span(t, 1)], tap_of(1, t), acc,
                                                         ALU.mult, ALU.add)
                    acc = to
                    if t > 0:
                        st.mark(ins)
                    else:
                        ins.then_inc(conv_ready, 1)

            def conv(s, u, blk):
                dve.wait_ge(front_used, FRONT * s + block_step(blk) + 1)
                mid = centre[blk % 2]
                n = st.mark(nc.vector.tensor_scalar(mid[:], xbc[:, blk, REACH:REACH + T], tap_of(blk, REACH), None,
                                                    ALU.mult))
                acc, done = [mid[:], mid[:]], [n, n]
                for t, d in TERMS:
                    st.need(done[d])
                    ins = nc.vector.scalar_tensor_tensor(act_x[u][:, d, blk, :], xbc[:, blk, span(t, d)],
                                                         tap_of(blk, t), acc[d], ALU.mult, ALU.add)
                    if t > 0:
                        done[d] = st.mark(ins)
                    else:
                        ins.then_inc(conv_ready, 1)
                    acc[d] = act_x[u][:, d, blk, :]

            def own_dve(s, u, c):
                d, j = chunk(c)
                dve.wait_ge(own_ready, C * s + c + 1)
                nc.vector.tensor_tensor(heads(xdt[:, c, :]), heads(OWN[c % 2][:, 0:DI]),
                                        per_head(dt[u][:, j, :]), ALU.mult).then_inc(xdt_ready, 1)
                nc.vector.tensor_tensor(cb[c % 2][:], OWN[c % 2][:, DI + P:DI + 2 * P],
                                        k[SUMS[d][1]][:], ALU.mult).then_inc(cb_ready, 1)

            def mix(s, c):
                dve.wait_ge(decay_ready, C * s + c + 1)
                dve.wait_ge(cb_ready, C * s + c + 1)
                nc.vector.tensor_tensor(mixer[:, c], decay[c % 2][:],
                                        cb[c % 2][:].unsqueeze(1).broadcast_to([P, NH, P]),
                                        ALU.mult).then_inc(mixer_ready, 1)

            def own(s, u, c, first=False):
                if c >= 2 or not first:
                    dve.wait_ge(mixer_ready, C * s + c - 1)
                own_dve(s, u, c)
                if c >= 1:
                    mix(s, c - 1)

            def recur(s, u, c):
                d, j = chunk(c)
                dve.wait_ge(y_ready, C * s + c + 1)
                if c >= 2:
                    n = st.mark(nc.vector.tensor_tensor(heads(y_off[d][:]), heads(Y[d][:, DI:2 * DI]),
                                                        per_head(dec[u][:, OUT[d], j, :]), ALU.mult))
                    st.need(n)
                    nc.vector.tensor_tensor(y_sum[d][:], Y[d][:, 0:DI], y_off[d][:], ALU.add).then_inc(y_used, 1)
                    dve.wait_ge(y_used, C * s + c + 1)
                    nc.vector.tensor_tensor(y[:, c, :], y_sum[d][:], zs[u][:, j, :], ALU.mult).then_inc(y2_ready, 1)
                else:
                    n = st.mark(nc.vector.tensor_copy(y_sum[d][:], Y[d][:, 0:DI]))
                    st.need(n)
                    dve.sem_inc(y_used, 1)
                    nc.vector.tensor_tensor(y[:, c, :], y_sum[d][:], zs[u][:, j, :], ALU.mult).then_inc(y2_ready, 1)
                if c < 2:
                    dve.wait_ge(st_ready, CS * s + c + 1)
                    nc.vector.tensor_copy(state[d][:], ST[d][:, 0:DI]).then_inc(st_used, 1)
                elif c < CS:
                    dve.wait_ge(st_ready, CS * s + c + 1)
                    dve.wait_ge(sd_ready, (CS - 2) * s + c - 1)
                    nc.vector.tensor_tensor(state[d][:], state_d[d][:], ST[d][:, 0:DI], ALU.add).then_inc(st_used, 1)

            st.n, st.base = 0, 0
            for s in range(2):
                stats(s)
                scale(s, s)
                block1(s, s, first=s == 0)
                dt_in(s)
                conv(s, s, 2)
                dt_out(s, s)
                conv(s, s, 3)
                if s == 0:
                    for c in range(C):
                        own(0, 0, c, first=True)
                    mix(0, C - 1)
            assert st.n == AHEAD, (st.n, AHEAD)
            dve.wait_ge(late_gathered, 16 * LATE)
            for t in range(LATE):
                at = NSEQ * NT - LATE + t
                nc.vector.scalar_tensor_tensor(h[:, at, :], back[:, t, :], k["weight0"][:, at:at + 1], h[:, at, :],
                                               ALU.mult, ALU.add).then_inc(late_added, 1)
            dve.wait_ge(late_added, LATE)

            def norm(s, half):
                dve.wait_ge(rr_ready, 2 * s + half + 1)
                for c in range(NT * half, NT * (half + 1)):
                    nc.vector.tensor_scalar(yn[:, c, :], y[:, c, :], rr[:, c:c + 1], None, ALU.mult).then_inc(yn_ready, 1)

            def step(s, u, left):
                if left:
                    st.slab(s)
                for c in range(LEAD):
                    recur(s, u, c)
                for c in range(C):
                    if c + LEAD < C:
                        recur(s, u, c + LEAD)
                    if left:
                        own(s + 1, 1 - u, c)
                    if left == 2 and c == 2:
                        stats(s + 2)
                    if left == 2 and c == 5:
                        scale(s + 2, u)
                    if c == 6:
                        norm(s, 0)
                if left:
                    mix(s + 1, C - 1)
                norm(s, 1)
                if left == 2:
                    block1(s + 2, u)
                    dt_in(s + 2)
                    conv(s + 2, u, 2)
                    dt_out(s + 2, u)
                dve.wait_ge(out_ready, NT * s + NT + 2)
                n = st.mark(nc.vector.tensor_tensor(o[:], OUT_BANK[:].rearrange("p (j d) -> p j d", d=D),
                                                    k["fuse_b"][:].unsqueeze(1).broadcast_to([P, NT, D]), ALU.add))
                st.need(n)
                hs = h[:, bass.ds(NT * s, NT), :]
                nc.vector.tensor_tensor(hs, hs, o[:], ALU.add).then_inc(out_used, 1)
                if left == 2:
                    conv(s + 2, u, 3)
                if left == 2:
                    st.end()

            slabs(dve, step)

        @block.gpsimd
        def _(pool):
            def seg(s, u, c, first=False):
                d, j = chunk(c)
                if c >= 2 or not first:
                    pool.wait_ge(seg_ready, C * s + c - 1)
                nc.gpsimd.tensor_tensor(seg_in[c % 2][:], k[SUMS[d][1]][:].unsqueeze(1).broadcast_to([P, NH, P]),
                                        da[u][:, j, :].unsqueeze(2).broadcast_to([P, NH, P]),
                                        ALU.mult).then_inc(seg_in_ready, 1)

            def into_state(s, u, c):
                d, j = chunk(c)
                pool.wait_ge(xdt_ready, C * s + c + 1)
                nc.gpsimd.tensor_tensor(heads(xdd[:, c, :]), heads(xdt[:, c, :]), per_head(dec[u][:, INTO[d], j, :]),
                                        ALU.mult).then_inc(xdd_ready, 1)

            def conv_sums(s, u, blk):
                terms = SUMMED[blk]
                for i, (t, d) in enumerate(terms):
                    pool.wait_ge(prod_ready[blk], (1 + len(terms)) * s + i + 2)
                    chain = 2 - blk
                    if i >= chain:
                        pool.wait_ge(conv_sum, ADDS * s + blk * len(TERMS) + i - chain + 1)
                    to = act_x[u][:, d, blk, :]
                    nc.gpsimd.tensor_tensor(to, prod[blk][:, 0, :] if i < chain else to, prod[blk][:, 1 + i, :],
                                            ALU.add).then_inc(conv_sum, 1)

            def rms(s, half):
                cols = slice(NT * half, NT * (half + 1))
                pool.wait_ge(ss_ready, C * s + NT * (half + 1))
                nc.gpsimd.tensor_tensor(ms[:, cols], ss[:, cols], k["inv_di"][:, cols], ALU.mult).then_inc(ms_step, 1)
                pool.wait_ge(ms_step, 4 * s + 2 * half + 1)
                nc.gpsimd.tensor_tensor(mse[:, cols], ms[:, cols], k["eps"][:, cols], ALU.add).then_inc(ms_step, 1)
                pool.wait_ge(ms_step, 4 * s + 2 * half + 2)
                nc.gpsimd.tensor_tensor(rr[:, cols], mse[:, cols], k["mhalf"][:, cols], ALU.pow).then_inc(rr_ready, 1)

            for s in range(2):
                rstd_steps(nc, pool, f, k, var_ready, var_eps, rstd_ready, s + 1)
                if s == 0:
                    late_gather(nc, pool, k, range(FIRST_LATE), back, rows_out, late_gathered)
                for blk in range(HB):
                    conv_sums(s, s, blk)
                if s == 0:
                    late_gather(nc, pool, k, range(FIRST_LATE, LATE), back, rows_out, late_gathered)
                if s == 0:
                    pool.wait_ge(da_ready, 1)
                    pool.wait_ge(dec_ready, 1)
                    for c in range(C):
                        seg(0, 0, c, first=True)
                        if 1 <= c <= CS:
                            into_state(0, 0, c - 1)

            def step(s, u, left):
                if left:
                    pool.wait_ge(da_ready, s + 2)
                for c in range(C):
                    if left:
                        seg(s + 1, 1 - u, c)
                    r = c + LEAD
                    if 2 <= r < CS:
                        d, j = chunk(r)
                        pool.wait_ge(st_used, CS * s + r - 1)
                        nc.gpsimd.tensor_tensor(heads(state_d[d][:]), heads(state[d][:]),
                                                per_head(dec[u][:, TOTAL, j, :]), ALU.mult).then_inc(sd_ready, 1)
                    if left and c == 1:
                        pool.wait_ge(dec_ready, s + 2)
                    if left and 1 <= c <= CS:
                        into_state(s + 1, 1 - u, c - 1)
                    if left == 2 and c == 3:
                        rstd_steps(nc, pool, f, k, var_ready, var_eps, rstd_ready, s + 3)
                    if c == 5:
                        rms(s, 0)
                rms(s, 1)
                if left == 2:
                    for blk in range(HB):
                        conv_sums(s + 2, u, blk)

            slabs(pool, step)

        @block.tensor
        def _(pe):
            pe.wait_ge(edges, 6)
            pe.sem_inc(out_ready, 2)

            def turn(s, n):
                if n >= 4:
                    pe.wait_ge(front_used, FRONT * s + n - 3)
                return FRONT_BANK[n % 4]

            def front_tokens(s, u, first=False):
                if not first:
                    pe.wait_ge(cb_ready, C * s - 1)
                pe.wait_ge(xn_ready, s + 1)
                b = turn(s, 0)
                for j in range(NT):
                    last = nc.tensor.transpose(b[:, P * j:P * (j + 1)], f["xn"][u][:, j, :], k["ident"][:])
                last.then_inc(front_ready, 1)

            def front_products(s, u, first=False):
                x = f["xf"][u]
                pe.wait_ge(front_used, FRONT * s + 1)
                for n in range(1, 2 + CB):
                    if not first and n <= 3:
                        pe.wait_ge(cb_ready if n == 2 else decay_ready, C * s - 1 if n == 1 else C * s)
                    b = turn(s, n)
                    if n == 2:
                        for j in range(NT):
                            last = nc.tensor.matmul(b[:, NH * j:NH * (j + 1)], x[:, PAD + P * j:PAD + P * (j + 1)],
                                                    k["dt_w"][:], start=True, stop=True)
                    else:
                        blk = 0 if n == 1 else n - 2
                        last = nc.tensor.matmul(b[:], k["xbc_w"][:, P * blk:P * (blk + 1)], x[:, PAD:PAD + T],
                                                start=True, stop=True)
                    last.then_inc(front_ready, 1)

            def front_z(s, u, n):
                x = f["xf"][u]
                b = turn(s, 6 + n)
                for j in (2 * n, 2 * n + 1):
                    last = nc.tensor.matmul(b[:, DI * (j % 2):DI * (j % 2 + 1)],
                                            x[:, PAD + P * j:PAD + P * (j + 1)], k["z_w"][:], start=True, stop=True)
                last.then_inc(front_ready, 1)

            def front(s, u, first=False):
                front_tokens(s, u, first)
                front_products(s, u, first)
                for n in range(2):
                    front_z(s, u, n)

            def dt_sums(s, u):
                pe.wait_ge(front_used, FRONT * s + 6)
                pe.wait_ge(da_ready, s + 1)
                for n, name in enumerate(("gt", "le", "ones", "lt", "ge")):
                    last = nc.tensor.matmul(SUM_BANK[:, NT * NH * n:NT * NH * (n + 1)], k[name][:],
                                            da[u][:].rearrange("p j h -> p (j h)"), start=True, stop=True)
                last.then_inc(sums_ready, 1)

            def own(s, u, c):
                x = act_x[u]
                d, j = chunk(c)
                tile = slice(P * j, P * (j + 1))
                if c >= 2:
                    pe.wait_ge(cb_ready, C * s + c - 1)
                    pe.wait_ge(bt_ready, CS * s + c - 1)
                for n in range(3 if c < CS else 2):
                    nc.tensor.transpose(OWN[c % 2][:, P * n:P * (n + 1)], x[:, d, n, tile], k["ident"][:])
                nc.tensor.matmul(OWN[c % 2][:, DI + P:DI + 2 * P], x[:, d, 2, tile], x[:, d, 3, tile],
                                 start=True, stop=True).then_inc(own_ready, 1)
                if c >= 2:
                    pe.wait_ge(decay_ready, C * s + c - 1)
                elif c == 0:
                    pe.wait_ge(dec_ready, s + 1)
                pe.wait_ge(seg_in_ready, C * s + c + 1)
                nc.tensor.matmul(SEG[c % 2][:], k[SUMS[d][0]][:], seg_in[c % 2][:].rearrange("p h l -> p (h l)"),
                                 start=True, stop=True).then_inc(seg_ready, 1)

            def recur(s, u, c):
                x = act_x[u]
                d, j = chunk(c)
                tile = slice(P * j, P * (j + 1))
                if c >= 2:
                    pe.wait_ge(y_used, C * s + c - 1)
                b = Y[d]
                for g in range(HB):
                    nc.tensor.matmul(b[:, P * g:P * (g + 1)], x[:, d, g, tile], k["skip"][:, g, :],
                                     start=(g == 0), stop=False, skip_group_check=True)
                pe.wait_ge(mixer_ready, C * s + c + 1)
                for n in range(NH):
                    last = nc.tensor.matmul(b[:, HD * n:HD * (n + 1)], mixer[:, c, n, :],
                                            xdt[:, c, HD * n:HD * (n + 1)], start=False, stop=(n == NH - 1),
                                            skip_group_check=True)
                if c >= 2:
                    pe.wait_ge(st_used, CS * s + c - 1)
                    last = nc.tensor.matmul(b[:, DI:2 * DI], x[:, d, 3, tile], state[d][:], start=False, stop=True,
                                            skip_group_check=True)
                last.then_inc(y_ready, 1)
                if c < CS:
                    pe.wait_ge(bt_ready, CS * s + c + 1)
                    pe.wait_ge(xdd_ready, CS * s + c + 1)
                    nc.tensor.matmul(ST[d][:, 0:DI], b_t[:, c, :], xdd[:, c, :],
                                     start=True, stop=True).then_inc(st_ready, 1)

            front(0, 0, first=True)
            dt_sums(0, 0)
            pe.wait_ge(silu_ready, 2 * CB)
            for c in range(C):
                own(0, 0, c)
            front(1, 1)
            dt_sums(1, 1)

            def step(s, u, left):
                pe.wait_ge(yt_used, NT * s + 1)
                pe.wait_ge(out_used, s + 1)
                for c in range(LEAD):
                    recur(s, u, c)
                for c in range(C):
                    if c + LEAD < C:
                        recur(s, u, c + LEAD)
                    if left:
                        if c == 0:
                            pe.wait_ge(silu_ready, 2 * CB * (s + 2))
                            pe.wait_ge(front_used, FRONT * (s + 2))
                        if left == 2 and c == C - 1:
                            front_tokens(s + 2, u)
                        own(s + 1, 1 - u, c)
                if left == 2:
                    front_products(s + 2, u)

                def output(j):
                    pe.wait_ge(yt_used, NT * s + j + 2)
                    for n in range(4):
                        last = nc.tensor.matmul(OUT_BANK[:, D * j:D * (j + 1)], yt[j % 2][:, n, :],
                                                k["fuse_w"][:, n % HB, n // HB, :], start=(n == 0), stop=(n == 3))
                    last.then_inc(out_ready, 1)

                pe.wait_ge(yn_ready, C * s + C)
                for j in range(NT):
                    if j >= 2:
                        pe.wait_ge(yt_used, NT * s + j)
                    for n in range(4):
                        d, g = n // HB, n % HB
                        c = 2 * j if d == 0 else 2 * (NT - 1 - j) + 1
                        last = nc.tensor.transpose(YT[j % 2][:, P * n:P * (n + 1)], yn[:, c, P * g:P * (g + 1)],
                                                   k["ident"][:])
                    last.then_inc(yt_ready, 1)
                    if left == 2 and 1 <= j <= 2:
                        front_z(s + 2, u, j - 1)
                    if j >= 1:
                        output(j - 1)
                output(NT - 1)
                if left == 2:
                    dt_sums(s + 2, u)

            slabs(pe, step)

        @block.scalar
        def _(act):
            act.wait_ge(edges, 6)
            act.sem_inc(yt_used, 1)

            def own(s, c, first=False):
                if c < CS:
                    act.wait_ge(cb_ready, C * s + c + 1)
                    nc.scalar.activation(b_t[:, c, :], OWN[c % 2][:, DI:DI + P], ACT.Copy).then_inc(bt_ready, 1)
                if c >= 2 or not first:
                    act.wait_ge(mixer_ready, C * s + c - 1)
                act.wait_ge(seg_ready, C * s + c + 1)
                nc.scalar.activation(decay[c % 2][:].rearrange("p h l -> p (h l)"), SEG[c % 2][:],
                                     ACT.Exp).then_inc(decay_ready, 1)

            def take(s, n):
                act.wait_ge(front_ready, FRONT * s + n + 1)
                return FRONT_BANK[n % 4]

            def into_sbuf(s, blk):
                nc.scalar.activation(xbc[:, blk, REACH:REACH + T], take(s, block_step(blk))[:],
                                     ACT.Copy).then_inc(front_used, 1)

            def products(s, numbers):
                act.wait_ge(front_used, FRONT * s + 2)
                for n in numbers:
                    t, d = (REACH, 0) if n == 0 else TERMS[n - 1]
                    nc.scalar.activation(prod[0][:, n, :], xbc[:, 0, span(t, d)], ACT.Copy,
                                         scale=k["mtap"][:, 0, t:t + 1]).then_inc(prod_ready[0], 1)

            def front_tokens(s, u):
                nc.scalar.activation(f["xf"][u][:, PAD:PAD + T], take(s, 0)[:], ACT.Copy).then_inc(front_used, 1)

            def front(s, u, between=lambda j: None):
                into_sbuf(s, 0)
                nc.scalar.activation(dt_raw[:].rearrange("p j h -> p (j h)"), take(s, 2)[:, 0:NT * NH],
                                     ACT.Copy).then_inc(front_used, 1)
                into_sbuf(s, 1)
                products(s, range(3))
                into_sbuf(s, 2)
                between(0)
                products(s, range(3, 5))
                into_sbuf(s, 3)
                between(1)
                products(s, range(5, 7))
                between(2)
                act.wait_ge(dtx_ready, s + 1)
                nc.scalar.activation(dt_e[:], dt_n[:], ACT.Exp).then_inc(sp_step, 1)
                act.wait_ge(sp_step, s + 1)
                nc.scalar.activation(dt_l[:], dt_e[:], ACT.Ln, bias=1.0).then_inc(sp_ready, 1)
                between(3)

            def decays(s, u):
                nc.scalar.preload_act_table_set("natural_log_exp_and_others")
                act.wait_ge(sums_ready, s + 1)
                nc.scalar.activation(dec[u][:].rearrange("p n j h -> p (n j h)"), SUM_BANK[:, 0:5 * NT * NH],
                                     ACT.Exp).then_inc(dec_ready, 1)

            def silu(s, u, blk):
                for d in range(2):
                    if blk == 0:
                        act.wait_ge(conv_sum, ADDS * s + len(TERMS) - 1 + d)
                    elif (blk, d) == (1, 0):
                        act.wait_ge(conv_sum, ADDS * (s + 1))
                    else:
                        act.wait_ge(conv_ready, CONVED * s + 2 * (blk - 1) + d)
                    nc.scalar.activation(act_x[u][:, d, blk, :], act_x[u][:, d, blk, :], ACT.Silu,
                                         bias=k["conv_b"][:, blk:blk + 1]).then_inc(silu_ready, 1)

            def silu_z(s, u):
                for n in range(2):
                    nc.scalar.activation(zs[u][:, 2 * n:2 * n + 2, :].rearrange("p j c -> p (j c)"),
                                         take(s, 6 + n)[:], ACT.Silu).then_inc(front_used, 1)

            nc.scalar.preload_act_table_set("natural_log_exp_and_others")
            for s in range(2):
                front_tokens(s, s)
                front(s, s)
                silu_z(s, s)
                for blk in (2, 0, 3, 1):
                    silu(s, s, blk)
                decays(s, s)
                if s == 0:
                    for c in range(C):
                        own(0, c, first=True)

            def step(s, u, left):
                def square(c):
                    act.wait_ge(y2_ready, C * s + c + 1)
                    nc.scalar.activation(yn[:, c, :], y[:, c, :], ACT.Square, accum_out=ss[:, c:c + 1]).then_inc(ss_ready, 1)

                def yt_copy(j):
                    act.wait_ge(yt_ready, NT * s + j + 1)
                    act.wait_ge(out_ready, NT * s + j + 1)
                    nc.scalar.activation(yt[j % 2][:].rearrange("p n t -> p (n t)"), YT[j % 2][:],
                                         ACT.Copy).then_inc(yt_used, 1)

                for c in range(LEAD):
                    square(c)
                for c in range(C):
                    if left == 2 and c == C - 1:
                        front_tokens(s + 2, u)
                    if c + LEAD < C:
                        square(c + LEAD)
                    if left:
                        own(s + 1, c)
                if left == 2:
                    front(s + 2, u, yt_copy)
                    silu_z(s + 2, u)
                    for blk in (2, 0, 3, 1):
                        silu(s + 2, u, blk)
                    decays(s + 2, u)
                else:
                    for j in range(NT):
                        yt_copy(j)

            slabs(act, step)


def sorted_mixture(nc, k, n, width, picks, rows_in, rows_out, out=None):
    with ExitStack() as ctx:
        sb, pb, sem = parts(nc, ctx, f"s{n}_")
        G = width // P
        NTT = NSEQ * NT
        NA = picks * NTT
        GT = NTT // GROUPS
        GA = picks * GT
        TILES = sorted_tiles(picks)
        GTILES = TILES // GROUPS
        RING = 4
        LAG = 3
        rows_in, rows_out = rows_in[0:P * TILES, :], rows_out[0:P * TILES, :]
        GS = NSEQ // GROUPS
        stats = sb("stats", [P, NTT, 6])
        mv = sb("mv", [P, NTT, 2])
        var, rstd = sb("var", [P, NTT]), sb("rstd", [P, NTT])
        eps, mhalf = (k[name][:, 0:1].broadcast_to([P, GT]) for name in ("eps", "mhalf"))
        xf = [sb(f"xf{u}", [P, T]) for u in range(2)]
        xn_all = sb("xn_all", [P, NTT, D])
        back = sb("back", [P, NA, D])
        logit = sb("logit", [P, NTT, E])
        picked = sb("picked", [P, NA, E])
        weight = k["weight0"] if n == 0 else sb("weight", [P, NA])
        big = {name: sb(name, [P, NTT, E]) for name in ("shift", "ex", "eq", "rk", "rest")}
        col = {name: sb("col_" + name, [P, NTT]) for name in ("mx", "sum", "mr", "mx2", "d", "ed", "den")}
        cnt = sb("cnt", [P, GROUPS, E])
        tot_i, pad_i = sb("tot_i", [P, GROUPS, E], I32), sb("pad_i", [P, GROUPS, E], I32)
        pad_f, end, start, init = (sb(name, [P, GROUPS, E]) for name in ("pad_f", "end", "start", "init"))
        run = sb("run", [P, GROUPS, E, GA])
        sel = sb("sel", [P, NA, E])
        pos_f = sb("pos_f", [P, NA])
        pos = k["pos0"] if n == 0 else sb("pos", [P, NA], I32)
        BACK = NTT - GT if n == 0 else NTT
        first_i = sb("first_i", [P, TILES], I32)
        first = sb("first", [P, TILES])
        past = sb("past", [P, TILES, E])
        tile_e = sb("tile_e", [P, TILES])
        tile_ec = sb("tile_ec", [P, TILES])
        expert = sb("expert", [P, TILES], I32)
        xs = [sb(f"xs{u}", [P, D]) for u in range(RING)]
        xt = [sb(f"xt{u}", [P, P]) for u in range(RING)]
        W1, W2, B1, B2 = expert_parts(width)
        we = [sb(f"we{u}", [P, B2.stop]) for u in range(RING)]
        hid = [sb(f"hid{u}", [P, G, P]) for u in range(RING)]
        ys = [sb(f"ys{u}", [P, D]) for u in range(RING)]
        bank = [pb(f"bank{i}") for i in range(8)]
        var_ready, var_eps, rstd_ready = sem("var"), sem("eps"), sem("rstd")
        xn_ready, xt_ready, xf_ready = sem("xn"), sem("xt_slab"), sem("xf")
        logit_ready = sem("logit_ready")
        pool_const, shift_ready, ex_ready = sem("pool_const"), sem("shift_ready"), sem("ex_ready")
        cnt_ready, sums_ready, pos_ready = sem("cnt_ready"), sem("sums"), sem("pos_ready")
        scattered = [sem(f"scattered{g}") for g in range(GROUPS)]
        gathered = [sem(f"gathered{i}") for i in range(PAIRS)]
        xs_in = [sem(f"xs_in{u}") for u in range(RING)]
        ys_out = [sem(f"ys_out{u}") for u in range(RING)]
        tr_ready, xt_copied, w_copied = sem("tr"), sem("xt_copied"), sem("w_copied")
        hid_ready, hid_done, y_ready, ys_ready = sem("hid_ready"), sem("hid_done"), sem("y_ready"), sem("ys_ready")
        stat_step, seq_step, add_step = sem("stat_step"), sem("seq_step"), sem("add_step")
        func = ACT.Gelu if n == 0 else ACT.Relu
        h = k["h"]

        block = ctx.enter_context(nc.Block())

        def lagged(eng, step):
            for i in range(2 * RING):
                step(i, i % RING)
            with eng.Fori(2, TILES // RING) as q:
                for u in range(RING):
                    step(RING * q + u, u)
            for i in range(TILES // RING * RING, TILES + RING):
                step(i, i % RING)

        def since(i, lag):
            return not isinstance(i, int) or i >= lag

        def turns(i, u):
            return i // RING + 1 if isinstance(i, int) else (i - u) // RING + 1

        def is_tile(i, lag):
            return not isinstance(i, int) or 0 <= i - lag < TILES

        def column(t, pick):
            return GA * (t // GT) + GT * pick + t % GT

        @block.vector
        def _(dve):
            for g in range(GROUPS):
                for t in range(GT * g, GT * (g + 1)):
                    last = nc.vector.bn_stats(stats[:, t, :], h[:, t, :])
                last.then_inc(stat_step, 1)
                dve.wait_ge(stat_step, 2 * g + 1)
                for t in range(GT * g, GT * (g + 1)):
                    last = nc.vector.bn_aggr(mv[:, t, :], stats[:, t, :])
                last.then_inc(stat_step, 1)
                tiles = slice(GT * g, GT * (g + 1))
                dve.wait_ge(stat_step, 2 * g + 2)
                nc.vector.tensor_copy(var[:, tiles], mv[:, tiles, 1]).then_inc(var_ready, 1)
            for t in range(NTT):
                if t % GT == 0:
                    dve.wait_ge(rstd_ready, t // GT + 1)
                nc.vector.tensor_scalar(xn_all[:, t, :], h[:, t, :], mv[:, t, 0:1], rstd[:, t:t + 1],
                                        ALU.subtract, ALU.mult).then_inc(xn_ready, 1)

            seq = [0]

            def do(ins):
                ins.then_inc(seq_step, 1)
                seq[0] += 1
                dve.wait_ge(seq_step, seq[0])

            def over_e(t, m=GT):
                return t.unsqueeze(2).broadcast_to([P, m, E])

            def route(g):
                tiles = slice(GT * g, GT * (g + 1))
                mine = slice(GA * g, GA * (g + 1))
                b = {name: big[name][:, tiles, :] for name in big}
                c = {name: col[name][:, tiles] for name in col}
                lg = logit[:, tiles, :]

                def pick_of(pick):
                    return picked[:, GA * g + GT * pick:GA * g + GT * (pick + 1), :]

                def weight_of(pick):
                    return weight[:, GA * g + GT * pick:GA * g + GT * (pick + 1)]

                def top(pick, logits, mx):
                    do(nc.vector.tensor_tensor(b["eq"], logits, over_e(mx), ALU.is_equal))
                    do(nc.vector.tensor_tensor(b["rk"], b["eq"], k["rank"][:].unsqueeze(1).broadcast_to([P, GT, E]),
                                               ALU.mult))
                    do(nc.vector.tensor_reduce(c["mr"], b["rk"], AX, ALU.max))
                    do(nc.vector.tensor_tensor(pick_of(pick), b["rk"], over_e(c["mr"]), ALU.is_equal))

                do(nc.vector.tensor_reduce(c["mx"], lg, AX, ALU.max))
                if picks == 1:
                    nc.vector.tensor_tensor(b["shift"], lg, over_e(c["mx"]), ALU.subtract).then_inc(shift_ready, 1)
                top(0, lg, c["mx"])
                if picks == 2:
                    do(nc.vector.scalar_tensor_tensor(b["rest"], pick_of(0), -3.0e38, lg, ALU.mult, ALU.add))
                    do(nc.vector.tensor_reduce(c["mx2"], b["rest"], AX, ALU.max))
                    nc.vector.tensor_tensor(c["d"], c["mx2"], c["mx"], ALU.subtract).then_inc(shift_ready, 1)
                    top(1, b["rest"], c["mx2"])

                nc.vector.tensor_reduce(cnt[:, g, :], picked[:, mine, :].rearrange("p n e -> p e n"), AX,
                                        ALU.add).then_inc(cnt_ready, 1)
                dve.wait_ge(sums_ready, g + 1)
                before, total = (bank[4 + g][:, E * m:E * (m + 1)] for m in range(2))
                do(nc.vector.tensor_scalar(tot_i[:, g], total, float(P - 1), None, ALU.add))
                do(nc.vector.tensor_scalar(pad_i[:, g], tot_i[:, g], 7, 7, ALU.arith_shift_right,
                                           ALU.logical_shift_left))
                do(nc.vector.tensor_copy(pad_f[:, g], pad_i[:, g]))
                do(nc.vector.tensor_tensor_scan(end[:, g, :], k["ones"][:, 0:E], pad_f[:, g, :],
                                                float(P * GTILES * g), ALU.mult, ALU.add))
                do(nc.vector.tensor_tensor(start[:, g], end[:, g], pad_f[:, g], ALU.subtract))
                do(nc.vector.scalar_tensor_tensor(init[:, g], start[:, g], -1.0, before, ALU.add, ALU.add))
                for e in range(E):
                    nc.vector.tensor_tensor_scan(run[:, g, e, :], k["ones"][:, 0:GA], picked[:, mine, e],
                                                 init[:, g, e:e + 1], ALU.mult, ALU.add).then_inc(seq_step, 1)
                seq[0] += E
                dve.wait_ge(seq_step, seq[0])
                do(nc.vector.tensor_tensor(sel[:, mine, :], run[:, g].rearrange("p e n -> p n e"), picked[:, mine, :],
                                           ALU.mult))
                do(nc.vector.tensor_reduce(pos_f[:, mine], sel[:, mine, :], AX, ALU.add))
                nc.vector.tensor_copy(pos[:, mine], pos_f[:, mine]).then_inc(pos_ready, 1)

                ts = slice(GTILES * g, GTILES * (g + 1))
                do(nc.vector.tensor_tensor(past[:, ts], over_e(first[:, ts], GTILES),
                                           end[:, g].unsqueeze(1).broadcast_to([P, GTILES, E]), ALU.is_ge))
                do(nc.vector.tensor_reduce(tile_e[:, ts], past[:, ts], AX, ALU.add))
                do(nc.vector.tensor_scalar(tile_ec[:, ts], tile_e[:, ts], float(E - 1), None, ALU.min))
                do(nc.vector.tensor_copy(expert[:, ts], tile_ec[:, ts]))

                dve.wait_ge(ex_ready, g + 1)
                if picks == 1:
                    do(nc.vector.tensor_reduce(c["sum"], b["ex"], AX, ALU.add))
                    do(nc.vector.reciprocal(weight_of(0), c["sum"]))
                else:
                    do(nc.vector.tensor_scalar(c["den"], c["ed"], 1.0, None, ALU.add))
                    do(nc.vector.reciprocal(weight_of(0), c["den"]))
                    do(nc.vector.tensor_tensor(weight_of(1), c["ed"], weight_of(0), ALU.mult))

            dve.wait_ge(pool_const, 1)
            do(nc.vector.tensor_copy(first[:], first_i[:]))
            for g in range(GROUPS):
                dve.wait_ge(logit_ready, GS * (g + 1))
                do(nc.vector.tensor_tensor(logit[:, GT * g:GT * (g + 1), :],
                                           bank[1 + 2 * g][:, 0:GT * E].rearrange("p (t e) -> p t e", e=E),
                                           k[f"r_b{n}"][:].unsqueeze(1).broadcast_to([P, GT, E]), ALU.add))
                route(g)

            dve.wait_ge(k[f"moe{n}_in"], 16 * EXPERT_LOADS[n])

            def tile_round(i, u):
                if is_tile(i, 0):
                    e = dve.value_load(expert[0:1, bass.ds(i, 1)], min_val=0, max_val=E - 1)
                    if since(i, RING):
                        dve.wait_ge(ys_ready, i - RING + 1)
                    nc.vector.tensor_copy(we[u][:], k[f"experts{n}"][:, bass.ds(e, 1), :].rearrange("p a c -> p (a c)")
                                          ).then_inc(w_copied, 1)
                if is_tile(i, LAG):
                    v = (u - LAG) % RING
                    dve.wait_ge(y_ready, i - LAG + 1)
                    if since(i, LAG + RING):
                        dve.wait_ge(ys_out[v], 16 * (turns(i - LAG, v) - 1))
                    nc.vector.tensor_tensor(ys[v][:], bank[4 + v % 2][:, 0:D], we[v][:, B2], ALU.add).then_inc(ys_ready, 1)

            lagged(dve, tile_round)

            adds = 0
            for s in range(BACK // NT):
                if s % 2 == 0:
                    dve.wait_ge(gathered[s // 2], 16 * picks * 2 * NT)
                for pick in range(picks):
                    if pick:
                        dve.wait_ge(add_step, adds)
                    for t in range(NT * s, NT * (s + 1)):
                        at = column(t, pick)
                        nc.vector.scalar_tensor_tensor(h[:, t, :], back[:, at, :], weight[:, at:at + 1], h[:, t, :],
                                                       ALU.mult, ALU.add).then_inc(add_step, 1)
                        adds += 1

        @block.gpsimd
        def _(pool):
            nc.gpsimd.iota(first_i[:], pattern=[[P, TILES]], base=0, channel_multiplier=0).then_inc(pool_const, 1)
            for g in range(GROUPS):
                tiles = slice(GT * g, GT * (g + 1))
                pool.wait_ge(var_ready, g + 1)
                nc.gpsimd.tensor_tensor(var[:, tiles], var[:, tiles], eps, ALU.add).then_inc(var_eps, 1)
                pool.wait_ge(var_eps, g + 1)
                nc.gpsimd.tensor_tensor(rstd[:, tiles], var[:, tiles], mhalf, ALU.pow).then_inc(rstd_ready, 1)
            pool.wait_ge(k["blank"], 16)
            for g in range(GROUPS):
                pool.wait_ge(pos_ready, g + 1)
                for a in range(GA):
                    at = GA * g + a
                    pool.indirect_dma_start(out=rows_in, in_=xn_all[:, GT * g + a % GT, :], in_offset=None,
                                            out_offset=bass.IndirectOffsetOnAxis(ap=pos[:, at:at + 1], axis=0)
                                            ).then_inc(scattered[g], 16)
            for g in range(GROUPS):
                for u in range(RING):
                    pool.wait_ge(ys_out[u], 16 * len(range(u, GTILES * (g + 1), RING)))
                for t in range(GT * g, min(GT * (g + 1), BACK)):
                    for pick in range(picks):
                        at = column(t, pick)
                        pool.indirect_dma_start(out=back[:, at, :], out_offset=None,
                                                in_=rows_out[0:P * GTILES * (g + 1), :],
                                                in_offset=bass.IndirectOffsetOnAxis(ap=pos[:, at:at + 1], axis=0)
                                                ).then_inc(gathered[t // (2 * NT)], 16)

        @block.sync
        def _(sp):
            def tile_round(i, u):
                if is_tile(i, 0):
                    if isinstance(i, int) and i % GTILES == 0:
                        sp.wait_ge(scattered[i // GTILES], 16 * GA)
                    if since(i, RING):
                        sp.wait_ge(tr_ready, i - RING + 1)
                    sp.dma_start(xs[u][:], rows_in[bass.ds(P * i, P), :]).then_inc(xs_in[u], 16)

            assert GROUPS == 2
            for i in range(2 * RING):
                tile_round(i, i % RING)
            with sp.Fori(2, GTILES // RING) as q:
                for u in range(RING):
                    tile_round(RING * q + u, u)
            for i in range(GTILES // RING * RING, (GTILES // RING + 1) * RING):
                tile_round(i, i % RING)
            with sp.Fori(GTILES // RING + 1, TILES // RING) as q:
                for u in range(RING):
                    tile_round(RING * q + u, u)
            for i in range(TILES // RING * RING, TILES + RING):
                tile_round(i, i % RING)
            if out is not None:
                for s in range(NSEQ):
                    sp.wait_ge(add_step, picks * NT * (s + 1))
                    sp.dma_start(out[s].rearrange("(j p) d -> p j d", p=P),
                                 h[:, NT * s:NT * (s + 1), :]).then_inc(k["stored"], 16)
                sp.wait_ge(k["stored"], 16 * NSEQ)

        @block.tensor
        def _(pe):
            pe.wait_ge(k[f"moe{n}_in"], 16 * EXPERT_LOADS[n])

            def slab(s):
                for j in range(NT):
                    pe.wait_ge(xn_ready, NT * s + j + 1)
                    last = nc.tensor.transpose(bank[2 * (s % 2)][:, P * j:P * (j + 1)], xn_all[:, NT * s + j, :],
                                               k["ident"][:])
                last.then_inc(xt_ready, 1)

            def logits(s):
                pe.wait_ge(xf_ready, s + 1)
                for j in range(NT):
                    at = E * (NT * (s % GS) + j)
                    last = nc.tensor.matmul(bank[1 + 2 * (s // GS)][:, at:at + E], xf[s % 2][:, P * j:P * (j + 1)],
                                            k[f"r_w{n}"][:], start=True, stop=True)
                last.then_inc(logit_ready, 1)

            for g in range(GROUPS):
                for s in range(GS * g, GS * (g + 1)):
                    if s >= 2:
                        pe.wait_ge(xf_ready, s - 1)
                    slab(s)
                    if s > GS * g:
                        logits(s - 1)
                logits(GS * (g + 1) - 1)
                pe.wait_ge(cnt_ready, g + 1)
                for m, name in enumerate(("lt", "ones")):
                    last = nc.tensor.matmul(bank[4 + g][:, E * m:E * (m + 1)], k[name][:], cnt[:, g, :],
                                            start=True, stop=True)
                last.then_inc(sums_ready, 1)

            def tile_round(i, u):
                if is_tile(i, 0):
                    pe.wait_ge(xs_in[u], 16 * turns(i, u))
                    if since(i, 2):
                        pe.wait_ge(xt_copied, i - 1)
                    nc.tensor.transpose(bank[u % 2][:, 0:P], xs[u][:], k["ident"][:]).then_inc(tr_ready, 1)
                if is_tile(i, LAG):
                    v = (u - LAG) % RING
                    pe.wait_ge(hid_done, i - LAG + 1)
                    if since(i, LAG + 2):
                        pe.wait_ge(ys_ready, i - LAG - 1)
                    for g in range(G):
                        last = nc.tensor.matmul(bank[4 + v % 2][:, 0:D], hid[v][:, g, :],
                                                we[v][:, W2.start + D * g:W2.start + D * (g + 1)],
                                                start=(g == 0), stop=(g == G - 1))
                    last.then_inc(y_ready, 1)
                if is_tile(i, 1):
                    v = (u - 1) % RING
                    pe.wait_ge(xt_copied, i)
                    pe.wait_ge(w_copied, i)
                    if since(i, 3):
                        pe.wait_ge(hid_done, i - 2)
                    for g in range(G):
                        last = nc.tensor.matmul(bank[2 + v % 2][:, P * g:P * (g + 1)], we[v][:, W1.start + P * g:W1.start + P * (g + 1)],
                                                xt[v][:], start=True, stop=True)
                    last.then_inc(hid_ready, 1)

            lagged(pe, tile_round)

        @block.scalar
        def _(act):
            for g in range(GROUPS):
                for s in range(GS * g, GS * (g + 1)):
                    act.wait_ge(xt_ready, s + 1)
                    if s >= 2:
                        act.wait_ge(logit_ready, s - 1)
                    nc.scalar.activation(xf[s % 2][:], bank[2 * (s % 2)][:], ACT.Copy).then_inc(xf_ready, 1)
                tiles = slice(GT * g, GT * (g + 1))
                act.wait_ge(shift_ready, g + 1)
                nc.scalar.activation(*((big["ex"][:, tiles], big["shift"][:, tiles]) if picks == 1 else
                                       (col["ed"][:, tiles], col["d"][:, tiles])), ACT.Exp).then_inc(ex_ready, 1)

            def tile_round(i, u):
                if is_tile(i, 0):
                    act.wait_ge(tr_ready, i + 1)
                    nc.scalar.activation(xt[u][:], bank[u % 2][:, 0:P], ACT.Copy).then_inc(xt_copied, 1)
                if is_tile(i, 1):
                    v = (u - 1) % RING
                    act.wait_ge(hid_ready, i)
                    for g in range(G):
                        last = nc.scalar.activation(hid[v][:, g, :], bank[2 + v % 2][:, P * g:P * (g + 1)], func,
                                                    bias=we[v][:, B1.start + g:B1.start + g + 1])
                    last.then_inc(hid_done, 1)
                if is_tile(i, RING):
                    act.wait_ge(ys_ready, i - RING + 1)
                    act.dma_start(rows_out[bass.ds(P * (i - RING), P), :], ys[u][:]).then_inc(ys_out[u], 16)

            lagged(act, tile_round)


_INS = ['x', 'L0_tok_w', 'L0_attn_in_proj_w', 'L0_attn_conv_fwd_w', 'L0_attn_conv_fwd_b', 'L0_attn_proj_fwd_w',
        'L0_attn_proj_fwd_b', 'L0_attn_conv_bwd_w', 'L0_attn_conv_bwd_b', 'L0_attn_proj_bwd_w', 'L0_attn_proj_bwd_b',
        'L0_attn_diag_weight', 'L0_attn_gate_scale', 'L0_attn_out_proj_w', 'L0_attn_ln_g', 'L0_attn_ln_b',
        'L0_ffn_Ws', 'L0_ffn_bs', 'L0_ffn_W1', 'L0_ffn_b1', 'L0_ffn_W2', 'L0_ffn_b2', 'L1_attn_in_proj_w',
        'L1_attn_conv_w', 'L1_attn_conv_b', 'L1_attn_dt_bias', 'L1_attn_A_log', 'L1_attn_D_skip', 'L1_attn_norm_w',
        'L1_attn_ssm_out_w', 'L1_attn_fuse_w', 'L1_attn_fuse_b', 'L1_ffn_gate_w', 'L1_ffn_gate_b', 'L1_ffn_w1',
        'L1_ffn_b1', 'L1_ffn_w2', 'L1_ffn_b2']


def kernel(**inputs):
    import numpy as _np
    import concourse.bacc as _bacc
    from concourse import mybir as _mybir
    from concourse.bass_utils import run_bass_kernel_spmd as _run

    nc = _bacc.Bacc("TRN2", target_bir_lowering=False, num_devices=1)
    arrays, aps = {}, {}
    for name in _INS:
        a = _np.ascontiguousarray(inputs[name])
        arrays[f"in_{name}"] = a
        aps[name] = nc.dram_tensor(f"in_{name}", a.shape, _mybir.dt.from_np(a.dtype), kind="ExternalInput").ap()
    out = nc.dram_tensor("out", (NSEQ, T, D), _mybir.dt.float32, kind="ExternalOutput").ap()
    build(nc, aps, out)
    r = _run(nc, [arrays], core_ids=[0])
    return r.results[0]["out"]
```
